# Optimizing a Trainium2 kernel written in Bass

```python
import numpy as np
import jax
import jax.numpy as jnp

def _softmax(x, axis=-1):
    return jax.nn.softmax(x, axis=axis)

def _gelu(x):
    return jax.nn.gelu(x, approximate=True)

def _silu(x):
    return jax.nn.silu(x)

def _sigmoid(x):
    return jax.nn.sigmoid(x)

def _layernorm(x, axis=-1, eps=1e-05):
    m = jnp.mean(x, axis=axis, keepdims=True)
    v = jnp.var(x, axis=axis, keepdims=True)
    return (x - m) / jnp.sqrt(v + eps)

def _scatter_add(tgt, idx, src, axis=0):
    return tgt.at[idx].add(src)

def _segment_sum(src, seg, n):
    return jax.ops.segment_sum(src, seg, n)
kernel_name = 'mk_adaln_ffn_d4_seqx_r4_2f38bd'

def setup_inputs(seed: int=0):
    np.random.seed(seed)
    _w = jnp.asarray

    def _rec_inputs():
        import jax
        import jax.numpy as jnp
        _rk = jax.random.key(seed)
        x = -0.000125 + 0.9999 * jax.random.normal(jax.random.fold_in(_rk, 1), (32, 64, 1024), jnp.float32)
        _lenS = 64 - jax.random.randint(jax.random.fold_in(_rk, 7), (32,), 0, max(1, 64 // 4) + 1, jnp.int32)
        _lenS2 = 64 - jax.random.randint(jax.random.fold_in(_rk, 8), (32,), 0, max(1, 64 // 4) + 1, jnp.int32)
        cond_128 = 0.0061147 + 1.02565 * jax.random.normal(jax.random.fold_in(_rk, 11), (32, 128), jnp.float32)
        fside_S_0 = -0.022604 + 0.987366 * jax.random.normal(jax.random.fold_in(_rk, 12), (64,), jnp.float32)
        return (x, cond_128, fside_S_0)
    x, cond_128, fside_S_0 = _rec_inputs()

    def _L0_cond_setup():
        import jax, jax.numpy as jnp
        import numpy as np
        K = 8
        T = 1.0
        D_EMBD = 128
        IN_C = 64
        OUT_C = 64
        BS = 32
        H = 1024
        HID = 128
        key = jax.random.key(seed)
        ks = jax.random.split(key, 10)
        s = lambda fan_in: 1.0 / np.sqrt(fan_in)
        return {'x': jax.random.normal(ks[0], (BS, IN_C, H), dtype=jnp.float32), 'embedding': jax.random.normal(ks[1], (BS, D_EMBD), dtype=jnp.float32), 'W0': jax.random.normal(ks[2], (D_EMBD, HID), dtype=jnp.float32) * s(D_EMBD), 'b0': jnp.zeros((HID,), dtype=jnp.float32), 'W1': jax.random.normal(ks[3], (HID, HID), dtype=jnp.float32) * s(HID), 'b1': jnp.zeros((HID,), dtype=jnp.float32), 'W2': jax.random.normal(ks[4], (HID, K), dtype=jnp.float32) * s(HID), 'b2': jnp.zeros((K,), dtype=jnp.float32), 'weight': jax.random.normal(ks[5], (K, OUT_C, IN_C, 1), dtype=jnp.float32) * s(IN_C), 'bias_k': jax.random.normal(ks[6], (K, OUT_C), dtype=jnp.float32) * 0.1}
    _L0_cond_all = _L0_cond_setup()
    _L0_cond_in = {k: v for k, v in _L0_cond_all.items() if k in ('W0', 'b0', 'W1', 'b1', 'W2', 'b2', 'weight', 'bias_k')}
    del _L0_cond_all

    def _L0_ffn_setup():
        import jax, jax.numpy as jnp
        import numpy as np
        R = 16
        LORA_ALPHA = 16
        SCALING = LORA_ALPHA / R
        key = jax.random.key(seed)
        kx, kr, ka = jax.random.split(key, 3)
        B, S, D, DO, E = (4, 512, 1024, 1024, 8)
        x = jax.random.normal(kx, (B, S, D), dtype=jnp.float32)
        bound_r = 1.0 / np.sqrt(D)
        route_w = jax.random.uniform(kr, (E, D), jnp.float32, -bound_r, bound_r)
        bound_a = 1.0 / np.sqrt(D)
        A = jax.random.uniform(ka, (E, R, D), jnp.float32, -bound_a, bound_a)
        kb = jax.random.fold_in(key, 7)
        Bw = jax.random.normal(kb, (E, DO, R), dtype=jnp.float32) * 0.02
        return {'x': x, 'route_w': route_w, 'A': A, 'Bw': Bw}
    _L0_ffn_all = _L0_ffn_setup()
    _L0_ffn_in = {k: v for k, v in _L0_ffn_all.items() if k in ('route_w', 'A', 'Bw')}
    del _L0_ffn_all

    def _L1_cond_setup():
        import jax, jax.numpy as jnp
        import numpy as np
        from jax import lax
        N, C_IN, L = (32, 64, 1024)
        C_OUT, K, GROUPS = (64, 9, 4)
        C_DIM, PAD, STRIDE = (128, 4, 1)
        key = jax.random.key(seed)
        k1, k2, k3, k4, k5 = jax.random.split(key, 5)
        x = jax.random.normal(k1, (N, C_IN, L), dtype=jnp.float32)
        c = jax.random.normal(k2, (N, C_DIM), dtype=jnp.float32)
        weight = jax.random.normal(k3, (C_OUT, C_IN // GROUPS, K), dtype=jnp.float32)
        c_weight = jax.random.normal(k4, (C_OUT, C_DIM), dtype=jnp.float32)
        bias = jax.random.normal(k5, (C_OUT,), dtype=jnp.float32)
        return {'x': x, 'c': c, 'weight': weight, 'c_weight': c_weight, 'bias': bias}
    _L1_cond_all = _L1_cond_setup()
    _L1_cond_in = {k: v for k, v in _L1_cond_all.items() if k in ('weight', 'c_weight')}
    del _L1_cond_all

    def _L1_ffn_setup():
        import jax, jax.numpy as jnp
        import numpy as np
        THRESHOLD = 6.0
        N_OUTLIER_COLS = 16

        def _quantize_weight_rowwise(w):
            scb = jnp.max(jnp.abs(w), axis=1)
            cb = jnp.round(w * (127.0 / jnp.maximum(scb, 1e-08))[:, None])
            cb = jnp.clip(cb, -127.0, 127.0).astype(jnp.int8)
            return (cb, scb)
        key = jax.random.key(seed)
        kx, kw, kb, kc = jax.random.split(key, 4)
        B, S, D, O = (2, 512, 1024, 1024)
        x = jax.random.normal(kx, (B, S, D), dtype=jnp.float32)
        cols = jax.random.choice(kc, D, shape=(N_OUTLIER_COLS,), replace=False)
        x = x.at[:, :, cols].multiply(4.0)
        weight = jax.random.normal(kw, (O, D), dtype=jnp.float32) * 0.02
        bias = jax.random.normal(kb, (O,), dtype=jnp.float32) * 0.01
        return {'x': x, 'weight': weight, 'bias': bias}
    _L1_ffn_all = _L1_ffn_setup()
    _L1_ffn_in = {k: v for k, v in _L1_ffn_all.items() if k in ('weight', 'bias')}
    del _L1_ffn_all

    def _L2_cond_setup():
        import jax, jax.numpy as jnp
        import numpy as np
        from jax import lax
        N, C_IN, L = (32, 64, 1024)
        C_OUT, K, GROUPS = (64, 9, 4)
        C_DIM, PAD, STRIDE = (128, 4, 1)
        key = jax.random.key(seed)
        k1, k2, k3, k4, k5 = jax.random.split(key, 5)
        x = jax.random.normal(k1, (N, C_IN, L), dtype=jnp.float32)
        c = jax.random.normal(k2, (N, C_DIM), dtype=jnp.float32)
        weight = jax.random.normal(k3, (C_OUT, C_IN // GROUPS, K), dtype=jnp.float32)
        c_weight = jax.random.normal(k4, (C_OUT, C_DIM), dtype=jnp.float32)
        bias = jax.random.normal(k5, (C_OUT,), dtype=jnp.float32)
        return {'x': x, 'c': c, 'weight': weight, 'c_weight': c_weight, 'bias': bias}
    _L2_cond_all = _L2_cond_setup()
    _L2_cond_in = {k: v for k, v in _L2_cond_all.items() if k in ('weight', 'c_weight')}
    del _L2_cond_all

    def _L2_ffn_setup():
        import jax, jax.numpy as jnp
        import numpy as np
        TOP_K = 2
        SCALING = 32.0 / 64.0
        key = jax.random.key(seed)
        ks = jax.random.split(key, 6)
        Bsz, S, Din, Dout, R, E = (4, 512, 1024, 1024, 64, 16)
        x = jax.random.normal(ks[0], (Bsz, S, Din), dtype=jnp.float32)
        base_w = jax.random.normal(ks[1], (Dout, Din), dtype=jnp.float32) * 0.02
        base_b = jax.random.normal(ks[2], (Dout,), dtype=jnp.float32) * 0.02
        A = jax.random.normal(ks[3], (R, Din), dtype=jnp.float32) * (1.0 / np.sqrt(Din))
        B = jax.random.normal(ks[4], (E, Dout, R), dtype=jnp.float32) * 0.02
        router_w = jax.random.normal(ks[5], (E, Din), dtype=jnp.float32) * 0.02
        return {'x': x, 'base_w': base_w, 'base_b': base_b, 'A': A, 'B': B, 'router_w': router_w}
    _L2_ffn_all = _L2_ffn_setup()
    _L2_ffn_in = {k: v for k, v in _L2_ffn_all.items() if k in ('base_w', 'base_b', 'A', 'B', 'router_w')}
    del _L2_ffn_all

    def _L3_cond_setup():
        import jax, jax.numpy as jnp
        import numpy as np
        K = 8
        T = 1.0
        D_EMBD = 128
        IN_C = 64
        OUT_C = 64
        BS = 32
        H = 1024
        HID = 128
        key = jax.random.key(seed)
        ks = jax.random.split(key, 10)
        s = lambda fan_in: 1.0 / np.sqrt(fan_in)
        return {'x': jax.random.normal(ks[0], (BS, IN_C, H), dtype=jnp.float32), 'embedding': jax.random.normal(ks[1], (BS, D_EMBD), dtype=jnp.float32), 'W0': jax.random.normal(ks[2], (D_EMBD, HID), dtype=jnp.float32) * s(D_EMBD), 'b0': jnp.zeros((HID,), dtype=jnp.float32), 'W1': jax.random.normal(ks[3], (HID, HID), dtype=jnp.float32) * s(HID), 'b1': jnp.zeros((HID,), dtype=jnp.float32), 'W2': jax.random.normal(ks[4], (HID, K), dtype=jnp.float32) * s(HID), 'b2': jnp.zeros((K,), dtype=jnp.float32), 'weight': jax.random.normal(ks[5], (K, OUT_C, IN_C, 1), dtype=jnp.float32) * s(IN_C), 'bias_k': jax.random.normal(ks[6], (K, OUT_C), dtype=jnp.float32) * 0.1}
    _L3_cond_all = _L3_cond_setup()
    _L3_cond_in = {k: v for k, v in _L3_cond_all.items() if k in ('W0', 'b0', 'W1', 'b1', 'W2', 'b2', 'weight', 'bias_k')}
    del _L3_cond_all

    def _L3_ffn_setup():
        import jax, jax.numpy as jnp
        import numpy as np
        HID, INT, LAT, NE, K = (1024, 2048, 512, 8, 2)
        LN_EPS = 1e-05

        def _layernorm(x, gamma, beta):
            mu = jnp.mean(x, axis=-1, keepdims=True)
            var = jnp.var(x, axis=-1, keepdims=True)
            return (x - mu) * jax.lax.rsqrt(var + LN_EPS) * gamma + beta
        key = jax.random.key(seed)
        ks = jax.random.split(key, 8)
        s = lambda d: 1.0 / np.sqrt(d)
        return {'hidden_states': jax.random.normal(ks[0], (4, 512, HID), jnp.float32), 'gate_w': jax.random.normal(ks[1], (HID, NE), jnp.float32) * s(HID), 'up_w': jax.random.normal(ks[2], (HID, INT), jnp.float32) * s(HID), 'down_w': jax.random.normal(ks[3], (INT, HID), jnp.float32) * s(INT), 'fc1_w': jax.random.normal(ks[4], (HID, LAT), jnp.float32) * s(HID), 'fc2_w': jax.random.normal(ks[5], (LAT, HID), jnp.float32) * s(LAT), 'expert_w': jax.random.normal(ks[6], (LAT, LAT), jnp.float32), 'ln_gamma': jnp.ones((HID,), jnp.float32), 'ln_beta': jnp.zeros((HID,), jnp.float32)}
    _L3_ffn_all = _L3_ffn_setup()
    _L3_ffn_in = {k: v for k, v in _L3_ffn_all.items() if k in ('gate_w', 'up_w', 'down_w', 'fc1_w', 'fc2_w', 'expert_w', 'ln_gamma', 'ln_beta')}
    del _L3_ffn_all
    return {'x': x, 'cond_128': cond_128, 'fside_S_0': fside_S_0, 'L0_cond_W0': _L0_cond_in['W0'], 'L0_cond_b0': _L0_cond_in['b0'], 'L0_cond_W1': _L0_cond_in['W1'], 'L0_cond_b1': _L0_cond_in['b1'], 'L0_cond_W2': _L0_cond_in['W2'], 'L0_cond_b2': _L0_cond_in['b2'], 'L0_cond_weight': _L0_cond_in['weight'], 'L0_cond_bias_k': _L0_cond_in['bias_k'], 'L0_ffn_route_w': _L0_ffn_in['route_w'], 'L0_ffn_A': _L0_ffn_in['A'], 'L0_ffn_Bw': _L0_ffn_in['Bw'], 'L1_cond_weight': _L1_cond_in['weight'], 'L1_cond_c_weight': _L1_cond_in['c_weight'], 'L1_ffn_weight': _L1_ffn_in['weight'], 'L1_ffn_bias': _L1_ffn_in['bias'], 'L2_cond_weight': _L2_cond_in['weight'], 'L2_cond_c_weight': _L2_cond_in['c_weight'], 'L2_ffn_base_w': _L2_ffn_in['base_w'], 'L2_ffn_base_b': _L2_ffn_in['base_b'], 'L2_ffn_A': _L2_ffn_in['A'], 'L2_ffn_B': _L2_ffn_in['B'], 'L2_ffn_router_w': _L2_ffn_in['router_w'], 'L3_cond_W0': _L3_cond_in['W0'], 'L3_cond_b0': _L3_cond_in['b0'], 'L3_cond_W1': _L3_cond_in['W1'], 'L3_cond_b1': _L3_cond_in['b1'], 'L3_cond_W2': _L3_cond_in['W2'], 'L3_cond_b2': _L3_cond_in['b2'], 'L3_cond_weight': _L3_cond_in['weight'], 'L3_cond_bias_k': _L3_cond_in['bias_k'], 'L3_ffn_gate_w': _L3_ffn_in['gate_w'], 'L3_ffn_up_w': _L3_ffn_in['up_w'], 'L3_ffn_down_w': _L3_ffn_in['down_w'], 'L3_ffn_fc1_w': _L3_ffn_in['fc1_w'], 'L3_ffn_fc2_w': _L3_ffn_in['fc2_w'], 'L3_ffn_expert_w': _L3_ffn_in['expert_w'], 'L3_ffn_ln_gamma': _L3_ffn_in['ln_gamma'], 'L3_ffn_ln_beta': _L3_ffn_in['ln_beta']}

def reference(x, cond_128, fside_S_0, L0_cond_W0, L0_cond_b0, L0_cond_W1, L0_cond_b1, L0_cond_W2, L0_cond_b2, L0_cond_weight, L0_cond_bias_k, L0_ffn_route_w, L0_ffn_A, L0_ffn_Bw, L1_cond_weight, L1_cond_c_weight, L1_ffn_weight, L1_ffn_bias, L2_cond_weight, L2_cond_c_weight, L2_ffn_base_w, L2_ffn_base_b, L2_ffn_A, L2_ffn_B, L2_ffn_router_w, L3_cond_W0, L3_cond_b0, L3_cond_W1, L3_cond_b1, L3_cond_W2, L3_cond_b2, L3_cond_weight, L3_cond_bias_k, L3_ffn_gate_w, L3_ffn_up_w, L3_ffn_down_w, L3_ffn_fc1_w, L3_ffn_fc2_w, L3_ffn_expert_w, L3_ffn_ln_gamma, L3_ffn_ln_beta):
    import jax
    import jax.numpy as jnp

    def _L0_cond_ref(x, embedding, W0, b0, W1, b1, W2, b2, weight, bias_k):
        import jax, jax.numpy as jnp
        import numpy as np
        K = 8
        T = 1.0
        D_EMBD = 128
        IN_C = 64
        OUT_C = 64
        BS = 32
        H = 1024
        HID = 128
        h = jax.nn.gelu(embedding @ W0 + b0, approximate=False)
        h = jax.nn.gelu(h @ W1 + b1, approximate=False)
        att = jax.nn.softmax((h @ W2 + b2) / T, axis=-1)
        agg_w = jnp.einsum('bk,koi->boi', att, weight[..., 0])
        agg_b = att @ bias_k
        out = jnp.einsum('boi,bih->boh', agg_w, x) + agg_b[:, :, None]
        return out

    def _L0_ffn_ref(x, route_w, A, Bw):
        import jax, jax.numpy as jnp
        import numpy as np
        R = 16
        LORA_ALPHA = 16
        SCALING = LORA_ALPHA / R
        logits = jnp.einsum('bsd,ed->bse', x, route_w)
        topk_v, topk_idx = jax.lax.top_k(logits, 1)
        E = logits.shape[-1]
        route_weight = jax.nn.one_hot(topk_idx[..., 0], E, dtype=logits.dtype) * topk_v
        h = jnp.einsum('bsd,erd->bser', x, A)
        wh = route_weight[..., None] * h
        out = jnp.einsum('bser,eor->bso', wh, Bw) * SCALING
        return out

    def _L1_cond_ref(x, c, weight, c_weight, bias):
        import jax, jax.numpy as jnp
        import numpy as np
        from jax import lax
        N, C_IN, L = (32, 64, 1024)
        C_OUT, K, GROUPS = (64, 9, 4)
        C_DIM, PAD, STRIDE = (128, 4, 1)
        out = lax.conv_general_dilated(x, weight, window_strides=(STRIDE,), padding=[(PAD, PAD)], dimension_numbers=('NCH', 'OIH', 'NCH'), feature_group_count=GROUPS)
        ctx = jnp.einsum('nd,od->no', c, c_weight)
        out = out + ctx[:, :, None] + bias[None, :, None]
        return out

    def _L1_ffn_ref(x, weight, bias):
        import jax, jax.numpy as jnp
        import numpy as np
        THRESHOLD = 6.0
        N_OUTLIER_COLS = 16

        def _quantize_weight_rowwise(w):
            scb = jnp.max(jnp.abs(w), axis=1)
            cb = jnp.round(w * (127.0 / jnp.maximum(scb, 1e-08))[:, None])
            cb = jnp.clip(cb, -127.0, 127.0).astype(jnp.int8)
            return (cb, scb)
        CB, SCB = _quantize_weight_rowwise(weight)
        B, S, D = x.shape
        xf = x.reshape(-1, D)
        outlier = jnp.any(jnp.abs(xf) > THRESHOLD, axis=0)
        x_int = jnp.where(outlier[None, :], 0.0, xf)
        x_out = jnp.where(outlier[None, :], xf, 0.0)
        row_absmax = jnp.maximum(jnp.max(jnp.abs(x_int), axis=1), 1e-08)
        Cx = jnp.round(x_int * (127.0 / row_absmax)[:, None]).astype(jnp.int8)
        acc = jnp.matmul(Cx.astype(jnp.int32), CB.T.astype(jnp.int32))
        out_i8 = acc.astype(jnp.float32) * (row_absmax[:, None] / 127.0) * (SCB[None, :] / 127.0)
        W_deq_T = CB.T.astype(jnp.float32) * (SCB / 127.0)[None, :]
        out = out_i8 + jnp.matmul(x_out, W_deq_T) + bias[None, :]
        return out.reshape(B, S, -1)

    def _L2_cond_ref(x, c, weight, c_weight, bias):
        import jax, jax.numpy as jnp
        import numpy as np
        from jax import lax
        N, C_IN, L = (32, 64, 1024)
        C_OUT, K, GROUPS = (64, 9, 4)
        C_DIM, PAD, STRIDE = (128, 4, 1)
        out = lax.conv_general_dilated(x, weight, window_strides=(STRIDE,), padding=[(PAD, PAD)], dimension_numbers=('NCH', 'OIH', 'NCH'), feature_group_count=GROUPS)
        ctx = jnp.einsum('nd,od->no', c, c_weight)
        out = out + ctx[:, :, None] + bias[None, :, None]
        return out

    def _L2_ffn_ref(x, base_w, base_b, A, B, router_w):
        import jax, jax.numpy as jnp
        import numpy as np
        TOP_K = 2
        SCALING = 32.0 / 64.0
        base_out = jnp.einsum('bsi,oi->bso', x, base_w) + base_b
        res_hidden = jnp.einsum('bsi,ri->bsr', x, A)
        logits = jnp.einsum('bsi,ei->bse', x, router_w)
        probs = jax.nn.softmax(logits, axis=-1)
        topw, topi = jax.lax.top_k(probs, TOP_K)
        topw = topw / (jnp.sum(topw, axis=-1, keepdims=True) + 1e-06)
        num_experts = B.shape[0]
        combine = jnp.sum(jax.nn.one_hot(topi, num_experts, dtype=x.dtype) * topw[..., None], axis=-2)
        delta = jnp.einsum('bse,bsr,eor->bso', combine, res_hidden, B)
        return base_out + delta * SCALING

    def _L3_cond_ref(x, embedding, W0, b0, W1, b1, W2, b2, weight, bias_k):
        import jax, jax.numpy as jnp
        import numpy as np
        K = 8
        T = 1.0
        D_EMBD = 128
        IN_C = 64
        OUT_C = 64
        BS = 32
        H = 1024
        HID = 128
        h = jax.nn.gelu(embedding @ W0 + b0, approximate=False)
        h = jax.nn.gelu(h @ W1 + b1, approximate=False)
        att = jax.nn.softmax((h @ W2 + b2) / T, axis=-1)
        agg_w = jnp.einsum('bk,koi->boi', att, weight[..., 0])
        agg_b = att @ bias_k
        out = jnp.einsum('boi,bih->boh', agg_w, x) + agg_b[:, :, None]
        return out

    def _L3_ffn_ref(hidden_states, gate_w, up_w, down_w, fc1_w, fc2_w, expert_w, ln_gamma, ln_beta):
        import jax, jax.numpy as jnp
        import numpy as np
        HID, INT, LAT, NE, K = (1024, 2048, 512, 8, 2)
        LN_EPS = 1e-05

        def _layernorm(x, gamma, beta):
            mu = jnp.mean(x, axis=-1, keepdims=True)
            var = jnp.var(x, axis=-1, keepdims=True)
            return (x - mu) * jax.lax.rsqrt(var + LN_EPS) * gamma + beta
        logits = jnp.einsum('bsh,he->bse', hidden_states, gate_w)
        routing_weights, selected_experts = jax.lax.top_k(logits, K)
        h = jax.nn.relu(jnp.einsum('bsh,hi->bsi', hidden_states, up_w)) ** 2
        shared_out = jnp.einsum('bsi,ih->bsh', h, down_w)
        x_latent = jnp.einsum('bsh,hl->bsl', hidden_states, fc1_w)
        expert_out = jnp.einsum('bsl,lm->bsm', x_latent, expert_w)
        moe_out = expert_out * jnp.sum(routing_weights, axis=-1, keepdims=True)
        routed_out = jnp.einsum('bsl,lh->bsh', moe_out, fc2_w)
        return _layernorm(shared_out + routed_out, ln_gamma, ln_beta)
    x = x + _L0_ffn_ref(_L0_cond_ref(x, cond_128, L0_cond_W0, L0_cond_b0, L0_cond_W1, L0_cond_b1, L0_cond_W2, L0_cond_b2, L0_cond_weight, L0_cond_bias_k), L0_ffn_route_w, L0_ffn_A, L0_ffn_Bw)
    x = x + _L1_ffn_ref(_L1_cond_ref(x, cond_128, L1_cond_weight, L1_cond_c_weight, fside_S_0), L1_ffn_weight, L1_ffn_bias)
    x = x + _L2_ffn_ref(_L2_cond_ref(x, cond_128, L2_cond_weight, L2_cond_c_weight, fside_S_0), L2_ffn_base_w, L2_ffn_base_b, L2_ffn_A, L2_ffn_B, L2_ffn_router_w)
    x = x + _L3_ffn_ref(_L3_cond_ref(x, cond_128, L3_cond_W0, L3_cond_b0, L3_cond_W1, L3_cond_b1, L3_cond_W2, L3_cond_b2, L3_cond_weight, L3_cond_bias_k), L3_ffn_gate_w, L3_ffn_up_w, L3_ffn_down_w, L3_ffn_fc1_w, L3_ffn_fc2_w, L3_ffn_expert_w, L3_ffn_ln_gamma, L3_ffn_ln_beta)
    return x

_drawn_inputs = setup_inputs


def setup_inputs(seed=0):
    import zlib

    import numpy as np

    out = dict(_drawn_inputs(seed))
    spreads = {'L0_cond_b0': (0.0, 0.1),
     'L0_cond_b1': (0.0, 0.1),
     'L0_cond_b2': (0.0, 0.1),
     'L3_cond_b0': (0.0, 0.1),
     'L3_cond_b1': (0.0, 0.1),
     'L3_cond_b2': (0.0, 0.1),
     'L3_ffn_ln_gamma': (1.0, 0.2),
     'L3_ffn_ln_beta': (0.0, 0.1)}
    factors = {}
    for name, (base, spread) in spreads.items():
        noise = np.random.default_rng([zlib.crc32(name.encode()), seed]).standard_normal(out[name].shape)
        drawn = base * np.exp(spread * noise) if base else spread * noise
        out[name] = jnp.asarray(drawn.astype(out[name].dtype))
    for name, factor in factors.items():
        out[name] = (out[name] * factor).astype(out[name].dtype)
    return out
```

```python
from contextlib import ExitStack

import concourse.bass as bass
from concourse import mybir

F32 = mybir.dt.float32
F32R = mybir.dt.float32r
ALU = mybir.AluOpType
ACT = mybir.ActivationFunctionType
AX = mybir.AxisListType

P = 128
BATCH, CH, D = 32, 64, 1024
TOK = BATCH * CH
NT = TOK // P
KC = D // P
HALF = D // 2
COND = 128
NK = 8
TAPS, PAD, GROUPS = 9, 4, 4
GI = CH // GROUPS
E0, R0 = 8, 16
E2, R2 = 16, 64
NINT, NLAT = 16, 4
ROUND = 1.5 * 2.0 ** 23
THRESHOLD = 6.0
LN_EPS = 1e-5
BIG = 3.0e38



def product(pe, out, lhs, rhs, start, stop, exact_rhs=False):
    pe.matmul(out, lhs[0], rhs[0], start=start, stop=False)
    if exact_rhs:
        return pe.matmul(out, lhs[1], rhs[0], start=False, stop=stop)
    pe.matmul(out, lhs[0], rhs[1], start=False, stop=False)
    return pe.matmul(out, lhs[1], rhs[0], start=False, stop=stop)


def as_f32(ap):
    return ap.bitcast(F32)


def pipelined(eng, body):
    body(0, 0, 1, 0, True, False)
    with eng.Fori(0, NT // 2 - 1) as j:
        body(2 * j + 1, 1, j + 1, j + 1, True, True)
        body(2 * j + 2, 0, j + 2, j + 1, True, True)
    body(NT - 1, 1, NT // 2, NT // 2, True, True)
    body(NT, 0, NT // 2 + 1, NT // 2, False, True)


class Scope:

    def __init__(self, nc, ctx):
        self.nc, self.ctx, self.owned = nc, ctx, []

    def semaphore(self, name):
        self.owned.append(self.ctx.enter_context(self.nc.semaphore(name)))
        return self.owned[-1]

    def block(self):
        self.ctx.callback(self.clear)
        return self.ctx.enter_context(self.nc.Block())

    def clear(self):
        numbers = sorted(sem.num for sem in self.owned)
        with self.nc.Block() as block:
            @block.gpsimd
            def _(pool):
                first = 0
                for n in range(1, len(numbers) + 1):
                    if n == len(numbers) or numbers[n] != numbers[n - 1] + 1:
                        pool.sem_clear(range(numbers[first], numbers[n - 1] + 1))
                        first = n

    def sb(self, name, shape, dt=F32):
        return self.ctx.enter_context(self.nc.sbuf_tensor(name, shape, dt))

    def split(self, name, shape):
        return self.sb(name + "_hi", shape, F32R), self.sb(name + "_lo", shape, F32R)

    def ps(self, name, shape):
        return self.ctx.enter_context(self.nc.psum_tensor(name, shape, F32))

    def sems(self, names):
        return [self.semaphore(n) for n in names.split()]

    def slot_sems(self, name, slots=2):
        return [self.semaphore(f"{name}{i}") for i in range(slots)]


def phase_constants(nc, K, A):
    with ExitStack() as ctx:
        s = Scope(nc, ctx)
        zeroed, made = s.sems("ident_zeroed ident_made")
        block = s.block()

        @block.gpsimd
        def _(pool):
            pool.memset(K["ident"][:], 0.0).then_inc(zeroed, 1)
            pool.memset(K["ones"][:], 1.0).then_inc(made, 1)
            pool.wait_ge(zeroed, 1)
            pool.affine_select(out=K["ident"][:], in_=K["ident"][:], compare_op=ALU.not_equal, fill=1.0,
                               base=0, pattern=[[-1, P]], channel_multiplier=1).then_inc(made, 1)
            for e in range(E2):
                pool.memset(K["desc"][:, e:e + 1], float(E2 - e)).then_inc(made, 1)

        @block.vector
        def _(dve):
            for raw in K["taps_raw"]:
                dve.memset(raw[:], 0.0).then_inc(made, 1)
            dve.wait_ge(made, 2 + E2 + 2)
            dve.tensor_copy(K["ones_r"][:], K["ones"][:]).then_inc(made, 1)


def phase_condition(nc, K, A, SC):
    with ExitStack() as ctx:
        s = Scope(nc, ctx)
        cT = s.sb("cT", [COND, BATCH])
        W = {}
        for L in "03":
            W[L] = dict(w0=s.sb(f"w0_{L}", [COND, P]), w1=s.sb(f"w1_{L}", [P, P]), w2=s.sb(f"w2_{L}", [P, NK]),
                        b0=s.sb(f"b0_{L}", [P, 1]), b1=s.sb(f"b1_{L}", [P, 1]), b2=s.sb(f"b2_{L}", [BATCH, NK]),
                        bk=s.sb(f"bk_{L}", [NK, CH]), h0=s.sb(f"h0_{L}", [P, BATCH]), h1=s.sb(f"h1_{L}", [P, BATCH]),
                        lg=s.sb(f"lg_{L}", [BATCH, NK]), m=s.sb(f"m_{L}", [BATCH, 1]), nm=s.sb(f"nm_{L}", [BATCH, 1]),
                        ex=s.sb(f"ex_{L}", [BATCH, NK]), z=s.sb(f"z_{L}", [BATCH, 1]), rz=s.sb(f"rz_{L}", [BATCH, 1]),
                        att=s.sb(f"att_{L}", [BATCH, NK]), attT=s.sb(f"attT_{L}", [NK, BATCH]),
                        bias=s.sb(f"bias_{L}", [BATCH, CH]))
        cw1 = s.sb("cw1", [COND, 2, CH])
        cw2 = s.sb("cw2", [COND, CH])
        fside_col = s.sb("fside_col", [P, 1])
        fside_row = s.sb("fside_row", [BATCH, CH])
        ctx2 = s.sb("ctx2", [BATCH, CH])
        pm = s.ps("pm", [P, 512])
        pc = s.ps("pc", [P, 512])
        pd = s.ps("pd", [P, 512])
        loaded, mlp, act, dve_done, stored, ctx_mm, ctx_out = s.sems(
            "cond_loaded mlp_mm mlp_act mlp_dve cond_stored ctx_mm ctx_out")
        block = s.block()
        loads = []
        for L in "03":
            w = W[L]
            loads += [(w["w0"][:], A[f"L{L}_cond_W0"]), (w["w1"][:], A[f"L{L}_cond_W1"]), (w["w2"][:], A[f"L{L}_cond_W2"]),
                      (w["b0"][:], A[f"L{L}_cond_b0"].rearrange("(p a) -> p a", a=1)),
                      (w["b1"][:], A[f"L{L}_cond_b1"].rearrange("(p a) -> p a", a=1)),
                      (w["b2"][:], A[f"L{L}_cond_b2"].partition_broadcast(BATCH)),
                      (w["bk"][:], A[f"L{L}_cond_bias_k"])]
        loads += [(cT[:], A["condT"]), (cw1[:, 0, :], A["L1_cond_c_weight_T"]), (cw1[:, 1, :], A["L1_cond_c_weight_T"]),
                  (cw2[:], A["L2_cond_c_weight_T"]), (fside_row[:], A["fside_S_0"].partition_broadcast(BATCH))]
        fcol = A["fside_S_0"].rearrange("(p a) -> p a", a=1)
        loads += [(fside_col[0:CH, :], fcol), (fside_col[CH:P, :], fcol)]
        for raw, name in zip(K["taps_raw"], ("L1_cond_taps", "L2_cond_taps")):
            for b in range(2):
                for g in range(GROUPS):
                    r = b * CH + g * GI
                    loads.append((raw[r:r + GI, :, r:r + GI], A[name][g].rearrange("i (k o) -> i k o", k=TAPS)))
        all_loaded = 16 * len(loads)

        @block.sync
        def _(sp):
            for dst, src in loads:
                sp.dma_start(dst, src).then_inc(loaded, 16)
            for n, L in enumerate("03"):
                sp.wait_ge(dve_done, 6 * n + 5)
                sp.dma_start(SC[f"att{L}"], W[L]["att"][:]).then_inc(stored, 16)
                sp.wait_ge(stored, 16 * (3 * n + 1))
                sp.dma_start(W[L]["attT"][:], SC[f"att{L}"].rearrange("b k -> k b"),
                             allow_slow_non_contiguous=True).then_inc(stored, 16)
                sp.wait_ge(dve_done, 6 * n + 6)
                sp.dma_start(SC[f"bias{L}"], W[L]["bias"][:]).then_inc(stored, 16)
                sp.wait_ge(stored, 16 * (3 * n + 3))
            sp.wait_ge(ctx_out, 3)
            sp.dma_start(SC["ctx2"], ctx2[:]).then_inc(stored, 16)
            sp.wait_ge(stored, 16 * 7)
            for n, L in enumerate("03"):
                src = SC[f"att{L}"].rearrange("(t b) k -> b t k", b=2)
                for b in range(2):
                    sp.dma_start(K[f"att{L}"][b * CH:(b + 1) * CH, :, :],
                                 src[b].partition_broadcast(CH)).then_inc(stored, 16)
                for b in range(2):
                    sp.dma_start(K[f"kern{L}"][b * CH:(b + 1) * CH, :, :],
                                 A[f"L{L}_cond_kernels"].rearrange("i (k o) -> i k o", k=NK)).then_inc(stored, 16)
            sp.wait_ge(stored, 16 * 15)

        @block.tensor
        def _(pe):
            pe.wait_ge(loaded, all_loaded)
            pe.matmul(pc[:, 0:BATCH], cw1[:].rearrange("d b o -> d (b o)"), cT[:], start=True, stop=True).then_inc(ctx_mm, 1)
            pe.matmul(pd[0:BATCH, 0:CH], cT[:], cw2[:], start=True, stop=True).then_inc(ctx_mm, 1)
            for n, L in enumerate("03"):
                w = W[L]
                if n:
                    pe.wait_ge(dve_done, 6)
                pe.matmul(pm[:, 0:BATCH], w["w0"][:], cT[:], start=True, stop=True).then_inc(mlp, 1)
                pe.wait_ge(act, 3 * n + 1)
                pe.matmul(pm[:, 0:BATCH], w["w1"][:], w["h0"][:], start=True, stop=True).then_inc(mlp, 1)
                pe.wait_ge(act, 3 * n + 2)
                pe.matmul(pm[0:BATCH, 0:NK], w["h1"][:], w["w2"][:], start=True, stop=True).then_inc(mlp, 1)
                pe.wait_ge(stored, 16 * (3 * n + 2))
                pe.wait_ge(dve_done, 6 * n + 1)
                pe.matmul(pm[0:BATCH, 0:CH], w["attT"][:], w["bk"][:], start=True, stop=True).then_inc(mlp, 1)

        @block.scalar
        def _(act_e):
            act_e.wait_ge(loaded, all_loaded)
            for n, L in enumerate("03"):
                w = W[L]
                act_e.wait_ge(mlp, 4 * n + 1)
                act_e.activation(w["h0"][:], pm[:, 0:BATCH], ACT.Gelu, bias=w["b0"][:]).then_inc(act, 1)
                act_e.wait_ge(mlp, 4 * n + 2)
                act_e.activation(w["h1"][:], pm[:, 0:BATCH], ACT.Gelu, bias=w["b1"][:]).then_inc(act, 1)
                act_e.wait_ge(dve_done, 6 * n + 3)
                act_e.activation(w["ex"][:], w["lg"][:], ACT.Exp, bias=w["nm"][:],
                                 accum_out=w["z"][:]).then_inc(act, 1)

        @block.vector
        def _(dve):
            dve.wait_ge(ctx_mm, 1)
            dve.wait_ge(loaded, all_loaded)
            pcv = pc[:, 0:BATCH].rearrange("p (t b) -> p b t", b=2)
            for b in range(2):
                rows = slice(b * CH, (b + 1) * CH)
                dve.tensor_scalar(K["ctx1"][rows, :], pcv[rows, b, :], fside_col[rows, :], None, ALU.add).then_inc(ctx_out, 1)
            dve.wait_ge(ctx_mm, 2)
            dve.tensor_tensor(ctx2[:], pd[0:BATCH, 0:CH], fside_row[:], ALU.add).then_inc(ctx_out, 1)
            for n, L in enumerate("03"):
                w, base = W[L], 6 * n
                dve.wait_ge(mlp, 4 * n + 3)
                dve.tensor_tensor(w["lg"][:], pm[0:BATCH, 0:NK], w["b2"][:], ALU.add).then_inc(dve_done, 1)
                dve.wait_ge(dve_done, base + 1)
                dve.tensor_reduce(w["m"][:], w["lg"][:], AX.X, ALU.max).then_inc(dve_done, 1)
                dve.wait_ge(dve_done, base + 2)
                dve.tensor_scalar(w["nm"][:], w["m"][:], -1.0, None, ALU.mult).then_inc(dve_done, 1)
                dve.wait_ge(act, 3 * n + 3)
                dve.reciprocal(w["rz"][:], w["z"][:]).then_inc(dve_done, 1)
                dve.wait_ge(dve_done, base + 4)
                dve.tensor_scalar(w["att"][:], w["ex"][:], w["rz"][:], None, ALU.mult).then_inc(dve_done, 1)
                dve.wait_ge(mlp, 4 * n + 4)
                dve.tensor_copy(w["bias"][:], pm[0:BATCH, 0:CH]).then_inc(dve_done, 1)


def exact_quotient(dve, order, at, out, den, tmp):
    q, dh, dl, qh, ql, r = [tmp[:, i:i + 1] for i in range(6)]
    rec = out
    steps = [
        lambda: dve.reciprocal(rec, den),
        lambda: dve.tensor_scalar(q, rec, 127.0, None, ALU.mult),
        lambda: dve.tensor_scalar(qh, q, 4097.0, None, ALU.mult),
        lambda: dve.tensor_tensor(ql, qh, q, ALU.subtract),
        lambda: dve.tensor_tensor(qh, qh, ql, ALU.subtract),
        lambda: dve.tensor_tensor(ql, q, qh, ALU.subtract),
        lambda: dve.tensor_scalar(dh, den, 4097.0, None, ALU.mult),
        lambda: dve.tensor_tensor(dl, dh, den, ALU.subtract),
        lambda: dve.tensor_tensor(dh, dh, dl, ALU.subtract),
        lambda: dve.tensor_tensor(dl, den, dh, ALU.subtract),
        lambda: dve.tensor_tensor(r, qh, dh, ALU.mult),
        lambda: dve.tensor_scalar(r, r, -1.0, 127.0, ALU.mult, ALU.add),
        lambda: dve.tensor_tensor(dh, dh, ql, ALU.mult),
        lambda: dve.tensor_tensor(r, r, dh, ALU.subtract),
        lambda: dve.tensor_tensor(qh, qh, dl, ALU.mult),
        lambda: dve.tensor_tensor(r, r, qh, ALU.subtract),
        lambda: dve.tensor_tensor(ql, ql, dl, ALU.mult),
        lambda: dve.tensor_tensor(r, r, ql, ALU.subtract),
        lambda: dve.tensor_tensor(r, r, rec, ALU.mult),
        lambda: dve.tensor_tensor(out, q, r, ALU.add),
    ]
    for n, step in enumerate(steps):
        step().then_inc(order, 1)
        dve.wait_ge(order, at + n + 1)
    return at + len(steps)


QUOT = 20


def broadcast_columns(pe, dve, K, ps_pair, col, diag, row, made, copied, n0):
    pass


def phase_quantize_weight(nc, K, A):
    with ExitStack() as ctx:
        s = Scope(nc, ctx)
        raw = s.sb("qw_raw", [P, 2, D])
        cb = s.sb("qw_cb", [P, D])
        col = s.sb("qw_col", [P, 4])
        tmp = s.sb("qw_tmp", [P, 8])
        diag = s.sb("qw_diag", [P, P])
        tp = [s.ps(f"qw_tp{i}", [P, 512]) for i in range(2)]
        bc = s.ps("qw_bc", [P, 512])
        loaded = s.slot_sems("qw_loaded")
        order, rounded, turned, taken, diag_made, spread, spread_out = s.sems(
            "qw_order cb_rounded cb_turned cb_taken scb_diag scb_spread scb_row_out")
        per = QUOT + 4
        block = s.block()

        @block.sync
        def _(sp):
            for c in range(KC):
                if c >= 2:
                    sp.wait_ge(rounded, c - 1)
                sp.dma_start(raw[:, c % 2, :], A["L1_ffn_weight"][c * P:(c + 1) * P, :]).then_inc(loaded[c % 2], 16)

        @block.vector
        def _(dve):
            for c in range(KC):
                at, w = per * c, raw[:, c % 2, :]
                dve.wait_ge(loaded[c % 2], 16 * (c // 2 + 1))
                dve.tensor_reduce(col[:, 0:1], w, AX.X, ALU.max, apply_absolute_value=True).then_inc(order, 1)
                dve.wait_ge(order, at + 1)
                dve.tensor_scalar(col[:, 1:2], col[:, 0:1], 1e-8, None, ALU.max).then_inc(order, 1)
                dve.wait_ge(order, at + 2)
                at = exact_quotient(dve, order, at + 2, col[:, 2:3], col[:, 1:2], tmp)
                dve.tensor_scalar(col[:, 3:4], col[:, 0:1], 1.0 / 127.0, None, ALU.mult).then_inc(order, 1)
                dve.tensor_scalar(w, w, col[:, 2:3], ROUND, ALU.mult, ALU.add).then_inc(order, 1)
                dve.wait_ge(order, at + 2)
                if c:
                    dve.wait_ge(turned, 2 * c)
                    dve.wait_ge(spread, c)
                dve.tensor_scalar(cb[:], w, ROUND, None, ALU.subtract).then_inc(rounded, 1)
                dve.tensor_scalar(diag[:], K["ident"][:], col[:, 3:4], None, ALU.mult).then_inc(diag_made, 1)
                dve.wait_ge(diag_made, c + 1)
                dve.wait_ge(spread, c + 1)
                dve.tensor_copy(K["scb_row"][:, c * P:(c + 1) * P], bc[:, 0:P]).then_inc(spread_out, 1)

        @block.tensor
        def _(pe):
            for c in range(KC):
                pe.wait_ge(rounded, c + 1)
                for h in range(2):
                    if c:
                        pe.wait_ge(taken, 2 * (c - 1) + h + 1)
                    for j in range(4):
                        k = 4 * h + j
                        mm = pe.transpose(tp[h][:, j * P:(j + 1) * P], cb[:, k * P:(k + 1) * P], K["ident"][:])
                    mm.then_inc(turned, 1)
                pe.wait_ge(diag_made, c + 1)
                if c:
                    pe.wait_ge(spread_out, c)
                pe.matmul(bc[:, 0:P], K["ones"][:], diag[:], start=True, stop=True).then_inc(spread, 1)

        @block.scalar
        def _(act):
            for c in range(KC):
                for h in range(2):
                    act.wait_ge(turned, 2 * c + h + 1)
                    act.copy(K["cbT"][:, 4 * h:4 * h + 4, c * P:(c + 1) * P],
                             tp[h][:].rearrange("p (k o) -> p k o", k=4)).then_inc(taken, 1)


def phase_latent_weight(nc, K, A, SC):
    with ExitStack() as ctx:
        s = Scope(nc, ctx)
        fc1 = s.sb("fc1_raw", [P, NLAT, D])
        exp = s.sb("exp_raw", [P, NLAT, 512])
        fc1s = s.split("fc1_s", [P, NLAT, D])
        exps = s.split("exp_s", [P, NLAT, 512])
        gout = s.sb("g_out", [P, 2, 512])
        pg = [s.ps(f"pg{i}", [P, 512]) for i in range(2)]
        loaded, hi, lo, mm, out = s.sems("fc_loaded fc_hi fc_lo g_mm g_out_ready")
        stored = s.slot_sems("g_stored")
        block = s.block()

        @block.sync
        def _(sp):
            sp.dma_start(fc1[:], A["fc1T"].rearrange("(l p) h -> p l h", p=P)).then_inc(loaded, 16)
            sp.dma_start(exp[:], A["L3_ffn_expert_w"].rearrange("(l p) m -> p l m", p=P)).then_inc(loaded, 16)
            for k in range(KC):
                sp.wait_ge(out, k + 1)
                sp.dma_start(SC["g"][:, :, k, :].rearrange("c p j -> p c j"),
                             gout[:, k % 2, :].rearrange("p (c j) -> p c j", c=NLAT)).then_inc(stored[k % 2], 16)
            for slot in stored:
                sp.wait_ge(slot, 16 * KC // 2)

        @block.scalar
        def _(act):
            act.wait_ge(loaded, 32)
            act.copy(fc1s[0][:], fc1[:]).then_inc(hi, 1)
            act.copy(exps[0][:], exp[:]).then_inc(hi, 1)

        @block.vector
        def _(dve):
            dve.wait_ge(hi, 1)
            dve.tensor_tensor(fc1s[1][:], fc1[:], as_f32(fc1s[0][:]), ALU.subtract).then_inc(lo, 1)
            dve.wait_ge(hi, 2)
            dve.tensor_tensor(exps[1][:], exp[:], as_f32(exps[0][:]), ALU.subtract).then_inc(lo, 1)
            for k in range(KC):
                dve.wait_ge(mm, k + 1)
                if k >= 2:
                    dve.wait_ge(stored[k % 2], 16 * (k // 2))
                dve.tensor_copy(gout[:, k % 2, :], pg[k % 2][:]).then_inc(out, 1)

        @block.tensor
        def _(pe):
            pe.wait_ge(lo, 2)
            for k in range(KC):
                if k >= 2:
                    pe.wait_ge(out, k - 1)
                for l in range(NLAT):
                    last = product(pe, pg[k % 2][:], [w[:, l, k * P:(k + 1) * P] for w in fc1s],
                                   [w[:, l, :] for w in exps], l == 0, l == NLAT - 1)
                last.then_inc(mm, 1)


def split_chunks(nc, jobs, tag):
    n_max = max(src.shape[-1] if len(src.shape) == 2 else src.shape[-1] * src.shape[-2] for src, _, _ in jobs)
    ring = 4
    with ExitStack() as ctx:
        s = Scope(nc, ctx)
        raw = s.sb(f"{tag}_raw", [P, ring, n_max])
        loaded = s.slot_sems(f"{tag}_loaded", ring)
        hi, lo = s.sems(f"{tag}_hi {tag}_lo")
        block = s.block()

        def views(n):
            src, h, l = jobs[n]
            shape = h.shape
            flat = raw[:, n % ring, 0:int(shape[1]) * (int(shape[2]) if len(shape) == 3 else 1)]
            return (flat.rearrange("p (a b) -> p a b", a=int(shape[1])) if len(shape) == 3 else flat), src, h, l

        @block.sync
        def _(sp):
            for n in range(len(jobs)):
                if n >= ring:
                    sp.wait_ge(lo, n - ring + 1)
                r, src, _, _ = views(n)
                sp.dma_start(r, src).then_inc(loaded[n % ring], 16)

        @block.scalar
        def _(act):
            for n in range(len(jobs)):
                r, _, h, _ = views(n)
                act.wait_ge(loaded[n % ring], 16 * (n // ring + 1))
                act.copy(h, r).then_inc(hi, 1)

        @block.vector
        def _(dve):
            for n in range(len(jobs)):
                r, _, h, l = views(n)
                dve.wait_ge(hi, n + 1)
                dve.tensor_tensor(l, r, as_f32(h), ALU.subtract).then_inc(lo, 1)


def split_taps(nc, K):
    with ExitStack() as ctx:
        s = Scope(nc, ctx)
        (hi,) = s.sems("taps_hi")
        block = s.block()

        @block.scalar
        def _(act):
            for raw, t in zip(K["taps_raw"], K["taps"]):
                act.copy(t[0][:], raw[:]).then_inc(hi, 1)

        @block.vector
        def _(dve):
            for n, (raw, t) in enumerate(zip(K["taps_raw"], K["taps"])):
                dve.wait_ge(hi, n + 1)
                dve.tensor_tensor(t[1][:], raw[:], as_f32(t[0][:]), ALU.subtract)


class Mixer:

    def __init__(self, s, tag, att, kern):
        self.att, self.kern = att, kern
        self.acc = s.sb(f"{tag}_acc", [P, CH])
        self.mat = s.split(f"{tag}_mat", [P, P])
        self.row_raw = s.sb(f"{tag}_row_raw", [1, P])
        self.row = s.split(f"{tag}_row", [1, P])
        self.order, self.made, self.hi, self.row_loaded, self.row_hi, self.row_lo, self.zeroed = s.sems(
            " ".join(f"{tag}_{n}" for n in
                     "kern_sum mat_made mat_hi row_loaded row_hi row_lo mat_zeroed".split()))

    def zero(self, dve):
        dve.memset(as_f32(self.mat[0][:]), 0.0).then_inc(self.zeroed, 1)
        dve.memset(as_f32(self.mat[1][:]), 0.0).then_inc(self.zeroed, 1)
        dve.wait_ge(self.zeroed, 2)

    def blocks(self, part):
        return [part[b * CH:(b + 1) * CH, b * CH:(b + 1) * CH] for b in range(2)]

    def build(self, dve, n, t, products):
        for k in range(NK):
            scalar = self.att[:, bass.ds(t, 1), k:k + 1].rearrange("p a b -> p (a b)")
            if k == 0:
                dve.tensor_scalar(self.acc[:], self.kern[:, 0, :], scalar, None, ALU.mult).then_inc(self.order, 1)
            else:
                dve.wait_ge(self.order, n * NK + k)
                dve.scalar_tensor_tensor(out=self.acc[:], in0=self.kern[:, k, :], scalar=scalar, in1=self.acc[:],
                                         op0=ALU.mult, op1=ALU.add).then_inc(self.order, 1)
        dve.wait_ge(self.order, n * NK + NK)
        dve.wait_ge(products, 2 * n + 2)
        for b, dst in enumerate(self.blocks(self.mat[0])):
            dve.tensor_copy(dst, self.acc[b * CH:(b + 1) * CH, :]).then_inc(self.hi, 1)
        dve.wait_ge(self.hi, 2 * n + 2)
        for b, (dst, h) in enumerate(zip(self.blocks(self.mat[1]), self.blocks(self.mat[0]))):
            dve.tensor_tensor(dst, self.acc[b * CH:(b + 1) * CH, :], as_f32(h), ALU.subtract).then_inc(self.made, 1)
        dve.wait_ge(self.row_loaded, 16 * (n + 1))
        dve.tensor_copy(self.row[0][:], self.row_raw[:]).then_inc(self.row_hi, 1)
        dve.wait_ge(self.row_hi, n + 1)
        dve.tensor_tensor(self.row[1][:], self.row_raw[:], as_f32(self.row[0][:]), ALU.subtract).then_inc(self.row_lo, 1)

    def load_row(self, sp, n, bias_dram, t):
        sp.wait_ge(self.row_lo, n + 1)
        sp.dma_start(self.row_raw[:], bias_dram[bass.ds(t, 1), :]).then_inc(self.row_loaded, 16)

    def credits(self, dve):
        dve.sem_inc(self.row_lo, 1)

    def multiply(self, pe, n, x, out, ones_row):
        pe.wait_ge(self.made, 2 * (n + 1))
        pe.wait_ge(self.row_lo, n + 2)
        for c in range(KC):
            o = out[c // 4][:, (c % 4) * P:(c % 4 + 1) * P]
            product(pe, o, [v[:, c * P:(c + 1) * P] for v in x], [m[:] for m in self.mat], True, False)
            pe.matmul(o, ones_row, self.row[0][:], start=False, stop=False)
            last = pe.matmul(o, ones_row, self.row[1][:], start=False, stop=True)
            yield c, last


def first_of_largest(dve, order, at, lg, desc, n, m, key, kmax, mask):
    dve.tensor_reduce(m, lg, AX.X, ALU.max).then_inc(order, 1)
    dve.wait_ge(order, at + 1)
    dve.scalar_tensor_tensor(out=key, in0=lg, scalar=m, in1=desc, op0=ALU.is_ge, op1=ALU.mult).then_inc(order, 1)
    dve.wait_ge(order, at + 2)
    dve.tensor_reduce(kmax, key, AX.X, ALU.max).then_inc(order, 1)
    dve.wait_ge(order, at + 3)
    dve.tensor_scalar(mask, key, kmax, None, ALU.is_equal).then_inc(order, 1)
    dve.wait_ge(order, at + 4)
    return at + 4


def phase_l0(nc, K, A, SC):
    with ExitStack() as ctx:
        s = Scope(nc, ctx)
        wa = s.split("wa", [P, KC, P + E0])
        wb = s.split("wb", [P, D])
        split_chunks(nc, [(A["l0_wa"][k], wa[0][:, k, :], wa[1][:, k, :]) for k in range(KC)]
                     + [(A["l0_wb"], wb[0][:], wb[1][:])], "l0w")
        mix = Mixer(s, "mix0", K["att0"], K["kern0"])
        x = s.sb("x_in", [P, 2, D])
        xs = s.split("x_s", [P, D])
        ys = s.split("y0_s", [P, D])
        wh = s.sb("wh", [P, P])
        whs = s.split("wh_s", [P, P])
        x1 = s.sb("x1", [P, D])
        x1s = [s.split(f"x1_s{i}", [P, D + 2 * PAD]) for i in range(2)]
        y1 = s.sb("y1", [P, 2, D])
        mag = s.sb("y1_mag", [P, D])
        small = s.sb("l0_small", [P, 32])
        m, kmax = small[:, 0:1], small[:, 1:2]
        lg, key, mask = small[:, 8:16], small[:, 16:24], small[:, 24:32]
        py = [s.ps(f"py{i}", [P, 512]) for i in range(2)]
        ph = s.ps("ph", [P, 512])
        pt = s.ps("pt", [P, 512])
        po = [s.ps(f"po{i}", [P, 512]) for i in range(2)]
        pv = [s.ps(f"pv{i}", [P, 512]) for i in range(2)]
        x_loaded, y1_stored = s.slot_sems("x_loaded"), s.slot_sems("y1_stored")
        (x_hi, x_lo, x_free, y_mm, y_hi, y_lo, h_mm, route, wh_made, wh_turned, wh_hi, wh_lo,
         o_mm, x1_made, x1_stored, x1_hi, x1_lo, conv_done, y1_made, mag_made, y1_seen, edge, cmax_set) = s.sems(
            "x_hi x_lo x_read y0_mm y0_hi y0_lo h_mm route_step wh_made wh_turned wh_hi wh_lo o_mm x1_made "
            "x1_stored x1_hi x1_lo conv_done y1_made mag_made y1_seen x1_edges_zeroed cmax_zeroed")
        block = s.block()
        cmax = K["cmax"]

        @block.sync
        def _(sp):
            def body(t, u, nf, nb, front, back):
                if front:
                    sp.wait_ge(x_free, t + 1)
                    sp.dma_start(x[:, u, :], A["x"][bass.ds(t, 1), :, :].rearrange("a p d -> (a p) d")).then_inc(x_loaded[u], 16)
                    mix.load_row(sp, t, SC["bias0"].rearrange("(t b) o -> t (b o)", b=2), t)
                if back:
                    sp.wait_ge(x1_made, 2 * t)
                    sp.dma_start(SC["x1"][bass.ds(t - 1, 1), :, :].rearrange("a p d -> (a p) d"), x1[:]).then_inc(x1_stored, 16)
                    sp.wait_ge(y1_made, 2 * t)
                    sp.dma_start(SC["y1"][bass.ds(t - 1, 1), :, :].rearrange("a p d -> (a p) d"), y1[:, 1 - u, :]).then_inc(y1_stored[1 - u], 16)
            pipelined(sp, body)
            sp.wait_ge(x1_stored, 16 * (NT + 1))
            for slot in y1_stored:
                sp.wait_ge(slot, 16 * (NT // 2 + 1))

        @block.scalar
        def _(act):
            def body(t, u, nf, nb, front, back):
                if front:
                    act.wait_ge(x_loaded[u], 16 * nf)
                    act.wait_ge(y_mm, 2 * t + 2)
                    act.copy(xs[0][:], x[:, u, :]).then_inc(x_hi, 1)
                    for h in range(2):
                        act.wait_ge(y_mm, 2 * t + h + 3)
                        if h == 0:
                            act.wait_ge(h_mm, t + 1)
                        act.copy(ys[0][:, h * HALF:(h + 1) * HALF], py[h][:]).then_inc(y_hi, 1)
                if front:
                    act.wait_ge(wh_turned, t + 1)
                    act.copy(whs[0][:], pt[:, 0:P]).then_inc(wh_hi, 1)
                if back:
                    act.wait_ge(y1_stored[1 - u], 16 * nb)
                    act.wait_ge(y1_seen, t)
                    act.wait_ge(conv_done, t)
                    for h in range(2):
                        act.activation(y1[:, 1 - u, h * HALF:(h + 1) * HALF], pv[h][:], ACT.Identity,
                                       bias=K["ctx1"][:, bass.ds(t - 1, 1)]).then_inc(y1_made, 1)
                        act.activation(mag[:, h * HALF:(h + 1) * HALF], pv[h][:], ACT.Abs,
                                       bias=K["ctx1"][:, bass.ds(t - 1, 1)]).then_inc(mag_made, 1)
                if front:
                    act.wait_ge(x1_made, 2 * (t + 1))
                    if not back:
                        act.wait_ge(edge, 4)
                    act.wait_ge(conv_done, t)  if back else None
                    act.copy(x1s[u][0][:, PAD:PAD + D], x1[:]).then_inc(x1_hi, 1)
            pipelined(act, body)

        @block.vector
        def _(dve):
            mix.zero(dve)
            for pair in x1s:
                for part in pair:
                    dve.memset(as_f32(part[:, 0:PAD]), 0.0)
                    dve.memset(as_f32(part[:, PAD + D:]), 0.0).then_inc(edge, 1)
            dve.memset(cmax[:], 0.0).then_inc(cmax_set, 1)
            dve.wait_ge(cmax_set, 1)
            dve.wait_ge(edge, 4)
            mix.credits(dve)
            dve.sem_inc(x_free, 2)
            dve.sem_inc(y1_seen, 1)
            for slot in y1_stored:
                dve.sem_inc(slot, 16)
            dve.sem_inc(x1_stored, 16)

            def body(t, u, nf, nb, front, back):
                if front:
                    mix.build(dve, t, t, y_mm)
                    dve.wait_ge(x_hi, t + 1)
                    dve.tensor_tensor(xs[1][:], x[:, u, :], as_f32(xs[0][:]), ALU.subtract).then_inc(x_lo, 1)
                    for h in range(2):
                        cols = slice(h * HALF, (h + 1) * HALF)
                        dve.wait_ge(y_hi, 2 * t + h + 1)
                        dve.tensor_tensor(ys[1][:, cols], py[h][:], as_f32(ys[0][:, cols]), ALU.subtract).then_inc(y_lo, 1)
                if front:
                    dve.wait_ge(h_mm, t + 2)
                    dve.tensor_copy(lg, ph[:, P:P + E0]).then_inc(route, 1)
                    dve.wait_ge(route, 6 * t + 1)
                    at = first_of_largest(dve, route, 6 * t + 1, lg, K["desc"][:, E2 - E0:E2], E0, m, key, kmax, mask)
                    dve.tensor_scalar(key, mask, m, None, ALU.mult).then_inc(route, 1)
                    dve.wait_ge(route, at + 1)
                    dve.tensor_tensor(wh[:].rearrange("p (e r) -> p e r", e=E0),
                                      ph[:, 0:P].rearrange("p (e r) -> p e r", e=E0),
                                      key.unsqueeze(2).to_broadcast([P, E0, R0]), ALU.mult).then_inc(wh_made, 1)
                    dve.wait_ge(wh_hi, t + 1)
                    dve.tensor_tensor(whs[1][:], pt[:, 0:P], as_f32(whs[0][:]), ALU.subtract).then_inc(wh_lo, 1)
                if back:
                    dve.wait_ge(mag_made, 2 * t)
                    dve.tensor_tensor(cmax[:], mag[:], cmax[:], ALU.max).then_inc(y1_seen, 1)
                if front:
                    dve.wait_ge(o_mm, t + 1)
                    dve.wait_ge(x1_stored, 16 * (t + 1))
                    if back:
                        dve.wait_ge(x1_lo, t)
                    for h in range(2):
                        cols = slice(h * HALF, (h + 1) * HALF)
                        ins = dve.tensor_tensor(x1[:, cols], po[h][:], x[:, u, cols], ALU.add)
                        ins.then_inc(x1_made, 1)
                    dve.wait_ge(x1_made, 2 * (t + 1))
                    dve.sem_inc(x_free, 1)
                    dve.wait_ge(x1_hi, t + 1)
                    dve.tensor_tensor(x1s[u][1][:, PAD:PAD + D], x1[:], as_f32(x1s[u][0][:, PAD:PAD + D]),
                                      ALU.subtract).then_inc(x1_lo, 1)
            pipelined(dve, body)

        @block.tensor
        def _(pe):
            pe.sem_inc(y_mm, 2)
            pe.sem_inc(h_mm, 1)

            def conv(t, u, n0, n1):
                for n in range(n0, n1):
                    for h in range(2):
                        last = product(pe, pv[h][:], [w[:, n, :] for w in K["taps"][0]],
                                       [v[:, n + h * HALF:n + (h + 1) * HALF] for v in x1s[u]], n == 0, n == TAPS - 1)
                return last

            def body(t, u, nf, nb, front, back):
                if front:
                    pe.wait_ge(x_lo, t + 1)
                    for c, last in mix.multiply(pe, t, xs, py, K["ones_r"][0:1, :]):
                        if c % 4 == 3:
                            last.then_inc(y_mm, 1)
                if back:
                    pe.wait_ge(x1_lo, t)
                    if not isinstance(t, int) or t > 1:
                        pe.wait_ge(mag_made, 2 * (t - 1))
                    conv(t - 1, 1 - u, 0, 4)
                if front:
                    pe.wait_ge(y_lo, 2 * (t + 1))
                    if back:
                        pe.wait_ge(wh_made, t)
                    for k in range(KC):
                        last = product(pe, ph[:, 0:P + E0], [v[:, k * P:(k + 1) * P] for v in ys],
                                       [w[:, k, :] for w in wa], k == 0, k == KC - 1)
                    last.then_inc(h_mm, 1)
                if back:
                    conv(t - 1, 1 - u, 4, 7)
                if front:
                    pe.wait_ge(wh_made, t + 1)
                    if back:
                        pe.wait_ge(wh_lo, t)
                    pe.transpose(pt[:, 0:P], wh[:], K["ident"][:]).then_inc(wh_turned, 1)
                if back:
                    conv(t - 1, 1 - u, 7, TAPS).then_inc(conv_done, 1)
                if front:
                    pe.wait_ge(wh_lo, t + 1)
                    if back:
                        pe.wait_ge(x1_made, 2 * t)
                    for h in range(2):
                        last = product(pe, po[h][:], [v[:] for v in whs],
                                       [w[:, h * HALF:(h + 1) * HALF] for w in wb], True, True)
                    last.then_inc(o_mm, 1)
            pipelined(pe, body)


def phase_outliers(nc, K):
    with ExitStack() as ctx:
        s = Scope(nc, ctx)
        tp = [s.ps(f"ot{i}", [P, 512]) for i in range(2)]
        bc = [s.ps(f"ob{i}", [P, 512]) for i in range(2)]
        top = s.sb("col_top", [P, KC])
        keep = s.sb("col_keep", [P, KC])
        diag = s.sb("keep_diag", [P, KC, P])
        turned, topped, kept, diag_made, spread = s.sems("cmax_turned col_topped col_kept keep_diag_made keep_spread")
        block = s.block()

        @block.tensor
        def _(pe):
            for c in range(KC):
                mm = pe.transpose(tp[c // 4][:, (c % 4) * P:(c % 4 + 1) * P], K["cmax"][:, c * P:(c + 1) * P], K["ident"][:])
            mm.then_inc(turned, 1)
            pe.wait_ge(diag_made, KC)
            for c in range(KC):
                mm = pe.matmul(bc[c // 4][:, (c % 4) * P:(c % 4 + 1) * P], K["ones"][:], diag[:, c, :], start=True, stop=True)
            mm.then_inc(spread, 1)

        @block.vector
        def _(dve):
            dve.wait_ge(turned, 1)
            for h in range(2):
                dve.tensor_reduce(top[:, 4 * h:4 * h + 4], tp[h][:].rearrange("p (c k) -> p c k", c=4), AX.X,
                                  ALU.max).then_inc(topped, 1)
            dve.wait_ge(topped, 2)
            dve.tensor_scalar(keep[:], top[:], THRESHOLD, None, ALU.is_le).then_inc(kept, 1)
            dve.wait_ge(kept, 1)
            for c in range(KC):
                dve.tensor_scalar(diag[:, c, :], K["ident"][:], keep[:, c:c + 1], None, ALU.mult).then_inc(diag_made, 1)
            dve.wait_ge(spread, 1)
            for h in range(2):
                dve.tensor_copy(K["keep_row"][:, h * HALF:(h + 1) * HALF], bc[h][:])


def phase_l1(nc, K, A, SC):
    with ExitStack() as ctx:
        s = Scope(nc, ctx)
        y1 = s.sb("l1_y1", [P, 2, D])
        x1 = s.sb("l1_x1", [P, 2, D])
        bias = s.sb("l1_bias", [P, D])
        yi = s.sb("yi", [P, D])
        z = s.sb("z", [P, D])
        zs = s.split("z_s", [P, D])
        x2 = s.sb("x2", [P, D])
        x2s = [s.split(f"x2_s{i}", [P, D + 2 * PAD]) for i in range(2)]
        y2 = s.sb("y2", [P, 2, D])
        row_raw = s.sb("ctx2_row_raw", [1, 2, P])
        row = s.split("ctx2_row", [1, 2, P])
        col = s.sb("l1_col", [P, 4])
        tmp = s.sb("l1_tmp", [P, 8])
        pz = [s.ps(f"pz{i}", [P, 512]) for i in range(2)]
        pf = [s.ps(f"pf{i}", [P, 512]) for i in range(2)]
        pv = [s.ps(f"pw{i}", [P, 512]) for i in range(2)]
        in_loaded, y2_stored, row_loaded = [s.slot_sems(n) for n in ("l1_in_loaded", "y2_stored", "ctx2_loaded")]
        (x1_free, bias_loaded, q, z_made, z_turned, z_hi, z_lo, f_mm, xb, x2_step, x2_made,
         x2_stored, x2_hi, x2_lo, conv_done, y2_made, edge, row_hi, row_lo) = s.sems(
            "l1_x1_read l1_bias_loaded quant_step z_made z_turned z_hi z_lo f_mm xb_made "
            "x2_step x2_made x2_stored x2_hi x2_lo conv2_done y2_made x2_edges_zeroed "
            "ctx2_hi ctx2_lo")
        QS = 7 + QUOT
        block = s.block()

        def tile(ap, t):
            return ap[bass.ds(t, 1), :, :].rearrange("a p d -> (a p) d")

        @block.sync
        def _(sp):
            sp.dma_start(bias[:], A["L1_ffn_bias"].partition_broadcast(P)).then_inc(bias_loaded, 16)

            def body(t, u, nf, nb, front, back):
                if front:
                    sp.wait_ge(z_made, t + 1)
                    sp.dma_start(y1[:, u, :], tile(SC["y1"], t)).then_inc(in_loaded[u], 16)
                    sp.wait_ge(x1_free, t + 1)
                    sp.dma_start(x1[:, u, :], tile(SC["x1"], t)).then_inc(in_loaded[u], 16)
                    sp.wait_ge(row_lo, t + 1)
                    sp.dma_start(row_raw[:, u, :], SC["ctx2"].rearrange("(t b) o -> t (b o)", b=2)[bass.ds(t, 1), :]
                                 ).then_inc(row_loaded[u], 16)
                if back:
                    sp.wait_ge(x2_made, 2 * t)
                    sp.dma_start(tile(SC["x2"], t - 1), x2[:]).then_inc(x2_stored, 16)
                    sp.wait_ge(y2_made, 2 * t)
                    sp.dma_start(tile(SC["y2T"], t - 1), y2[:, 1 - u, :]).then_inc(y2_stored[1 - u], 16)
            pipelined(sp, body)
            sp.wait_ge(x2_stored, 16 * (NT + 1))
            for slot in y2_stored:
                sp.wait_ge(slot, 16 * (NT // 2 + 1))

        @block.gpsimd
        def _(pool):
            pool.sem_inc(x1_free, 2)
            pool.wait_ge(bias_loaded, 16)

            def body(t, u, nf, nb, front, back):
                if front:
                    pool.wait_ge(in_loaded[u], 32 * nf)
                    pool.tensor_tensor(x1[:, u, :], x1[:, u, :], bias[:], ALU.add).then_inc(xb, 1)
            pipelined(pool, body)

        @block.scalar
        def _(act):
            def body(t, u, nf, nb, front, back):
                if front:
                    for h in range(2):
                        act.wait_ge(z_turned, 2 * t + h + 1)
                        if h == 0:
                            act.wait_ge(f_mm, t + 1)
                        act.copy(zs[0][:, h * HALF:(h + 1) * HALF], pz[h][:]).then_inc(z_hi, 1)
                if back:
                    act.wait_ge(y2_stored[1 - u], 16 * nb)
                    act.wait_ge(conv_done, 2 * t - 1)
                    act.copy(y2[:, 1 - u, 0:HALF], pv[0][:]).then_inc(y2_made, 1)
                if front:
                    act.wait_ge(x2_made, 2 * (t + 1))
                    if not back:
                        act.wait_ge(edge, 4)
                    act.copy(x2s[u][0][:, PAD:PAD + D], x2[:]).then_inc(x2_hi, 1)
                if back:
                    act.wait_ge(conv_done, 2 * t)
                    act.copy(y2[:, 1 - u, HALF:D], pv[1][:]).then_inc(y2_made, 1)
            pipelined(act, body)

        @block.vector
        def _(dve):
            for pair in x2s:
                for part in pair:
                    dve.memset(as_f32(part[:, 0:PAD]), 0.0)
                    dve.memset(as_f32(part[:, PAD + D:]), 0.0).then_inc(edge, 1)
            dve.wait_ge(edge, 4)
            dve.sem_inc(z_made, 2)
            dve.sem_inc(row_lo, 2)
            dve.sem_inc(x2_stored, 16)
            for slot in y2_stored:
                dve.sem_inc(slot, 16)

            def body(t, u, nf, nb, front, back):
                if not front:
                    return
                at = QS * t
                y = y1[:, u, :]
                dve.wait_ge(row_loaded[u], 16 * nf)
                dve.tensor_copy(row[0][:, u, :], row_raw[:, u, :]).then_inc(row_hi, 1)
                dve.wait_ge(row_hi, t + 1)
                dve.tensor_tensor(row[1][:, u, :], row_raw[:, u, :], as_f32(row[0][:, u, :]), ALU.subtract).then_inc(row_lo, 1)
                dve.wait_ge(in_loaded[u], 32 * nf)
                dve.tensor_tensor(yi[:], y, K["keep_row"][:], ALU.mult).then_inc(q, 1)
                dve.wait_ge(q, at + 1)
                dve.tensor_reduce(col[:, 0:1], yi[:], AX.X, ALU.max, apply_absolute_value=True).then_inc(q, 1)
                dve.wait_ge(q, at + 2)
                dve.tensor_scalar(col[:, 1:2], col[:, 0:1], 1e-8, None, ALU.max).then_inc(q, 1)
                dve.tensor_tensor(y, y, yi[:], ALU.subtract).then_inc(q, 1)
                dve.wait_ge(q, at + 4)
                exact_quotient(dve, q, at + 4, col[:, 2:3], col[:, 1:2], tmp)
                at = at + 4 + QUOT
                dve.tensor_scalar(col[:, 3:4], col[:, 1:2], 1.0 / 127.0, None, ALU.mult).then_inc(q, 1)
                dve.tensor_scalar(yi[:], yi[:], col[:, 2:3], ROUND, ALU.mult, ALU.add).then_inc(q, 1)
                dve.wait_ge(q, at + 2)
                dve.tensor_scalar(yi[:], yi[:], ROUND, None, ALU.subtract).then_inc(q, 1)
                dve.wait_ge(q, at + 3)
                if back:
                    dve.wait_ge(z_turned, 2 * t)
                dve.scalar_tensor_tensor(out=z[:], in0=yi[:], scalar=col[:, 3:4], in1=y, op0=ALU.mult,
                                         op1=ALU.add).then_inc(z_made, 1)
                dve.wait_ge(z_made, t + 3)
                for h in range(2):
                    cols = slice(h * HALF, (h + 1) * HALF)
                    dve.wait_ge(z_hi, 2 * t + h + 1)
                    dve.tensor_tensor(zs[1][:, cols], pz[h][:], as_f32(zs[0][:, cols]), ALU.subtract).then_inc(z_lo, 1)
                dve.wait_ge(f_mm, t + 2)
                dve.wait_ge(x2_stored, 16 * (t + 1))
                if back:
                    dve.wait_ge(x2_lo, t)
                for h in range(2):
                    cols = slice(h * HALF, (h + 1) * HALF)
                    dve.tensor_tensor(x2[:, cols], pf[h][:], K["scb_row"][:, cols], ALU.mult).then_inc(x2_step, 1)
                dve.wait_ge(xb, t + 1)
                for h in range(2):
                    cols = slice(h * HALF, (h + 1) * HALF)
                    dve.wait_ge(x2_step, 2 * t + h + 1)
                    dve.tensor_tensor(x2[:, cols], x2[:, cols], x1[:, u, cols], ALU.add).then_inc(x2_made, 1)
                dve.wait_ge(x2_made, 2 * (t + 1))
                dve.sem_inc(x1_free, 1)
                dve.wait_ge(x2_hi, t + 1)
                dve.tensor_tensor(x2s[u][1][:, PAD:PAD + D], x2[:], as_f32(x2s[u][0][:, PAD:PAD + D]),
                                  ALU.subtract).then_inc(x2_lo, 1)
            pipelined(dve, body)

        @block.tensor
        def _(pe):
            pe.sem_inc(f_mm, 1)

            def conv(u, c0, c1):
                for c in range(c0, c1):
                    o = pv[c // 4][:, (c % 4) * P:(c % 4 + 1) * P]
                    for n in range(TAPS):
                        product(pe, o, [v[:, c * P + n:c * P + n + P] for v in x2s[u]],
                                [w[:, n, :] for w in K["taps"][1]], n == 0, False)
                    pe.matmul(o, K["ones_r"][0:1, :], row[0][:, u, :], start=False, stop=False)
                    last = pe.matmul(o, K["ones_r"][0:1, :], row[1][:, u, :], start=False, stop=True)
                    if c % 4 == 3:
                        last.then_inc(conv_done, 1)

            def body(t, u, nf, nb, front, back):
                if front:
                    pe.wait_ge(z_made, t + 3)
                    for h in range(2):
                        if back:
                            pe.wait_ge(z_lo, 2 * t)
                        for j in range(4):
                            k = 4 * h + j
                            mm = pe.transpose(pz[h][:, j * P:(j + 1) * P], z[:, k * P:(k + 1) * P], K["ident"][:])
                        mm.then_inc(z_turned, 1)
                if back:
                    pe.wait_ge(x2_lo, t)
                    if not isinstance(t, int) or t > 1:
                        pe.wait_ge(y2_made, 2 * (t - 1))
                    conv(1 - u, 0, 4)
                if front:
                    pe.wait_ge(z_lo, 2 * (t + 1))
                    if back:
                        pe.wait_ge(x2_made, 2 * t)
                    for h in range(2):
                        for k in range(KC):
                            last = product(pe, pf[h][:], [v[:, k * P:(k + 1) * P] for v in zs],
                                           [K["cbT"][:, k, h * HALF:(h + 1) * HALF]], k == 0, k == KC - 1, exact_rhs=True)
                    last.then_inc(f_mm, 1)
                if back:
                    conv(1 - u, 4, 8)
            pipelined(pe, body)


def phase_l2(nc, K, A, SC, W):
    with ExitStack() as ctx:
        s = Scope(nc, ctx)
        war = s.split("war", [P, KC, R2 + E2])
        split_chunks(nc, [(A["l2_war"][k], war[0][:, k, :], war[1][:, k, :]) for k in range(KC)]
                     + [(A["l2_base"][k], W[0][:, k, :], W[1][:, k, :]) for k in range(KC)]
                     + [(A["l2_B"][k], W[0][:, KC + k, :], W[1][:, KC + k, :]) for k in range(KC)], "l2w")
        y2 = s.sb("l2_y2", [P, 2, D])
        x2 = s.sb("l2_x2", [P, 2, D])
        ys = [s.split(f"l2_ys{i}", [P, D]) for i in range(2)]
        bias = s.sb("l2_bias", [P, D])
        cr = s.sb("cr", [P, D])
        crs = s.split("cr_s", [P, D])
        x3 = s.sb("x3", [P, D])
        sm = s.sb("l2_small", [P, 16, E2])
        res = s.sb("l2_res", [P, R2])
        m, nm, kmax, z, tot = [sm[:, 0, i:i + 1] for i in range(5)]
        m2 = sm[:, 0, 5:6]
        lg, key, one, two, ex, lg2 = [sm[:, i, :] for i in range(1, 7)]
        pr = s.ps("pr", [P, 512])
        pc = [s.ps(f"pcr{i}", [P, 512]) for i in range(2)]
        po = [s.ps(f"pl2_{i}", [P, 512]) for i in range(2)]
        in_loaded = s.slot_sems("l2_in_loaded")
        (bias_loaded, y_hi, y_lo, r_mm, mixw, e_done, cr_made, cr_turned, cr_hi, cr_lo, o_mm, xb, x3_made,
         x3_stored, x2_free, recip_done, mix_ready) = s.sems(
            "l2_bias_loaded l2_y_hi l2_y_lo r_mm mix_step exp_done cr_made cr_turned cr_hi cr_lo l2_o_mm "
            "l2_xb x3_made x3_stored l2_x2_read recip_done mix_ready")
        MS = 17
        block = s.block()

        def tile(ap, t):
            return ap[bass.ds(t, 1), :, :].rearrange("a p d -> (a p) d")

        @block.sync
        def _(sp):
            sp.dma_start(bias[:], A["L2_ffn_base_b"].partition_broadcast(P)).then_inc(bias_loaded, 16)

            def body(t, u, nf, nb, front, back):
                if front:
                    sp.wait_ge(y_lo, t + 1)
                    sp.dma_start(y2[:, u, :], tile(SC["y2T"], t)).then_inc(in_loaded[u], 16)
                    sp.wait_ge(x2_free, t + 1)
                    sp.dma_start(x2[:, u, :], tile(SC["x2"], t)).then_inc(in_loaded[u], 16)
                if back:
                    sp.wait_ge(x3_made, 2 * t)
                    sp.dma_start(tile(SC["x3"], t - 1), x3[:]).then_inc(x3_stored, 16)
            pipelined(sp, body)
            sp.wait_ge(x3_stored, 16 * (NT + 1))

        @block.gpsimd
        def _(pool):
            pool.wait_ge(bias_loaded, 16)

            def body(t, u, nf, nb, front, back):
                if front:
                    pool.wait_ge(in_loaded[u], 32 * nf)
                    pool.tensor_tensor(x2[:, u, :], x2[:, u, :], bias[:], ALU.add).then_inc(xb, 1)
            pipelined(pool, body)

        @block.scalar
        def _(act):
            def body(t, u, nf, nb, front, back):
                if back:
                    for h in range(2):
                        act.wait_ge(cr_turned, 2 * (t - 1) + h + 1)
                        if h == 0:
                            act.wait_ge(o_mm, t)
                        act.copy(crs[0][:, h * HALF:(h + 1) * HALF], pc[h][:]).then_inc(cr_hi, 1)
                if front:
                    act.wait_ge(in_loaded[u], 32 * nf)
                    act.wait_ge(o_mm, t)  if back else None
                    act.copy(ys[u][0][:], y2[:, u, :]).then_inc(y_hi, 1)
                    act.wait_ge(mixw, MS * t + 3)
                    act.activation(ex, lg, ACT.Exp, bias=nm, accum_out=z).then_inc(e_done, 1)
            pipelined(act, body)

        @block.vector
        def _(dve):
            dve.sem_inc(y_lo, 2)
            dve.sem_inc(x2_free, 2)
            dve.sem_inc(x3_stored, 16)

            def body(t, u, nf, nb, front, back):
                if back:
                    for h in range(2):
                        cols = slice(h * HALF, (h + 1) * HALF)
                        dve.wait_ge(cr_hi, 2 * (t - 1) + h + 1)
                        dve.tensor_tensor(crs[1][:, cols], pc[h][:], as_f32(crs[0][:, cols]), ALU.subtract).then_inc(cr_lo, 1)
                if front:
                    dve.wait_ge(y_hi, t + 1)
                    dve.tensor_tensor(ys[u][1][:], y2[:, u, :], as_f32(ys[u][0][:]), ALU.subtract).then_inc(y_lo, 1)
                    at = MS * t
                    dve.wait_ge(r_mm, t + 1)
                    dve.tensor_copy(lg, pr[:, R2:R2 + E2]).then_inc(mixw, 1)
                    dve.wait_ge(mixw, at + 1)
                    dve.tensor_reduce(m, lg, AX.X, ALU.max).then_inc(mixw, 1)
                    dve.wait_ge(mixw, at + 2)
                    dve.tensor_scalar(nm, m, -1.0, None, ALU.mult).then_inc(mixw, 1)
                    dve.tensor_copy(res[:], pr[:, 0:R2]).then_inc(mixw, 1)
                    dve.wait_ge(mixw, at + 4)
                    at = first_of_largest(dve, mixw, at + 4, lg, K["desc"][:], E2, m, key, kmax, one)
                    dve.scalar_tensor_tensor(out=lg2, in0=one, scalar=-BIG, in1=lg, op0=ALU.mult, op1=ALU.add).then_inc(mixw, 1)
                    dve.wait_ge(mixw, at + 1)
                    at = first_of_largest(dve, mixw, at + 1, lg2, K["desc"][:], E2, m2, key, kmax, two)
                    dve.tensor_tensor(one, one, two, ALU.add).then_inc(mixw, 1)
                    dve.wait_ge(mixw, at + 1)
                    dve.wait_ge(e_done, t + 1)
                    dve.tensor_tensor(key, ex, one, ALU.mult).then_inc(mixw, 1)
                    dve.wait_ge(mixw, at + 2)
                    dve.tensor_reduce(tot, key, AX.X, ALU.add).then_inc(mixw, 1)
                    dve.wait_ge(mixw, at + 3)
                    dve.scalar_tensor_tensor(out=tot, in0=z, scalar=1e-6, in1=tot, op0=ALU.mult, op1=ALU.add).then_inc(mixw, 1)
                    dve.wait_ge(mixw, at + 4)
                    assert_steps(at + 4 - MS * t, MS, t)
                    dve.reciprocal(kmax, tot).then_inc(recip_done, 1)
                    dve.wait_ge(recip_done, t + 1)
                    dve.tensor_scalar(key, key, kmax, 0.5, ALU.mult, ALU.mult).then_inc(mix_ready, 1)
                    dve.wait_ge(mix_ready, t + 1)
                    if back:
                        dve.wait_ge(cr_turned, 2 * t)
                    dve.tensor_tensor(cr[:].rearrange("p (e r) -> p e r", e=E2),
                                      key.unsqueeze(2).to_broadcast([P, E2, R2]),
                                      res[:].unsqueeze(1).to_broadcast([P, E2, R2]), ALU.mult).then_inc(cr_made, 1)
                if back:
                    dve.wait_ge(o_mm, t + 1)
                    dve.wait_ge(xb, t)
                    dve.wait_ge(x3_stored, 16 * t)
                    for h in range(2):
                        cols = slice(h * HALF, (h + 1) * HALF)
                        dve.tensor_tensor(x3[:, cols], po[h][:], x2[:, 1 - u, cols], ALU.add).then_inc(x3_made, 1)
                    dve.wait_ge(x3_made, 2 * t)
                    dve.sem_inc(x2_free, 1)
            pipelined(dve, body)

        @block.tensor
        def _(pe):
            pe.sem_inc(o_mm, 1)

            def body(t, u, nf, nb, front, back):
                if back:
                    pe.wait_ge(cr_made, t)
                    for h in range(2):
                        if not isinstance(t, int) or t > 1:
                            pe.wait_ge(cr_lo, 2 * (t - 1))
                        for j in range(4):
                            k = 4 * h + j
                            mm = pe.transpose(pc[h][:, j * P:(j + 1) * P], cr[:, k * P:(k + 1) * P], K["ident"][:])
                        mm.then_inc(cr_turned, 1)
                    if not isinstance(t, int) or t > 1:
                        pe.wait_ge(x3_made, 2 * (t - 1))
                    for h in range(2):
                        for k in range(KC):
                            product(pe, po[h][:], [v[:, k * P:(k + 1) * P] for v in ys[1 - u]],
                                    [w[:, k, h * HALF:(h + 1) * HALF] for w in W], k == 0, False)
                if front:
                    pe.wait_ge(y_lo, t + 3)
                    if back:
                        pe.wait_ge(mixw, MS * (t - 1) + 4)
                    for k in range(KC):
                        last = product(pe, pr[:, 0:R2 + E2], [v[:, k * P:(k + 1) * P] for v in ys[u]],
                                       [w[:, k, :] for w in war], k == 0, k == KC - 1)
                    last.then_inc(r_mm, 1)
                if back:
                    pe.wait_ge(cr_lo, 2 * t)
                    for h in range(2):
                        for k in range(KC):
                            last = product(pe, po[h][:], [v[:, k * P:(k + 1) * P] for v in crs],
                                           [w[:, KC + k, h * HALF:(h + 1) * HALF] for w in W], False, k == KC - 1)
                    last.then_inc(o_mm, 1)
            pipelined(pe, body)


def assert_steps(got, want, t):
    if isinstance(t, int):
        assert got == want, (got, want)


HT = NT // 2
HTOK = HT * P


def phase_l3(nc, K, A, SC, half, out):
    with ExitStack() as ctx:
        s = Scope(nc, ctx)
        tag = f"h{half}_"
        ys = s.split(tag + "y3", [P, KC, HTOK])
        acc = s.sb(tag + "acc", [P, HT, D])
        srow = s.sb(tag + "srow", [P, HTOK])

        def tile(ap, t):
            return ap[bass.ds(t, 1), :, :].rearrange("a p d -> (a p) d")

        with ExitStack() as c2:
            s2 = Scope(nc, c2)
            mix = Mixer(s2, tag + "mix", K["att3"], K["kern3"])
            gate_raw = s2.sb(tag + "gate_raw", [P, KC, E0])
            gate = s2.split(tag + "gate", [P, KC, E0])
            x = s2.sb(tag + "x", [P, 2, D])
            xs = s2.split(tag + "xs", [P, D])
            top = s2.sb(tag + "top", [P, HT, 8])
            ssum = s2.sb(tag + "ssum", [P, HT])
            diag = s2.sb(tag + "diag", [P, HT, P])
            lgs = s2.sb(tag + "lgs", [P, HT, E0])
            py = [s2.ps(f"{tag}py{i}", [P, 512]) for i in range(2)]
            pg = s2.ps(tag + "pg", [P, 512])
            pb = [s2.ps(f"{tag}pb{i}", [P, 512]) for i in range(2)]
            x_loaded = s2.slot_sems(tag + "x_loaded")
            (x_hi, x_lo, y_mm, y_hi, y_lo, g_loaded, g_hi, g_lo, g_mm, g_step, spread, x_free) = s2.sems(
                " ".join(tag + n for n in "x_hi x_lo y_mm y_hi y_lo gate_loaded gate_hi gate_lo gate_mm "
                                          "gate_step s_spread x_free".split()))
            block = s2.block()

            @block.sync
            def _(sp):
                sp.dma_start(gate_raw[:], A["L3_ffn_gate_w"].rearrange("(k p) e -> p k e", p=P)).then_inc(g_loaded, 16)
                with sp.Fori(0, HT // 2) as pair:
                    for u in range(2):
                        t = 2 * pair + u
                        sp.wait_ge(x_lo, t + 1)
                        sp.dma_start(x[:, u, :], tile(SC["x3"], t + half * HT)).then_inc(x_loaded[u], 16)
                        mix.load_row(sp, t, SC["bias3"].rearrange("(t b) o -> t (b o)", b=2), t + half * HT)

            @block.scalar
            def _(act):
                act.wait_ge(g_loaded, 16)
                act.copy(gate[0][:], gate_raw[:]).then_inc(g_hi, 1)
                with act.Fori(0, HT // 2) as pair:
                    for u in range(2):
                        t = 2 * pair + u
                        act.wait_ge(x_loaded[u], 16 * (pair + 1))
                        act.wait_ge(y_mm, 2 * (t + 1))
                        act.copy(xs[0][:], x[:, u, :]).then_inc(x_hi, 1)
                        for h in range(2):
                            act.wait_ge(y_mm, 2 * t + h + 3)
                            act.copy(ys[0][:, 4 * h:4 * h + 4, bass.ds(t * P, P)],
                                     py[h][:].rearrange("p (c k) -> p c k", c=4)).then_inc(y_hi, 1)

            @block.vector
            def _(dve):
                mix.zero(dve)
                mix.credits(dve)
                dve.sem_inc(x_lo, 2)
                dve.wait_ge(g_hi, 1)
                dve.tensor_tensor(gate[1][:], gate_raw[:], as_f32(gate[0][:]), ALU.subtract).then_inc(g_lo, 1)
                with dve.Fori(0, HT // 2) as pair:
                    for u in range(2):
                        t = 2 * pair + u
                        mix.build(dve, t, t + half * HT, y_mm)
                        dve.wait_ge(x_hi, t + 1)
                        dve.tensor_tensor(xs[1][:], x[:, u, :], as_f32(xs[0][:]), ALU.subtract).then_inc(x_lo, 1)
                        for h in range(2):
                            dve.wait_ge(y_hi, 2 * t + h + 1)
                            dve.tensor_tensor(ys[1][:, 4 * h:4 * h + 4, bass.ds(t * P, P)],
                                              py[h][:].rearrange("p (c k) -> p c k", c=4),
                                              as_f32(ys[0][:, 4 * h:4 * h + 4, bass.ds(t * P, P)]),
                                              ALU.subtract).then_inc(y_lo, 1)
                dve.wait_ge(g_mm, 1)
                dve.tensor_copy(lgs[:].rearrange("p t e -> p (t e)"), pg[:, 0:HT * E0]).then_inc(g_step, 1)
                dve.wait_ge(g_step, 1)
                for t in range(HT):
                    dve.max(out=top[:, t, :], in_=lgs[:, t, :]).then_inc(g_step, 1)
                dve.wait_ge(g_step, 1 + HT)
                dve.tensor_tensor(ssum[:].unsqueeze(2), top[:, :, 0:1], top[:, :, 1:2], ALU.add).then_inc(g_step, 1)
                dve.wait_ge(g_step, 2 + HT)
                for t in range(HT):
                    dve.tensor_scalar(diag[:, t, :], K["ident"][:], ssum[:, t:t + 1], None, ALU.mult).then_inc(g_step, 1)
                dve.wait_ge(spread, 1)
                for h in range(2):
                    dve.tensor_copy(srow[:, h * HALF:(h + 1) * HALF], pb[h][:])

            @block.tensor
            def _(pe):
                pe.sem_inc(y_mm, 2)
                with pe.Fori(0, HT // 2) as pair:
                    for u in range(2):
                        t = 2 * pair + u
                        pe.wait_ge(x_lo, t + 3)
                        for c, last in mix.multiply(pe, t, xs, py, K["ones_r"][0:1, :]):
                            if c % 4 == 3:
                                last.then_inc(y_mm, 1)
                        pe.wait_ge(y_lo, 2 * (t + 1))
                pe.wait_ge(g_lo, 1)
                for t in range(HT):
                    for k in range(KC):
                        last = product(pe, pg[:, t * E0:(t + 1) * E0], [v[:, k, t * P:(t + 1) * P] for v in ys],
                                       [w[:, k, :] for w in gate], k == 0, k == KC - 1)
                last.then_inc(g_mm, 1)
                pe.wait_ge(g_step, 2 + 2 * HT)
                for t in range(HT):
                    last = pe.matmul(pb[t // 4][:, (t % 4) * P:(t % 4 + 1) * P], K["ones"][:], diag[:, t, :],
                                     start=True, stop=True)
                last.then_inc(spread, 1)

        with ExitStack() as c2:
            s2 = Scope(nc, c2)
            NCH = NINT + NLAT
            up_raw = s2.sb(tag + "up_raw", [P, 2, D])
            dn_raw = s2.sb(tag + "dn_raw", [P, 2, D])
            ups = [s2.split(f"{tag}up{i}", [P, KC, P]) for i in range(2)]
            dns = [s2.split(f"{tag}dn{i}", [P, D]) for i in range(2)]
            r = s2.sb(tag + "r", [P, HTOK])
            hid = s2.sb(tag + "hid", [P, HTOK])
            hs = [s2.split(f"{tag}h{i}", [P, HTOK]) for i in range(2)]
            pu = [s2.ps(f"{tag}pu{i}", [P, 512]) for i in range(2)]
            pd = [[s2.ps(f"{tag}pd{v}{i}", [P, 512]) for i in range(2)] for v in range(2)]
            w_loaded = s2.slot_sems(tag + "w_loaded")
            (up_hi, dn_hi, up_lo, dn_lo, up_mm, relu, sq, h_hi, h_lo, dn_mm, added, acc_set) = s2.sems(
                " ".join(tag + n for n in "up_hi dn_hi up_lo dn_lo up_mm relu squared h_hi h_lo dn_mm added acc_zeroed".split()))
            block = s2.block()

            def steps(eng, body):
                body(0, 0, 1, True, False, False)
                with eng.Fori(0, NINT // 2 - 1) as j:
                    body(2 * j + 1, 1, j + 1, True, True, False)
                    body(2 * j + 2, 0, j + 2, True, True, False)
                body(NINT - 1, 1, NINT // 2, True, True, False)
                for c in range(NINT, NCH):
                    body(c, c % 2, c // 2 + 1, True, True, True)
                body(NCH, NCH % 2, NCH // 2 + 1, False, True, True)

            @block.sync
            def _(sp):
                def body(c, u, nf, front, back, lat):
                    if not front:
                        return
                    sp.wait_ge(dn_lo, c + 1)
                    sp.wait_ge(up_lo, c + 1)
                    up, dn, j = (SC["g2"], A["fc2"], c - NINT) if lat else (A["up"], A["down"], c)
                    sp.dma_start(up_raw[:, u, :], up[bass.ds(j, 1), :, :].rearrange("a p d -> (a p) d")).then_inc(w_loaded[u], 16)
                    sp.dma_start(dn_raw[:, u, :], tile(dn, j)).then_inc(w_loaded[u], 16)
                steps(sp, body)

            @block.gpsimd
            def _(pool):
                for t in range(HT):
                    pool.memset(acc[:, t, :], 0.0).then_inc(acc_set, 1)
                pool.sem_inc(dn_lo, 2)

                def body(c, u, nf, front, back, lat):
                    if not front:
                        return
                    pool.wait_ge(dn_hi, c + 1)
                    pool.tensor_tensor(dns[u][1][:], dn_raw[:, u, :], as_f32(dns[u][0][:]), ALU.subtract).then_inc(dn_lo, 1)
                steps(pool, body)

            @block.scalar
            def _(act):
                def body(c, u, nf, front, back, lat):
                    if not front:
                        return
                    act.wait_ge(w_loaded[u], 32 * nf)
                    act.wait_ge(dn_mm, HT * c + HT)
                    act.copy(ups[u][0][:].rearrange("p k j -> p (k j)"), up_raw[:, u, :]).then_inc(up_hi, 1)
                    act.copy(dns[u][0][:], dn_raw[:, u, :]).then_inc(dn_hi, 1)
                    for h in range(2):
                        cols = slice(h * HALF, (h + 1) * HALF)
                        if not lat:
                            act.wait_ge(up_mm, 2 * c + h + 1)
                            act.wait_ge(sq, 2 * c + h)
                            act.activation(r[:, cols], pu[h][:], ACT.Relu).then_inc(relu, 1)
                    for h in range(2):
                        cols = slice(h * HALF, (h + 1) * HALF)
                        act.wait_ge(sq, 2 * c + h + 3)
                        act.copy(hs[u][0][:, cols], hid[:, cols]).then_inc(h_hi, 1)
                steps(act, body)

            @block.vector
            def _(dve):
                dve.sem_inc(up_lo, 2)
                dve.sem_inc(sq, 2)
                dve.sem_inc(added, 2)
                dve.wait_ge(acc_set, HT)

                def body(c, u, nf, front, back, lat):
                    if front:
                        dve.wait_ge(up_hi, c + 1)
                        dve.tensor_tensor(ups[u][1][:].rearrange("p k j -> p (k j)"), up_raw[:, u, :],
                                          as_f32(ups[u][0][:]).rearrange("p k j -> p (k j)"), ALU.subtract).then_inc(up_lo, 1)

                    def hidden():
                        for h in range(2):
                            cols = slice(h * HALF, (h + 1) * HALF)
                            if back:
                                dve.wait_ge(h_lo, 2 * (c - 1) + h + 1)
                            if lat:
                                dve.wait_ge(up_mm, 2 * c + h + 1)
                                dve.tensor_tensor(hid[:, cols], pu[h][:], srow[:, cols], ALU.mult).then_inc(sq, 1)
                            else:
                                dve.wait_ge(relu, 2 * c + h + 1)
                                dve.tensor_tensor(hid[:, cols], r[:, cols], r[:, cols], ALU.mult).then_inc(sq, 1)
                        for h in range(2):
                            cols = slice(h * HALF, (h + 1) * HALF)
                            dve.wait_ge(h_hi, 2 * c + h + 1)
                            dve.tensor_tensor(hs[u][1][:, cols], hid[:, cols], as_f32(hs[u][0][:, cols]),
                                              ALU.subtract).then_inc(h_lo, 1)
                    for t in range(HT):
                        if back:
                            dve.wait_ge(dn_mm, HT * (c - 1) + t + 1 + 2 * HT)
                            for h in range(2):
                                cols = slice(h * HALF, (h + 1) * HALF)
                                last = dve.tensor_tensor(acc[:, t, cols], pd[t % 2][h][:], acc[:, t, cols], ALU.add)
                            last.then_inc(added, 1)
                        if t == 1 and front:
                            hidden()
                steps(dve, body)

            @block.tensor
            def _(pe):
                pe.sem_inc(dn_mm, 2 * HT)

                def body(c, u, nf, front, back, lat):
                    def down(t):
                        if back:
                            pe.wait_ge(added, HT * (c - 1) + t + 1)
                            for h in range(2):
                                last = product(pe, pd[t % 2][h][:], [v[:, t * P:(t + 1) * P] for v in hs[1 - u]],
                                               [w[:, h * HALF:(h + 1) * HALF] for w in dns[1 - u]], True, True)
                            last.then_inc(dn_mm, 1)
                    if front:
                        pe.wait_ge(up_lo, c + 3)
                        for h in range(2):
                            if back:
                                pe.wait_ge(sq, 2 * (c - 1) + h + 3)
                            for k in range(KC):
                                last = product(pe, pu[h][:], [w[:, k, :] for w in ups[u]],
                                               [v[:, k, h * HALF:(h + 1) * HALF] for v in ys], k == 0, k == KC - 1)
                            last.then_inc(up_mm, 1)
                    if back:
                        pe.wait_ge(h_lo, 2 * c)
                        pe.wait_ge(dn_lo, c + 2)
                        for t in range(HT):
                            down(t)
                steps(pe, body)

        with ExitStack() as c2:
            s2 = Scope(nc, c2)
            gamma = s2.sb(tag + "gamma", [P, D])
            beta = s2.sb(tag + "beta", [P, D])
            x = s2.sb(tag + "xr", [P, 2, D])
            stats = s2.sb(tag + "stats", [P, HT, 2, 6])
            mv = s2.sb(tag + "mv", [P, HT, 2])
            rstd = s2.sb(tag + "rstd", [P, HT])
            nmr = s2.sb(tag + "nmr", [P, HT])
            eps = s2.sb(tag + "eps", [P, 1])
            x_loaded = s2.slot_sems(tag + "ln_x_loaded")
            (g_loaded, st, agg, rt, inv, nm, norm, scaled, xb, done, stored, eps_set) = s2.sems(
                " ".join(tag + n for n in "ln_g_loaded ln_stats ln_agg ln_root ln_inv ln_shift ln_norm ln_scaled "
                                          "ln_xb ln_done ln_stored ln_eps".split()))
            block = s2.block()

            @block.sync
            def _(sp):
                sp.dma_start(gamma[:], A["L3_ffn_ln_gamma"].partition_broadcast(P)).then_inc(g_loaded, 16)
                sp.dma_start(beta[:], A["L3_ffn_ln_beta"].partition_broadcast(P)).then_inc(g_loaded, 16)
                for t in range(HT):
                    if t >= 2:
                        sp.wait_ge(done, t - 1)
                    sp.dma_start(x[:, t % 2, :], SC["x3"][half * HT + t]).then_inc(x_loaded[t % 2], 16)
                    if t >= 1:
                        sp.wait_ge(done, t)
                        sp.dma_start(out[half * HT + t - 1], acc[:, t - 1, :]).then_inc(stored, 16)
                sp.wait_ge(done, HT)
                sp.dma_start(out[half * HT + HT - 1], acc[:, HT - 1, :]).then_inc(stored, 16)
                sp.wait_ge(stored, 16 * HT)

            @block.gpsimd
            def _(pool):
                pool.wait_ge(g_loaded, 32)
                for t in range(HT):
                    pool.wait_ge(x_loaded[t % 2], 16 * (t // 2 + 1))
                    pool.tensor_tensor(x[:, t % 2, :], x[:, t % 2, :], beta[:], ALU.add).then_inc(xb, 1)

            @block.scalar
            def _(act):
                act.wait_ge(agg, HT)
                act.wait_ge(eps_set, 1)
                act.activation(rstd[:].unsqueeze(2), mv[:, :, 1:2], ACT.Sqrt, bias=eps[:]).then_inc(rt, 1)
                for t in range(HT):
                    act.wait_ge(nm, 1)
                    act.activation(acc[:, t, :], acc[:, t, :], ACT.Identity, bias=nmr[:, t:t + 1],
                                   scale=rstd[:, t:t + 1]).then_inc(norm, 1)

            @block.vector
            def _(dve):
                dve.memset(eps[:], LN_EPS).then_inc(eps_set, 1)
                for t in range(HT):
                    for h in range(2):
                        dve.bn_stats(out=stats[:, t, h, :], in_=acc[:, t, h * HALF:(h + 1) * HALF]).then_inc(st, 1)
                dve.wait_ge(st, 2 * HT)
                for t in range(HT):
                    dve.bn_aggr(out=mv[:, t, :], in_=stats[:, t, :, :].rearrange("p a b -> p (a b)")).then_inc(agg, 1)
                dve.wait_ge(rt, 1)
                dve.reciprocal(rstd[:], rstd[:]).then_inc(inv, 1)
                dve.wait_ge(inv, 1)
                dve.scalar_tensor_tensor(out=nmr[:].unsqueeze(2), in0=mv[:, :, 0:1], scalar=-1.0,
                                         in1=rstd[:].unsqueeze(2), op0=ALU.mult, op1=ALU.mult).then_inc(nm, 1)
                dve.wait_ge(g_loaded, 32)
                for t in range(HT):
                    dve.wait_ge(norm, t + 1)
                    dve.tensor_tensor(acc[:, t, :], acc[:, t, :], gamma[:], ALU.mult).then_inc(scaled, 1)
                    dve.wait_ge(scaled, t + 1)
                    dve.wait_ge(xb, t + 1)
                    dve.tensor_tensor(acc[:, t, :], acc[:, t, :], x[:, t % 2, :], ALU.add).then_inc(done, 1)


def build(nc, A, out, stop_after=None):
    SC = {}
    for name, shape in (("att0", (BATCH, NK)), ("att3", (BATCH, NK)), ("bias0", (BATCH, CH)), ("bias3", (BATCH, CH)),
                        ("ctx2", (BATCH, CH)), ("g", (NLAT, P, KC, P)), ("x1", (NT, P, D)), ("y1", (NT, P, D)),
                        ("x2", (NT, P, D)), ("y2T", (NT, P, D)), ("x3", (NT, P, D))):
        SC[name] = nc.dram_tensor("scratch_" + name, shape, F32).ap()
    SC["g2"] = SC["g"].rearrange("c p k j -> c p (k j)")
    with ExitStack() as ctx:
        s = Scope(nc, ctx)
        K = dict(ident=s.sb("ident", [P, P]), ones=s.sb("ones", [P, P]), ones_r=s.sb("ones_r", [P, P], F32R),
                 desc=s.sb("desc", [P, E2]), ctx1=s.sb("ctx1", [P, NT]))
        for L in "03":
            K[f"att{L}"] = s.sb(f"att{L}", [P, NT, NK])
            K[f"kern{L}"] = s.sb(f"kern{L}", [P, NK, CH])
        with ExitStack() as c1:
            s1 = Scope(nc, c1)
            K["cbT"] = s1.sb("cbT", [P, KC, D], F32R)
            K["scb_row"] = s1.sb("scb_row", [P, D])
            K["keep_row"] = s1.sb("keep_row", [P, D])
            K["cmax"] = s1.sb("cmax", [P, D])
            K["taps"] = [s1.split(f"taps{i}", [P, TAPS, P]) for i in range(2)]
            with ExitStack() as c2:
                s2 = Scope(nc, c2)
                K["taps_raw"] = [s2.sb(f"taps_raw{i}", [P, TAPS, P]) for i in range(2)]
                phase_constants(nc, K, A)
                phase_condition(nc, K, A, SC)
                split_taps(nc, K)
            phase_quantize_weight(nc, K, A)
            phase_latent_weight(nc, K, A, SC)
            phase_l0(nc, K, A, SC)
            phase_outliers(nc, K)
            phase_l1(nc, K, A, SC)
        with ExitStack() as c1:
            s1 = Scope(nc, c1)
            W = s1.split("l2_w", [P, 2 * KC, D])
            phase_l2(nc, K, A, SC, W)
        for half in range(2):
            phase_l3(nc, K, A, SC, half, out)
    return SC


def lay_out(i):
    import numpy as np
    c = np.ascontiguousarray
    a = {}
    a["x"] = c(i["x"]).reshape(NT, P, D)
    a["condT"] = c(np.asarray(i["cond_128"]).T)
    for n in ("fside_S_0", "L1_ffn_weight", "L1_ffn_bias", "L2_ffn_base_b", "L3_ffn_gate_w", "L3_ffn_expert_w",
              "L3_ffn_ln_gamma", "L3_ffn_ln_beta"):
        a[n] = c(i[n])
    for L in "03":
        for n in ("W0", "b0", "W1", "b1", "W2", "b2", "bias_k"):
            a[f"L{L}_cond_{n}"] = c(i[f"L{L}_cond_{n}"])
        a[f"L{L}_cond_kernels"] = c(np.asarray(i[f"L{L}_cond_weight"])[..., 0].transpose(2, 0, 1)).reshape(CH, NK * CH)
    for L in "12":
        a[f"L{L}_cond_c_weight_T"] = c(np.asarray(i[f"L{L}_cond_c_weight"]).T)
        w = np.asarray(i[f"L{L}_cond_weight"]).reshape(GROUPS, GI, GI, TAPS)
        a[f"L{L}_cond_taps"] = c(w.transpose(0, 2, 3, 1)).reshape(GROUPS, GI, TAPS * GI)
    wa = np.concatenate([np.asarray(i["L0_ffn_A"]).reshape(E0 * R0, D), np.asarray(i["L0_ffn_route_w"])])
    a["l0_wa"] = c(wa.T).reshape(KC, P, P + E0)
    a["l0_wb"] = c(np.asarray(i["L0_ffn_Bw"]).transpose(0, 2, 1)).reshape(P, D)
    war = np.concatenate([np.asarray(i["L2_ffn_A"]), np.asarray(i["L2_ffn_router_w"])])
    a["l2_war"] = c(war.T).reshape(KC, P, R2 + E2)
    a["l2_base"] = c(np.asarray(i["L2_ffn_base_w"]).T).reshape(KC, P, D)
    a["l2_B"] = c(np.asarray(i["L2_ffn_B"]).transpose(0, 2, 1)).reshape(KC, P, D)
    a["up"] = c(np.asarray(i["L3_ffn_up_w"]).reshape(KC, P, NINT, P).transpose(2, 1, 0, 3)).reshape(NINT, P, D)
    a["down"] = c(i["L3_ffn_down_w"]).reshape(NINT, P, D)
    a["fc1T"] = c(np.asarray(i["L3_ffn_fc1_w"]).T)
    a["fc2"] = c(i["L3_ffn_fc2_w"]).reshape(NLAT, P, D)
    return a


def kernel(**inputs):
    import numpy as np
    import concourse.bacc as bacc
    from concourse.bass_utils import run_bass_kernel_spmd as run

    nc = bacc.Bacc("TRN2", target_bir_lowering=False, num_devices=1)
    arrays, aps = {}, {}
    for name, a in lay_out(inputs).items():
        arrays["in_" + name] = a
        aps[name] = nc.dram_tensor("in_" + name, a.shape, F32, kind="ExternalInput").ap()
    out = nc.dram_tensor("out", (NT, P, D), F32, kind="ExternalOutput").ap()
    build(nc, aps, out)
    result = run(nc, [arrays], core_ids=[0]).results[0]["out"]
    return np.asarray(result).reshape(BATCH, CH, D)
```

```python
from contextlib import ExitStack

import concourse.bass as bass
from concourse import mybir

F32 = mybir.dt.float32
ALU = mybir.AluOpType
ACT = mybir.ActivationFunctionType
AX = mybir.AxisListType

P = 128
BATCH, CH, D = 32, 64, 1024
NT = BATCH * CH // P
KC = D // P
HALF = D // 2
QC = HALF // P
COND = 128
NK = 8
TAPS, PAD, GROUPS = 9, 4, 4
GI = CH // GROUPS
SHIFTS = 5
HP = PAD // 2
E0, R0 = 8, 16
E2, R2 = 16, 64
NINT, NLAT = 16, 4
NPAIR, HPAIR = (NINT + NLAT) // 2, NINT // 2
EG = 8
ROUND = 1.5 * 2.0 ** 23
THRESHOLD = 6.0
LN_EPS = 1e-5
BIG = 3.0e38



def stepped(eng, body, depth):
    def peeled(s):
        uses = [max(s - k, 0) // 2 + 1 for k in range(depth + 1)]
        body(s, s % 2, uses, [0 <= s - k < NT for k in range(depth + 1)])

    pairs = (NT - depth) // 2
    for s in range(depth):
        peeled(s)
    with eng.Fori(0, pairs) as j:
        for r in range(2):
            s0 = depth + r
            body(2 * j + s0, s0 % 2, [j + (s0 - k) // 2 + 1 for k in range(depth + 1)], [True] * (depth + 1))
    for s in range(depth + 2 * pairs, NT + depth):
        peeled(s)


def later(s, n):
    return not isinstance(s, int) or s >= n


class Scope:

    def __init__(self, nc, ctx):
        self.nc, self.ctx, self.owned = nc, ctx, []

    def sb(self, name, shape, dt=F32):
        return self.ctx.enter_context(self.nc.sbuf_tensor(name, shape, dt))

    def banks(self, name, n):
        return [self.ctx.enter_context(self.nc.psum_tensor(f"{name}{i}", [P, HALF], F32)) for i in range(n)]

    def semaphore(self, name):
        self.owned.append(self.ctx.enter_context(self.nc.semaphore(name)))
        return self.owned[-1]

    def sems(self, names):
        return [self.semaphore(n) for n in names.split()]

    def slot_sems(self, name, slots=2):
        return [self.semaphore(f"{name}{i}") for i in range(slots)]

    def block(self):
        self.ctx.callback(self.clear)
        return self.ctx.enter_context(self.nc.Block())

    def clear(self):
        numbers = sorted(sem.num for sem in self.owned)
        with self.nc.Block() as block:
            @block.gpsimd
            def _(pool):
                first = 0
                for n in range(1, len(numbers) + 1):
                    if n == len(numbers) or numbers[n] != numbers[n - 1] + 1:
                        pool.sem_clear(range(numbers[first], numbers[n - 1] + 1))
                        first = n


def tile_of(ap, t):
    return ap[bass.ds(t, 1), :, :].rearrange("a p d -> (a p) d")


def parity_store(eng, dram, t, src, sem):
    view = dram.rearrange("t (b o) (q k) -> t q o b k", b=2, q=2)
    for q in range(2):
        dst = view[bass.ds(t, 1), q, :, :, :].rearrange("a o b k -> (a o) b k")
        eng.dma_start(dst, src[q * CH:(q + 1) * CH, :, :]).then_inc(sem, 16)


def parity_load(eng, dram, t, dst, sem):
    view = dram.rearrange("t (b o) (q k) -> t q o b k", b=2, q=2)
    for q in range(2):
        src = view[bass.ds(t, 1), q, :, :, :].rearrange("a o b k -> (a o) b k")
        eng.dma_start(dst[q * CH:(q + 1) * CH, :, :], src).then_inc(sem, 16)


def exact_quotient(dve, order, at, out, den, tmp):
    q, dh, dl, qh, ql, r, rec = [tmp[:, i:i + 1] for i in range(7)]
    steps = [
        lambda: dve.reciprocal(rec, den),
        lambda: dve.tensor_scalar(q, rec, 127.0, None, ALU.mult),
        lambda: dve.tensor_scalar(qh, q, 4097.0, None, ALU.mult),
        lambda: dve.tensor_tensor(ql, qh, q, ALU.subtract),
        lambda: dve.tensor_tensor(qh, qh, ql, ALU.subtract),
        lambda: dve.tensor_tensor(ql, q, qh, ALU.subtract),
        lambda: dve.tensor_scalar(dh, den, 4097.0, None, ALU.mult),
        lambda: dve.tensor_tensor(dl, dh, den, ALU.subtract),
        lambda: dve.tensor_tensor(dh, dh, dl, ALU.subtract),
        lambda: dve.tensor_tensor(dl, den, dh, ALU.subtract),
        lambda: dve.tensor_scalar(r, qh, dh, 127.0, ALU.mult, ALU.subtract),
        lambda: dve.scalar_tensor_tensor(out=r, in0=dh, scalar=ql, in1=r, op0=ALU.mult, op1=ALU.add),
        lambda: dve.scalar_tensor_tensor(out=r, in0=qh, scalar=dl, in1=r, op0=ALU.mult, op1=ALU.add),
        lambda: dve.scalar_tensor_tensor(out=r, in0=ql, scalar=dl, in1=r, op0=ALU.mult, op1=ALU.add),
        lambda: dve.tensor_tensor(r, r, rec, ALU.mult),
        lambda: dve.tensor_tensor(out, q, r, ALU.subtract),
    ]
    assert len(steps) == QUOT
    for n, step in enumerate(steps):
        step().then_inc(order, 1)
        dve.wait_ge(order, at + n + 1)
    return at + QUOT


QUOT = 16


def first_of_largest(dve, order, at, lg, desc, m, key, kmax, mask):
    dve.tensor_reduce(m, lg, AX.X, ALU.max).then_inc(order, 1)
    dve.wait_ge(order, at + 1)
    dve.scalar_tensor_tensor(out=key, in0=lg, scalar=m, in1=desc, op0=ALU.is_ge, op1=ALU.mult).then_inc(order, 1)
    dve.wait_ge(order, at + 2)
    dve.tensor_reduce(kmax, key, AX.X, ALU.max).then_inc(order, 1)
    dve.wait_ge(order, at + 3)
    dve.tensor_scalar(mask, key, kmax, None, ALU.is_equal).then_inc(order, 1)
    dve.wait_ge(order, at + 4)
    return at + 4


class Mixer:

    def __init__(self, s, tag, att, kern):
        self.att, self.kern = att, kern
        self.prod = s.sb(f"{tag}_prod", [P, CH, NK])
        self.acc = s.sb(f"{tag}_acc", [P, CH])
        self.mats = s.sb(f"{tag}_mats", [P, 2, P])
        self.weighted, self.summed, self.placed, self.zeroed = s.sems(
            f"{tag}_weighted {tag}_summed {tag}_placed {tag}_zeroed")

    def weigh(self, pool, t):
        pool.wait_ge(self.summed, t + 1)
        pool.tensor_tensor(self.prod[:], self.kern[:],
                           self.att[:, bass.ds(t, 1), :].to_broadcast([P, CH, NK]), ALU.mult).then_inc(self.weighted, 1)

    def sum(self, dve, t):
        dve.wait_ge(self.weighted, t + 1)
        dve.wait_ge(self.placed, 2 * t + 2)
        dve.tensor_reduce(self.acc[:].unsqueeze(2), self.prod[:], AX.X, ALU.add).then_inc(self.summed, 1)

    def place(self, act, t, slot):
        act.wait_ge(self.summed, t + 2)
        for b in range(2):
            rows = slice(b * CH, (b + 1) * CH)
            act.copy(self.mats[rows, slot, b * CH:(b + 1) * CH], self.acc[rows, :]).then_inc(self.placed, 1)

    def start(self, dve):
        dve.memset(self.mats[:], 0.0).then_inc(self.zeroed, 1)
        dve.sem_inc(self.summed, 1)
        dve.sem_inc(self.placed, 2)

    def multiply(self, pe, t, slot, x, out):
        pe.wait_ge(self.placed, 2 * t + 4)
        for h in range(2):
            for c in range(4):
                last = pe.matmul(out[h][:, c * P:(c + 1) * P], x[:, (4 * h + c) * P:(4 * h + c + 1) * P],
                                 self.mats[:, slot, :], start=True, stop=True)
            yield h, last


def phase_setup(nc, K, A, SC):
    with ExitStack() as ctx:
        s = Scope(nc, ctx)
        cT = s.sb("cT", [COND, BATCH])
        W = {}
        for L in "03":
            W[L] = dict(w0=s.sb(f"w0_{L}", [COND, P]), w1=s.sb(f"w1_{L}", [P, P]), w2=s.sb(f"w2_{L}", [P, NK]),
                        b0=s.sb(f"b0_{L}", [P, 1]), b1=s.sb(f"b1_{L}", [P, 1]), b2=s.sb(f"b2_{L}", [BATCH, NK]),
                        bk=s.sb(f"bk_{L}", [NK, CH]), h0=s.sb(f"h0_{L}", [P, BATCH]), h1=s.sb(f"h1_{L}", [P, BATCH]),
                        lg=s.sb(f"lg_{L}", [BATCH, NK]), m=s.sb(f"m_{L}", [BATCH, 1]), nm=s.sb(f"nm_{L}", [BATCH, 1]),
                        ex=s.sb(f"ex_{L}", [BATCH, NK]), z=s.sb(f"z_{L}", [BATCH, 1]), rz=s.sb(f"rz_{L}", [BATCH, 1]),
                        att=s.sb(f"att_{L}", [BATCH, NK]), attT=s.sb(f"attT_{L}", [NK, BATCH]),
                        bias=s.sb(f"bias_{L}", [BATCH, CH]))
        cw1 = s.sb("cw1", [COND, 2, CH])
        cw2 = s.sb("cw2", [COND, CH])
        fside_col = s.sb("fside_col", [P, 1])
        fside_row = s.sb("fside_row", [BATCH, CH])
        ctx2 = s.sb("ctx2_out", [BATCH, CH])
        raw = s.sb("qw_raw", [P, 2, D])
        cb = s.sb("qw_cb", [P, D])
        col = s.sb("qw_col", [P, 4])
        tmp = s.sb("qw_tmp", [P, 8])
        diag = s.sb("qw_diag", [P, P])
        fc1 = s.sb("fc1_raw", [P, NLAT, D])
        exp = s.sb("exp_raw", [P, NLAT, NLAT * P])
        gout = s.sb("g_out", [P, 2, NLAT * P])
        (pm,) = s.banks("pm", 1)
        (px,) = s.banks("px", 1)
        tp = s.banks("qw_tp", 2)
        (bc,) = s.banks("qw_bc", 1)
        pg = s.banks("pg", 2)
        (ident_zeroed, ident_made, desc_made, taps_zeroed, cond_loaded, mlp, gelus, mlp_step, ctx_mm, ctx_out,
         order, rounded, turned, taken, diag_made, spread, spread_out, fc_loaded, g_mm, g_out, bias_stored, att_turned,
         kept, exps) = s.sems(
            "ident_zeroed ident_made desc_made taps_zeroed cond_loaded mlp_mm gelus mlp_step ctx_mm ctx_out "
            "qw_step cb_rounded cb_turned cb_taken scb_diag scb_spread scb_row_out fc_loaded g_mm g_out_ready bias_stored "
            "att_turned setup_kept exps")
        att_stored = s.slot_sems("att_stored")
        qw_loaded, g_stored = s.slot_sems("qw_loaded"), s.slot_sems("g_stored")
        per = QUOT + 4
        block = s.block()

        loads = [(cT[:], A["condT"])]
        for L in "03":
            w = W[L]
            loads += [(w["w0"][:], A[f"L{L}_cond_W0"]), (w["b0"][:], A[f"L{L}_cond_b0"].rearrange("(p a) -> p a", a=1)),
                      (w["w1"][:], A[f"L{L}_cond_W1"]), (w["b1"][:], A[f"L{L}_cond_b1"].rearrange("(p a) -> p a", a=1)),
                      (w["w2"][:], A[f"L{L}_cond_W2"]), (w["b2"][:], A[f"L{L}_cond_b2"].partition_broadcast(BATCH)),
                      (w["bk"][:], A[f"L{L}_cond_bias_k"])]
        fcol = A["fside_S_0"].rearrange("(p a) -> p a", a=1)
        loads += [(cw1[:, 0, :], A["L1_cond_c_weight_T"]), (cw1[:, 1, :], A["L1_cond_c_weight_T"]),
                  (cw2[:], A["L2_cond_c_weight_T"]), (fside_row[:], A["fside_S_0"].partition_broadcast(BATCH)),
                  (fside_col[0:CH, :], fcol), (fside_col[CH:P, :], fcol)]
        all_loaded = 16 * len(loads)

        tap_loads = []
        for dst, name in zip(K["taps"], ("L1_cond_taps", "L2_cond_taps")):
            taps = A[name].rearrange("g i (k o) -> g i k o", k=TAPS)
            for p in range(2):
                for q in range(2):
                    js = [j for j in range(SHIFTS) if 0 <= 2 * j + p - q < TAPS]
                    k0 = 2 * js[0] + p - q
                    for g in range(GROUPS):
                        tap_loads.append((dst[p * CH + g * GI:p * CH + (g + 1) * GI, js[0]:js[-1] + 1,
                                              q * CH + g * GI:q * CH + (g + 1) * GI],
                                          taps[g][:, k0:k0 + 2 * len(js) - 1:2, :]))

        @block.sync
        def _(sp):
            for dst, src in loads:
                sp.dma_start(dst, src).then_inc(cond_loaded, 16)
            sp.dma_start(fc1[:], A["fc1T"].rearrange("(l p) h -> p l h", p=P)).then_inc(fc_loaded, 16)
            sp.dma_start(exp[:], A["L3_ffn_expert_w"].rearrange("(l p) m -> p l m", p=P)).then_inc(fc_loaded, 16)
            for n, L in enumerate("03"):
                sp.wait_ge(mlp_step, 6 * n + 5)
                sp.dma_start(SC[f"att{L}"], W[L]["att"][:]).then_inc(att_stored[n], 16)
                sp.wait_ge(att_stored[n], 16)
                src = SC[f"att{L}"].rearrange("(t b) k -> b t k", b=2)
                for b in range(2):
                    sp.dma_start(K[f"att{L}"][b * CH:(b + 1) * CH, :, :], src[b].partition_broadcast(CH)).then_inc(kept, 16)
                    sp.dma_start(K[f"kern{L}"][b * CH:(b + 1) * CH, :, :],
                                 A[f"L{L}_cond_kernels"].rearrange("i (o k) -> i o k", k=NK)).then_inc(kept, 16)
                sp.wait_ge(mlp_step, 6 * n + 6)
                sp.dma_start(SC[f"bias{L}"], W[L]["bias"][:]).then_inc(bias_stored, 16)
                sp.wait_ge(bias_stored, 16 * (2 * n + 1))
                sp.dma_start(K[f"bias{L}"][:], SC[f"bias{L}"].rearrange("b o -> (b o)").partition_broadcast(P)).then_inc(kept, 16)
                if n == 0:
                    sp.wait_ge(ctx_out, 3)
                    sp.dma_start(SC["ctx2"], ctx2[:]).then_inc(bias_stored, 16)
                    sp.wait_ge(bias_stored, 32)
                    sp.dma_start(K["ctx2"][:], SC["ctx2"].rearrange("b o -> (b o)").partition_broadcast(P)).then_inc(kept, 16)
            sp.wait_ge(kept, 16 * 11)

        @block.gpsimd
        def _(pool):
            for c in range(2):
                pool.dma_start(raw[:, c, :], A["L1_ffn_weight"][c * P:(c + 1) * P, :]).then_inc(qw_loaded[c], 16)
            pool.memset(K["ident"][:], 0.0).then_inc(ident_zeroed, 1)
            pool.memset(K["ones"][:], 1.0).then_inc(ident_made, 1)
            pool.wait_ge(ident_zeroed, 1)
            pool.affine_select(out=K["ident"][:], in_=K["ident"][:], compare_op=ALU.not_equal, fill=1.0,
                               base=0, pattern=[[-1, P]], channel_multiplier=1).then_inc(ident_made, 1)
            for e in range(E2):
                pool.memset(K["desc"][:, e:e + 1], float(E2 - e)).then_inc(desc_made, 1)
            pool.wait_ge(taps_zeroed, 2)
            for dst, src in tap_loads:
                pool.dma_start(dst, src).then_inc(K["taps_loaded"], 16)
            for k in range(KC):
                c = k + 2
                if c < KC:
                    pool.wait_ge(rounded, c - 1)
                    pool.dma_start(raw[:, c % 2, :], A["L1_ffn_weight"][c * P:(c + 1) * P, :]).then_inc(qw_loaded[c % 2], 16)
                pool.wait_ge(g_out, k + 1)
                pool.dma_start(SC["g"][:, :, k, :].rearrange("c p j -> p c j"),
                               gout[:, k % 2, :].rearrange("p (c j) -> p c j", c=NLAT)).then_inc(g_stored[k % 2], 16)
            for slot in g_stored:
                pool.wait_ge(slot, 16 * KC // 2)

        @block.tensor
        def _(pe):
            def mlp_layer(n, L):
                w = W[L]
                if n:
                    pe.wait_ge(mlp_step, 6)
                pe.matmul(pm[:, 0:BATCH], w["w0"][:], cT[:], start=True, stop=True).then_inc(mlp, 1)
                yield
                pe.wait_ge(gelus, 2 * n + 1)
                pe.matmul(pm[:, 0:BATCH], w["w1"][:], w["h0"][:], start=True, stop=True).then_inc(mlp, 1)
                yield
                pe.wait_ge(gelus, 2 * n + 2)
                pe.matmul(pm[0:BATCH, 0:NK], w["h1"][:], w["w2"][:], start=True, stop=True).then_inc(mlp, 1)
                yield
                pe.wait_ge(mlp_step, 6 * n + 5)
                pe.transpose(pm[0:NK, 0:BATCH], w["att"][:], K["ident"][0:BATCH, 0:BATCH]).then_inc(mlp, 1)
                yield
                pe.wait_ge(att_turned, n + 1)
                pe.matmul(pm[0:BATCH, 0:CH], w["attT"][:], w["bk"][:], start=True, stop=True).then_inc(mlp, 1)
                yield

            def latent(k):
                if k == 0:
                    pe.wait_ge(fc_loaded, 32)
                if k >= 2:
                    pe.wait_ge(g_out, k - 1)
                for l in range(NLAT):
                    last = pe.matmul(pg[k % 2][:], fc1[:, l, k * P:(k + 1) * P], exp[:, l, :], start=l == 0, stop=l == NLAT - 1)
                last.then_inc(g_mm, 1)

            def weight(c):
                pe.wait_ge(rounded, c + 1)
                for h in range(2):
                    if c:
                        pe.wait_ge(taken, 2 * (c - 1) + h + 1)
                    for j in range(4):
                        k = 4 * h + j
                        last = pe.transpose(tp[h][:, j * P:(j + 1) * P], cb[:, k * P:(k + 1) * P], K["ident"][:])
                    last.then_inc(turned, 1)
                pe.wait_ge(diag_made, c + 1)
                if c:
                    pe.wait_ge(spread_out, c)
                pe.matmul(bc[:, 0:P], K["ones"][:], diag[:], start=True, stop=True).then_inc(spread, 1)

            pe.wait_ge(cond_loaded, all_loaded)
            pe.wait_ge(ident_made, 2)
            pe.matmul(px[:, 0:BATCH], cw1[:].rearrange("d b o -> d (b o)"), cT[:], start=True, stop=True).then_inc(ctx_mm, 1)
            pe.matmul(px[0:BATCH, 2 * CH:3 * CH], cT[:], cw2[:], start=True, stop=True).then_inc(ctx_mm, 1)
            for n, L in enumerate("03"):
                for _ in mlp_layer(n, L):
                    pass
            for k in range(KC):
                weight(k)
                latent(k)

        @block.scalar
        def _(act):
            for dst, src, sem in K["kept_loads"]:
                act.dma_start(dst, src).then_inc(sem, 16)
            act.wait_ge(cond_loaded, all_loaded)
            for n, L in enumerate("03"):
                w = W[L]
                act.wait_ge(mlp, 5 * n + 1)
                act.activation(w["h0"][:], pm[:, 0:BATCH], ACT.Gelu, bias=w["b0"][:]).then_inc(gelus, 1)
                act.wait_ge(mlp, 5 * n + 2)
                act.activation(w["h1"][:], pm[:, 0:BATCH], ACT.Gelu, bias=w["b1"][:]).then_inc(gelus, 1)
                act.wait_ge(mlp_step, 6 * n + 3)
                act.activation(w["ex"][:], w["lg"][:], ACT.Exp, bias=w["nm"][:], accum_out=w["z"][:]).then_inc(exps, 1)
                act.wait_ge(mlp, 5 * n + 4)
                act.copy(w["attT"][:], pm[0:NK, 0:BATCH]).then_inc(att_turned, 1)
            for c in range(KC):
                for h in range(2):
                    act.wait_ge(turned, 2 * c + h + 1)
                    act.copy(K["cbT"][:, 4 * h:4 * h + 4, c * P:(c + 1) * P],
                             tp[h][:].rearrange("p (k o) -> p k o", k=4)).then_inc(taken, 1)
                act.wait_ge(g_mm, c + 1)
                if c >= 2:
                    act.wait_ge(g_stored[c % 2], 16 * (c // 2))
                act.copy(gout[:, c % 2, :], pg[c % 2][:]).then_inc(g_out, 1)

        @block.vector
        def _(dve):
            for taps in K["taps"]:
                dve.memset(taps[:], 0.0).then_inc(taps_zeroed, 1)
            dve.wait_ge(ctx_mm, 2)
            dve.wait_ge(cond_loaded, all_loaded)
            pcv = px[:, 0:BATCH].rearrange("p (t b) -> p b t", b=2)
            for b in range(2):
                dve.tensor_scalar(K["ctx1"][:, b, :], pcv[:, b, :], fside_col[:], None, ALU.add).then_inc(ctx_out, 1)
            dve.tensor_tensor(ctx2[:], px[0:BATCH, 2 * CH:3 * CH], fside_row[:], ALU.add).then_inc(ctx_out, 1)
            for n, L in enumerate("03"):
                w, base = W[L], 6 * n
                dve.wait_ge(mlp, 5 * n + 3)
                dve.tensor_tensor(w["lg"][:], pm[0:BATCH, 0:NK], w["b2"][:], ALU.add).then_inc(mlp_step, 1)
                dve.wait_ge(mlp_step, base + 1)
                dve.tensor_reduce(w["m"][:], w["lg"][:], AX.X, ALU.max).then_inc(mlp_step, 1)
                dve.wait_ge(mlp_step, base + 2)
                dve.tensor_scalar(w["nm"][:], w["m"][:], -1.0, None, ALU.mult).then_inc(mlp_step, 1)
                dve.wait_ge(exps, n + 1)
                dve.reciprocal(w["rz"][:], w["z"][:]).then_inc(mlp_step, 1)
                dve.wait_ge(mlp_step, base + 4)
                dve.tensor_scalar(w["att"][:], w["ex"][:], w["rz"][:], None, ALU.mult).then_inc(mlp_step, 1)
                dve.wait_ge(mlp, 5 * n + 5)
                dve.tensor_copy(w["bias"][:], pm[0:BATCH, 0:CH]).then_inc(mlp_step, 1)
            dve.wait_ge(ident_made, 2)
            for c in range(KC):
                at, w = per * c, raw[:, c % 2, :]
                dve.wait_ge(qw_loaded[c % 2], 16 * (c // 2 + 1))
                dve.tensor_reduce(col[:, 0:1], w, AX.X, ALU.max, apply_absolute_value=True).then_inc(order, 1)
                dve.wait_ge(order, at + 1)
                dve.tensor_scalar(col[:, 1:2], col[:, 0:1], 1e-8, None, ALU.max).then_inc(order, 1)
                dve.wait_ge(order, at + 2)
                at = exact_quotient(dve, order, at + 2, col[:, 2:3], col[:, 1:2], tmp)
                dve.tensor_scalar(col[:, 3:4], col[:, 0:1], 1.0 / 127.0, None, ALU.mult).then_inc(order, 1)
                dve.tensor_scalar(w, w, col[:, 2:3], ROUND, ALU.mult, ALU.add).then_inc(order, 1)
                dve.wait_ge(order, at + 2)
                if c:
                    dve.wait_ge(turned, 2 * c)
                    dve.wait_ge(spread, c)
                dve.tensor_scalar(cb[:], w, ROUND, None, ALU.subtract).then_inc(rounded, 1)
                dve.tensor_scalar(diag[:], K["ident"][:], col[:, 3:4], None, ALU.mult).then_inc(diag_made, 1)
                dve.wait_ge(spread, c + 1)
                dve.tensor_copy(K["scb_row"][:, c * P:(c + 1) * P], bc[:, 0:P]).then_inc(spread_out, 1)
            dve.wait_ge(desc_made, E2)


def phase_l0(nc, K, A, SC):
    with ExitStack() as ctx:
        s_ = Scope(nc, ctx)
        mix = Mixer(s_, "mix0", K["att0"], K["kern0"])
        wa, wb = K["l0_wa"], K["l0_wb"]
        x = s_.sb("x_in", [P, 2, D])
        yT = s_.sb("y0T", [P, D])
        wh = s_.sb("wh", [P, P])
        whT = s_.sb("whT", [P, P])
        x1 = [s_.sb(f"x1_{i}", [P, 2, HALF + PAD]) for i in range(2)]
        y1 = s_.sb("y1", [P, 2, 2, HALF])
        mag = s_.sb("y1_mag", [P, 2, HALF])
        xmov = s_.sb("x_moved", [P, HALF])
        small = s_.sb("l0_small", [P, 32])
        m, kmax = small[:, 0:1], small[:, 1:2]
        lg, key, mask = small[:, 8:16], small[:, 16:24], small[:, 24:32]
        py = s_.banks("py", 2)
        (ph,) = s_.banks("ph", 1)
        (pt,) = s_.banks("pt", 1)
        po = s_.banks("po", 2)
        pv = s_.banks("pv", 2)
        ctx_col = s_.sb("ctx_col", [P, 2, 2])
        x_loaded, y1_stored, x1_stored = [s_.slot_sems(n) for n in ("x_loaded", "y1_stored", "x1_stored")]
        conv_done, y1_made, mag_made, seen = [s_.slot_sems(n) for n in ("conv_done_b", "y1_made_b", "mag_made_b", "mag_seen_b")]
        (x_free, y_mm, y_made, h_mm, route, wh_made, wh_turned, whT_made, o_mm, x1_b0, x1_b1_moved, x1_b1, edge, cmax_set,
         ctx_placed) = s_.sems(
            "x_read y0_mm y0_made h_mm route_step wh_made wh_turned whT_made o_mm x1_b0_made x1_b1_moved x1_b1_made "
            "x1_edges cmax_zeroed ctx_placed")
        block = s_.block()
        cmax = K["cmax"]
        inner = slice(HP, HP + HALF)

        @block.sync
        def _(sp):
            def body(s, u, uses, has):
                if has[0]:
                    sp.wait_ge(x_free, s + 1)
                    sp.dma_start(x[:, u, :], tile_of(A["x"], s)).then_inc(x_loaded[u], 16)
                if has[1]:
                    sp.wait_ge(x1_b0, 2 * s)
                    sp.wait_ge(x1_b1, s)
                    parity_store(sp, SC["x1"], s - 1, x1[1 - u][:, :, inner], x1_stored[1 - u])
                if has[2]:
                    for b in range(2):
                        sp.wait_ge(y1_made[b], s - 1)
                    parity_store(sp, SC["y1"], s - 2, y1[:, u, :, :], y1_stored[u])
            stepped(sp, body, 2)
            for slot in x1_stored + y1_stored:
                sp.wait_ge(slot, 32 * (NT // 2) + 32)

        @block.gpsimd
        def _(pool):
            def body(s, u, uses, has):
                if has[0]:
                    mix.weigh(pool, s)
                if has[1]:
                    if later(s, 3):
                        pool.wait_ge(mag_made[1], s - 2)
                    pool.tensor_copy(ctx_col[:, 1 - u, :].unsqueeze(2),
                                     K["ctx1"][:, :, bass.ds(s - 1, 1)]).then_inc(ctx_placed, 1)
                    pool.wait_ge(x1_b1_moved, 4 * s)
                    pool.tensor_tensor(x1[1 - u][:, 1, inner], x1[1 - u][:, 1, inner], xmov[:], ALU.add).then_inc(x1_b1, 1)
            stepped(pool, body, 2)

        @block.scalar
        def _(act):
            act.wait_ge(mix.zeroed, 1)
            act.wait_ge(edge, 4)

            def conv_out(b, slot, tile, use):
                act.wait_ge(conv_done[b], tile + 1)
                if b == 0:
                    act.wait_ge(y1_stored[slot], 32 * use)
                act.wait_ge(ctx_placed, tile + 1)
                bias = ctx_col[:, slot, b:b + 1]
                act.activation(y1[:, slot, b, :], pv[b][:], ACT.Identity, bias=bias).then_inc(y1_made[b], 1)
                act.wait_ge(seen[b], tile + 1)
                act.activation(mag[:, b, :], pv[b][:], ACT.Abs, bias=bias).then_inc(mag_made[b], 1)

            def body(s, u, uses, has):
                if has[0]:
                    if later(s, 2):
                        act.wait_ge(y_mm, 2 * (s - 1))
                    mix.place(act, s, u)
                if has[1]:
                    act.wait_ge(o_mm, 2 * s)
                    act.wait_ge(x1_stored[1 - u], 32 * uses[1])
                    if later(s, 3):
                        act.wait_ge(conv_done[1], s - 2)
                    if later(s, 2):
                        act.wait_ge(x1_b1, s - 1)
                    for q in range(2):
                        act.copy(x1[1 - u][q * CH:(q + 1) * CH, 1, inner], po[q][CH:P, :]).then_inc(x1_b1_moved, 1)
                        act.copy(xmov[q * CH:(q + 1) * CH, :], x[CH:P, 1 - u, q * HALF:(q + 1) * HALF]).then_inc(x1_b1_moved, 1)
                if has[2]:
                    conv_out(1, u, s - 2, uses[2])
                if has[1]:
                    conv_out(0, 1 - u, s - 1, uses[1])
                if has[0]:
                    act.wait_ge(wh_turned, s + 1)
                    act.copy(whT[:], pt[:, 0:P]).then_inc(whT_made, 1)
            stepped(act, body, 2)

        @block.vector
        def _(dve):
            mix.start(dve)
            for tiles in x1:
                dve.memset(tiles[:, :, 0:HP], 0.0).then_inc(edge, 1)
                dve.memset(tiles[:, :, HP + HALF:], 0.0).then_inc(edge, 1)
            dve.memset(cmax[:], 0.0).then_inc(cmax_set, 1)
            dve.wait_ge(cmax_set, 1)
            dve.wait_ge(edge, 4)
            dve.sem_inc(x_free, 2)
            for sem in seen:
                dve.sem_inc(sem, 1)
            for sem in y1_stored + x1_stored:
                dve.sem_inc(sem, 32)

            def see(b, tile):
                dve.wait_ge(mag_made[b], tile + 1)
                dve.tensor_tensor(cmax[:], mag[:, b, :], cmax[:], ALU.max).then_inc(seen[b], 1)
                dve.wait_ge(seen[b], tile + 2)

            def body(s, u, uses, has):
                if has[0]:
                    mix.sum(dve, s)
                if has[1]:
                    dve.wait_ge(o_mm, 2 * s)
                    dve.wait_ge(x1_stored[1 - u], 32 * uses[1])
                    if later(s, 3):
                        dve.wait_ge(conv_done[0], s - 2)
                    for q in range(2):
                        dve.tensor_tensor(x1[1 - u][q * CH:(q + 1) * CH, 0, inner], po[q][0:CH, :],
                                          x[0:CH, 1 - u, q * HALF:(q + 1) * HALF], ALU.add).then_inc(x1_b0, 1)
                    dve.wait_ge(x1_b0, 2 * s)
                    dve.wait_ge(x1_b1_moved, 4 * s)
                    dve.sem_inc(x_free, 1)
                if has[0]:
                    if later(s, 1):
                        dve.wait_ge(h_mm, s)
                    for h in range(2):
                        dve.wait_ge(y_mm, 2 * s + h + 1)
                        dve.tensor_tensor(yT[:, h * HALF:(h + 1) * HALF].rearrange("p (c k) -> p c k", c=4),
                                          py[h][:].rearrange("p (c k) -> p c k", c=4),
                                          K["bias0"][:, bass.ds(s * P, P)].unsqueeze(1).to_broadcast([P, 4, P]),
                                          ALU.add).then_inc(y_made, 1)
                if has[2]:
                    see(1, s - 2)
                if has[0]:
                    at = 6 * s
                    dve.wait_ge(h_mm, s + 1)
                    dve.tensor_copy(lg, ph[:, P:P + E0]).then_inc(route, 1)
                    dve.wait_ge(route, at + 1)
                    at = first_of_largest(dve, route, at + 1, lg, K["desc"][:, E2 - E0:E2], m, key, kmax, mask)
                    dve.tensor_scalar(key, mask, m, None, ALU.mult).then_inc(route, 1)
                    dve.wait_ge(route, at + 1)
                    if later(s, 1):
                        dve.wait_ge(wh_turned, s)
                    dve.tensor_tensor(wh[:].rearrange("p (e r) -> p e r", e=E0),
                                      ph[:, 0:P].rearrange("p (e r) -> p e r", e=E0),
                                      key.unsqueeze(2).to_broadcast([P, E0, R0]), ALU.mult).then_inc(wh_made, 1)
                if has[1]:
                    see(0, s - 1)
            stepped(dve, body, 2)

        @block.tensor
        def _(pe):
            pe.wait_ge(K["l0_loaded"], 32)
            pe.wait_ge(K["taps_loaded"], 16 * 2 * 4 * GROUPS)

            def conv(b, slot, tile, n0, n1):
                for n in range(n0, n1):
                    last = pe.matmul(pv[b][:], K["taps"][0][:, n, :], x1[slot][:, b, n:n + HALF],
                                     start=n == 0, stop=n == SHIFTS - 1)
                if n1 == SHIFTS:
                    last.then_inc(conv_done[b], 1)

            def body(s, u, uses, has):
                if has[1]:
                    pe.wait_ge(whT_made, s)
                    if later(s, 2):
                        pe.wait_ge(x1_b0, 2 * (s - 1))
                        pe.wait_ge(x1_b1_moved, 4 * (s - 1))
                    for q in range(2):
                        pe.matmul(po[q][:], whT[:], wb[:, q * HALF:(q + 1) * HALF], start=True, stop=True).then_inc(o_mm, 1)
                if has[0]:
                    pe.wait_ge(x_loaded[u], 16 * uses[0])
                    if later(s, 1):
                        pe.wait_ge(y_made, 2 * s)
                    for h, last in mix.multiply(pe, s, u, x[:, u, :], py):
                        last.then_inc(y_mm, 1)
                if has[2]:
                    pe.wait_ge(x1_b1, s - 1)
                    if later(s, 3):
                        pe.wait_ge(mag_made[1], s - 2)
                    conv(1, u, s - 2, 0, SHIFTS)
                if has[0]:
                    pe.wait_ge(y_made, 2 * s + 2)
                    if later(s, 1):
                        pe.wait_ge(wh_made, s)
                    for k in range(KC):
                        last = pe.matmul(ph[:, 0:P + E0], yT[:, k * P:(k + 1) * P], wa[:, k, :], start=k == 0, stop=k == KC - 1)
                    last.then_inc(h_mm, 1)
                if has[1]:
                    pe.wait_ge(x1_b0, 2 * s)
                    if later(s, 2):
                        pe.wait_ge(mag_made[0], s - 1)
                    conv(0, 1 - u, s - 1, 0, 4)
                if has[0]:
                    pe.wait_ge(wh_made, s + 1)
                    if later(s, 1):
                        pe.wait_ge(whT_made, s)
                    pe.transpose(pt[:, 0:P], wh[:], K["ident"][:]).then_inc(wh_turned, 1)
                if has[1]:
                    conv(0, 1 - u, s - 1, 4, SHIFTS)
            stepped(pe, body, 2)


def phase_l1(nc, K, A, SC):
    with ExitStack() as ctx:
        s_ = Scope(nc, ctx)
        y1 = s_.sb("l1_y1", [P, 2, D])
        x1 = s_.sb("l1_x1", [P, 2, 2, HALF])
        bias = s_.sb("l1_bias", [P, HALF])
        keep_row = s_.sb("keep_row", [P, D])
        yi = s_.sb("yi", [P, D])
        z = s_.sb("z", [P, D])
        zT = [s_.sb(f"zT{i}", [P, D]) for i in range(2)]
        x2 = [s_.sb(f"x2_{i}", [P, 2, HALF + PAD]) for i in range(2)]
        y2 = s_.sb("y2", [P, 2, D])
        col = s_.sb("l1_col", [P, 4])
        tmp = s_.sb("l1_tmp", [P, 8])
        top = s_.sb("col_top", [P, QC, 2])
        keep = s_.sb("col_keep", [P, QC, 2])
        diag = s_.sb("keep_diag", [P, 2, P])
        pz = s_.banks("pz", 2)
        pf = s_.banks("pf", 2)
        pv = s_.banks("pw", 2)
        y_loaded, x_loaded, y2_stored, x2_stored = [
            s_.slot_sems(n) for n in ("l1_y_loaded", "l1_x_loaded", "y2_stored", "x2_stored")]
        conv_done, y2_made = [s_.slot_sems(n) for n in ("conv2_done_b", "y2_made_b")]
        (x_free, bias_loaded, q, rest, rounded, z_made, z_turned, zT_made, f_mm, xb, x2_scaled, x2_made, edge,
         turned, topped, kept, diag_made, spread, keep_out, y2_half) = s_.sems(
            "l1_x_read l1_bias_loaded quant_step outlier_part row_rounded z_made z_turned zT_made f_mm xb_made "
            "x2_scaled x2_made x2_edges cmax_turned col_topped col_kept keep_diag_made keep_spread keep_row_out y2_half_made")
        QS = 4 + QUOT
        block = s_.block()
        inner = slice(HP, HP + HALF)

        @block.sync
        def _(sp):
            for q_ in range(2):
                sp.dma_start(bias[q_ * CH:(q_ + 1) * CH, :],
                             A["L1_ffn_bias"][q_ * HALF:(q_ + 1) * HALF].partition_broadcast(CH)).then_inc(bias_loaded, 16)

            def body(s, u, uses, has):
                if has[0]:
                    sp.wait_ge(z_made, s + 1)
                    sp.dma_start(y1[:, u, :], tile_of(SC["y1"], s)).then_inc(y_loaded[u], 16)
                    sp.wait_ge(x_free, s + 1)
                    parity_load(sp, SC["x1"], s, x1[:, u, :, :], x_loaded[u])
                if has[1]:
                    sp.wait_ge(x2_made, s)
                    parity_store(sp, SC["x2"], s - 1, x2[1 - u][:, :, inner], x2_stored[1 - u])
                if has[2]:
                    for b in range(2):
                        sp.wait_ge(y2_made[b], s - 1)
                    sp.dma_start(tile_of(SC["y2T"], s - 2), y2[:, u, :]).then_inc(y2_stored[u], 16)
            stepped(sp, body, 2)
            for slot in x2_stored:
                sp.wait_ge(slot, 32 * (NT // 2) + 32)
            for slot in y2_stored:
                sp.wait_ge(slot, 16 * (NT // 2) + 16)

        @block.gpsimd
        def _(pool):
            pool.wait_ge(bias_loaded, 32)

            def body(s, u, uses, has):
                if has[0]:
                    pool.wait_ge(q, QS * s + 1)
                    pool.tensor_tensor(y1[:, u, :], y1[:, u, :], yi[:], ALU.subtract).then_inc(rest, 1)
                    pool.wait_ge(x_loaded[u], 32 * uses[0])
                    pool.tensor_tensor(x1[:, u, :, :], x1[:, u, :, :], bias[:].unsqueeze(1).to_broadcast([P, 2, HALF]),
                                       ALU.add).then_inc(xb, 1)
                if has[1]:
                    pool.wait_ge(x2_scaled, 4 * s)
                    pool.wait_ge(xb, s)
                    pool.tensor_tensor(x2[1 - u][:, :, inner], x2[1 - u][:, :, inner], x1[:, 1 - u, :, :],
                                       ALU.add).then_inc(x2_made, 1)
                    pool.wait_ge(x2_made, s)
                    pool.sem_inc(x_free, 1)
            pool.sem_inc(x_free, 2)
            stepped(pool, body, 2)

        @block.scalar
        def _(act):
            def body(s, u, uses, has):
                if has[0]:
                    for h in range(2):
                        act.wait_ge(z_turned, 2 * s + h + 1)
                        if h == 0 and later(s, 2):
                            act.wait_ge(f_mm, 2 * (s - 1))
                        act.copy(zT[u][:, h * HALF:(h + 1) * HALF], pz[h][:]).then_inc(zT_made, 1)
            stepped(act, body, 2)

        @block.vector
        def _(dve):
            for tiles in x2:
                dve.memset(tiles[:, :, 0:HP], 0.0).then_inc(edge, 1)
                dve.memset(tiles[:, :, HP + HALF:], 0.0).then_inc(edge, 1)
            dve.wait_ge(edge, 4)
            dve.sem_inc(z_made, 2)
            for sem in x2_stored:
                dve.sem_inc(sem, 32)
            for sem in y2_stored:
                dve.sem_inc(sem, 16)
            dve.wait_ge(turned, 1)
            dve.tensor_reduce(top[:].rearrange("p c q -> p (c q)").unsqueeze(2),
                              pz[0][:].rearrange("p (a o) -> p a o", o=CH), AX.X, ALU.max).then_inc(topped, 1)
            dve.wait_ge(topped, 1)
            dve.tensor_scalar(keep[:], top[:], THRESHOLD, None, ALU.is_le).then_inc(kept, 1)
            dve.wait_ge(kept, 1)
            for n in range(KC):
                if n >= 2:
                    dve.wait_ge(spread, n - 1)
                dve.tensor_scalar(diag[:, n % 2, :], K["ident"][:], keep[:, n % QC, n // QC:n // QC + 1], None,
                                  ALU.mult).then_inc(diag_made, 1)
            dve.wait_ge(spread, KC)
            for h in range(2):
                dve.tensor_copy(keep_row[:, h * HALF:(h + 1) * HALF], pf[h][:]).then_inc(keep_out, 1)
            dve.wait_ge(keep_out, 2)

            def conv_out(b, s, u, use):
                dve.wait_ge(conv_done[b], s - 1)
                if b == 0:
                    dve.wait_ge(y2_stored[u], 16 * use)
                out = y2[:, u, :].rearrange("p (q c b o) -> p b c q o", q=2, c=QC, b=2)[:, b]
                row = K["ctx2"][:, bass.ds((s - 2) * P + b * CH, CH)]
                for q_ in range(2):
                    dve.tensor_tensor(out[:, :, q_, :], pv[b][:].rearrange("p (c q o) -> p c q o", c=QC, q=2)[:, :, q_, :],
                                      row.unsqueeze(1).to_broadcast([P, QC, CH]), ALU.add).then_inc(y2_half, 1)
                dve.wait_ge(y2_half, 4 * (s - 2) + 2 * b + 2)
                dve.sem_inc(y2_made[b], 1)

            def scale(h, s, u):
                dve.wait_ge(f_mm, 2 * (s - 1) + h + 1)
                for b in range(2):
                    dve.tensor_tensor(x2[1 - u][h * CH:(h + 1) * CH, b, inner], pf[h][b * CH:(b + 1) * CH, :],
                                      K["scb_row"][b * CH:(b + 1) * CH, h * HALF:(h + 1) * HALF], ALU.mult).then_inc(x2_scaled, 1)

            def body(s, u, uses, has):
                if has[1]:
                    dve.wait_ge(x2_stored[1 - u], 32 * uses[1])
                    if later(s, 3):
                        for b in range(2):
                            dve.wait_ge(conv_done[b], s - 2)
                    scale(0, s, u)
                if has[0]:
                    at, y = QS * s, y1[:, u, :]
                    dve.wait_ge(y_loaded[u], 16 * uses[0])
                    if later(s, 1):
                        dve.wait_ge(rest, s)
                    dve.tensor_tensor(yi[:], y, keep_row[:], ALU.mult).then_inc(q, 1)
                    dve.wait_ge(q, at + 1)
                    dve.tensor_reduce(col[:, 0:1], yi[:], AX.X, ALU.max, apply_absolute_value=True).then_inc(q, 1)
                    dve.wait_ge(q, at + 2)
                    dve.tensor_scalar(col[:, 1:2], col[:, 0:1], 1e-8, None, ALU.max).then_inc(q, 1)
                    dve.wait_ge(q, at + 3)
                    at = exact_quotient(dve, q, at + 3, col[:, 2:3], col[:, 1:2], tmp)
                    dve.tensor_scalar(col[:, 3:4], col[:, 1:2], 1.0 / 127.0, None, ALU.mult).then_inc(q, 1)
                    dve.wait_ge(rest, s + 1)
                    dve.tensor_scalar(yi[:], yi[:], col[:, 2:3], ROUND, ALU.mult, ALU.add).then_inc(rounded, 1)
                    dve.wait_ge(rounded, 2 * s + 1)
                    dve.tensor_scalar(yi[:], yi[:], ROUND, None, ALU.subtract).then_inc(rounded, 1)
                    dve.wait_ge(rounded, 2 * s + 2)
                    dve.wait_ge(q, at + 1)
                    if later(s, 1):
                        dve.wait_ge(z_turned, 2 * s)
                    dve.scalar_tensor_tensor(out=z[:], in0=yi[:], scalar=col[:, 3:4], in1=y, op0=ALU.mult,
                                             op1=ALU.add).then_inc(z_made, 1)
                    dve.wait_ge(z_made, s + 3)
                if has[2]:
                    conv_out(0, s, u, uses[2])
                if has[1]:
                    scale(1, s, u)
                if has[2]:
                    conv_out(1, s, u, uses[2])
            stepped(dve, body, 2)

        @block.tensor
        def _(pe):
            for c in range(QC):
                last = pe.transpose(pz[0][:, c * P:(c + 1) * P], K["cmax"][:, c * P:(c + 1) * P], K["ident"][:])
            last.then_inc(turned, 1)
            for n in range(KC):
                pe.wait_ge(diag_made, n + 1)
                pe.matmul(pf[n // QC][:, (n % QC) * P:(n % QC + 1) * P], K["ones"][:], diag[:, n % 2, :],
                          start=True, stop=True).then_inc(spread, 1)

            def product(h, s, u):
                if later(s, 2):
                    pe.wait_ge(x2_scaled, 4 * (s - 2) + 2 * h + 2)
                else:
                    pe.wait_ge(keep_out, 2)
                for k in range(KC):
                    last = pe.matmul(pf[h][:], zT[1 - u][:, k * P:(k + 1) * P], K["cbT"][:, k, h * HALF:(h + 1) * HALF],
                                     start=k == 0, stop=k == KC - 1)
                last.then_inc(f_mm, 1)

            def conv(b, s, u):
                if later(s, 3):
                    pe.wait_ge(y2_made[b], s - 2)
                for c in range(QC):
                    for n in range(SHIFTS):
                        last = pe.matmul(pv[b][:, c * P:(c + 1) * P], x2[u][:, b, c * P + n:(c + 1) * P + n],
                                         K["taps"][1][:, n, :], start=n == 0, stop=n == SHIFTS - 1)
                last.then_inc(conv_done[b], 1)

            def body(s, u, uses, has):
                if has[1]:
                    pe.wait_ge(zT_made, 2 * s)
                    product(0, s, u)
                if has[0]:
                    pe.wait_ge(z_made, s + 3)
                    for h in range(2):
                        if later(s, 1):
                            pe.wait_ge(zT_made, 2 * s)
                        else:
                            pe.wait_ge(topped, 1)
                        for j in range(4):
                            k = 4 * h + j
                            last = pe.transpose(pz[h][:, j * P:(j + 1) * P], z[:, k * P:(k + 1) * P], K["ident"][:])
                        last.then_inc(z_turned, 1)
                if has[2]:
                    pe.wait_ge(x2_made, s - 1)
                    conv(0, s, u)
                if has[1]:
                    product(1, s, u)
                if has[2]:
                    conv(1, s, u)
            stepped(pe, body, 2)


def phase_l2(nc, K, A, SC):
    with ExitStack() as ctx:
        s_ = Scope(nc, ctx)
        mix = Mixer(s_, "mix3", K["att3"], K["kern3"])
        base, low, war = K["l2_base"], K["l2_B"], K["l2_war"]
        y2 = s_.sb("l2_y2", [P, 2, D])
        x2 = s_.sb("l2_x2", [P, 2, D])
        bias = s_.sb("l2_bias", [P, D])
        beta = s_.sb("l2_beta", [P, D])
        cr = s_.sb("cr", [P, D])
        crT = s_.sb("crT", [P, D])
        x3 = s_.sb("x3", [P, 2, D])
        x3b = s_.sb("x3b", [P, D])
        rT = s_.sb("rT", [R2 + E2, P])
        sm = s_.sb("l2_small", [P, 8, E2])
        res = s_.sb("l2_res", [P, R2])
        m, nm, kmax, z, tot, m2 = [sm[:, 0, i:i + 1] for i in range(6)]
        lg, key, one, two, ex, lg2 = [sm[:, i, :] for i in range(1, 7)]
        pr = s_.banks("pr", 2)
        pc = s_.banks("pc", 2)
        po = s_.banks("po2_", 2)
        py = s_.banks("py3_", 2)
        y_loaded, x_loaded = s_.slot_sems("l2_y_loaded"), s_.slot_sems("l2_x_loaded")
        (bias_loaded, beta_loaded, x_free, r_mm, r_out, r_turned, step, e_done, cr_made, cr_turned, crT_made, o_mm, xb,
         x3_made, x3b_made, x3b_stored, y_mm, y3_made) = s_.sems(
            "l2_bias_loaded beta_loaded l2_x_read r_mm r_out r_turned mix_step exp_done cr_made cr_turned crT_made l2_o_mm "
            "l2_xb_made x3_made x3b_made x3b_stored y3_mm y3_made")
        MS = 18
        block = s_.block()

        @block.sync
        def _(sp):
            sp.dma_start(bias[:], A["L2_ffn_base_b"].partition_broadcast(P)).then_inc(bias_loaded, 16)
            sp.dma_start(beta[:], A["L3_ffn_ln_beta"].partition_broadcast(P)).then_inc(beta_loaded, 16)

            def body(s, u, uses, has):
                if has[0]:
                    sp.wait_ge(o_mm, 2 * s + 2)
                    sp.dma_start(y2[:, u, :], tile_of(SC["y2T"], s)).then_inc(y_loaded[u], 16)
                    sp.wait_ge(x_free, s + 1)
                    sp.dma_start(x2[:, u, :], tile_of(SC["x2"], s)).then_inc(x_loaded[u], 16)
                if has[1]:
                    sp.wait_ge(x3b_made, s)
                    sp.dma_start(tile_of(SC["x3b"], s - 1), x3b[:]).then_inc(x3b_stored, 16)
            stepped(sp, body, 2)
            sp.wait_ge(x3b_stored, 16 * (NT + 1))

        @block.gpsimd
        def _(pool):
            pool.wait_ge(bias_loaded, 16)
            pool.wait_ge(beta_loaded, 16)

            def body(s, u, uses, has):
                if has[0]:
                    mix.weigh(pool, s)
                    pool.wait_ge(x_loaded[u], 16 * uses[0])
                    pool.tensor_tensor(x2[:, u, :], x2[:, u, :], bias[:], ALU.add).then_inc(xb, 1)
                if has[1]:
                    pool.wait_ge(x3_made, 2 * s)
                    pool.wait_ge(x3b_stored, 16 * s)
                    pool.tensor_tensor(x3b[:], x3[:, 1 - u, :], beta[:], ALU.add).then_inc(x3b_made, 1)
            stepped(pool, body, 2)

        @block.scalar
        def _(act):
            act.wait_ge(mix.zeroed, 1)

            def body(s, u, uses, has):
                if has[1]:
                    for h in range(2):
                        act.wait_ge(cr_turned, 2 * (s - 1) + h + 1)
                        if later(s, 2):
                            act.wait_ge(o_mm, 2 * (s - 2) + 6)
                        act.copy(crT[:, h * HALF:(h + 1) * HALF], pc[h][:]).then_inc(crT_made, 1)
                if has[0]:
                    if later(s, 2):
                        act.wait_ge(y_mm, 2 * (s - 1))
                    mix.place(act, s, u)
                    act.wait_ge(r_mm, s + 1)
                    act.copy(rT[:], pr[0][0:R2 + E2, 0:P]).then_inc(r_out, 1)
                if has[0]:
                    act.wait_ge(step, MS * s + 7)
                    act.activation(ex, lg, ACT.Exp, bias=nm, accum_out=z).then_inc(e_done, 1)
            stepped(act, body, 2)

        @block.vector
        def _(dve):
            mix.start(dve)
            dve.sem_inc(x_free, 2)
            dve.sem_inc(x3b_stored, 16)
            dve.sem_inc(o_mm, 4)

            def body(s, u, uses, has):
                if has[0]:
                    mix.sum(dve, s)
                if has[2]:
                    for h in range(2):
                        dve.wait_ge(y_mm, 2 * (s - 2) + h + 1)
                        dve.tensor_tensor(K["y3T"][:, 4 * h:4 * h + 4, bass.ds((s - 2) * P, P)],
                                          py[h][:].rearrange("p (c k) -> p c k", c=4),
                                          K["bias3"][:, bass.ds((s - 2) * P, P)].unsqueeze(1).to_broadcast([P, 4, P]),
                                          ALU.add).then_inc(y3_made, 1)
                if has[0]:
                    at = MS * s
                    dve.wait_ge(r_turned, s + 1)
                    dve.tensor_copy(lg, pr[1][:, R2:R2 + E2]).then_inc(step, 1)
                    if later(s, 1):
                        dve.wait_ge(cr_made, s)
                    dve.tensor_copy(res[:], pr[1][:, 0:R2]).then_inc(step, 1)
                    dve.wait_ge(step, at + 2)
                    at = first_of_largest(dve, step, at + 2, lg, K["desc"][:], m, key, kmax, one)
                    dve.tensor_scalar(nm, m, -1.0, None, ALU.mult).then_inc(step, 1)
                    dve.scalar_tensor_tensor(out=lg2, in0=one, scalar=-BIG, in1=lg, op0=ALU.mult, op1=ALU.add).then_inc(step, 1)
                    dve.wait_ge(step, at + 2)
                    at = first_of_largest(dve, step, at + 2, lg2, K["desc"][:], m2, key, kmax, two)
                    dve.tensor_tensor(one, one, two, ALU.add).then_inc(step, 1)
                    dve.wait_ge(step, at + 1)
                    dve.wait_ge(e_done, s + 1)
                    dve.tensor_tensor(key, ex, one, ALU.mult).then_inc(step, 1)
                    dve.wait_ge(step, at + 2)
                    dve.tensor_reduce(tot, key, AX.X, ALU.add).then_inc(step, 1)
                    dve.wait_ge(step, at + 3)
                    dve.scalar_tensor_tensor(out=tot, in0=z, scalar=1e-6, in1=tot, op0=ALU.mult, op1=ALU.add).then_inc(step, 1)
                    dve.wait_ge(step, at + 4)
                    dve.reciprocal(kmax, tot).then_inc(step, 1)
                    dve.wait_ge(step, at + 5)
                    dve.tensor_scalar(key, key, kmax, 0.5, ALU.mult, ALU.mult).then_inc(step, 1)
                    dve.wait_ge(step, at + 6)
                    if isinstance(s, int):
                        assert at + 6 == MS * (s + 1), at + 6 - MS * s
                if has[1]:
                    for h in range(2):
                        cols = slice(h * HALF, (h + 1) * HALF)
                        dve.wait_ge(o_mm, 2 * (s - 1) + h + 5)
                        if h == 0:
                            dve.wait_ge(xb, s)
                            if later(s, 3):
                                dve.wait_ge(y_mm, 2 * (s - 2))
                                dve.wait_ge(x3b_made, s - 2)
                        dve.tensor_tensor(x3[:, 1 - u, cols], po[h][:], x2[:, 1 - u, cols], ALU.add).then_inc(x3_made, 1)
                    dve.wait_ge(x3_made, 2 * s)
                    dve.sem_inc(x_free, 1)
                if has[0]:
                    if later(s, 1):
                        dve.wait_ge(cr_turned, 2 * s)
                    dve.tensor_tensor(cr[:].rearrange("p (e r) -> p e r", e=E2),
                                      key.unsqueeze(2).to_broadcast([P, E2, R2]),
                                      res[:].unsqueeze(1).to_broadcast([P, E2, R2]), ALU.mult).then_inc(cr_made, 1)
            stepped(dve, body, 2)

        @block.tensor
        def _(pe):
            pe.wait_ge(K["l2_loaded"], 16 * 4)

            def half(h, s, u):
                for k in range(KC):
                    last = pe.matmul(po[h][:], crT[:, k * P:(k + 1) * P], low[:, k, h * HALF:(h + 1) * HALF],
                                     start=False, stop=k == KC - 1)
                last.then_inc(o_mm, 1)

            def body(s, u, uses, has):
                if has[1]:
                    pe.wait_ge(cr_made, s)
                    for h in range(2):
                        if later(s, 2):
                            pe.wait_ge(crT_made, 2 * (s - 1))
                        for j in range(4):
                            k = 4 * h + j
                            last = pe.transpose(pc[h][:, j * P:(j + 1) * P], cr[:, k * P:(k + 1) * P], K["ident"][:])
                        last.then_inc(cr_turned, 1)
                    for h in range(2):
                        if later(s, 2):
                            pe.wait_ge(x3_made, 2 * (s - 2) + h + 1)
                        for k in range(KC):
                            pe.matmul(po[h][:], y2[:, 1 - u, k * P:(k + 1) * P], base[:, k, h * HALF:(h + 1) * HALF],
                                      start=k == 0, stop=False)
                if has[2]:
                    if later(s, 3):
                        pe.wait_ge(y3_made, 2 * (s - 2))
                    pe.wait_ge(x3_made, 2 * (s - 1))
                    for h, last in mix.multiply(pe, s - 2, u, x3[:, u, :], py):
                        last.then_inc(y_mm, 1)
                if has[0]:
                    pe.wait_ge(y_loaded[u], 16 * uses[0])
                    if later(s, 1):
                        pe.wait_ge(r_out, s)
                    for k in range(KC):
                        last = pe.matmul(pr[0][0:R2 + E2, 0:P], war[:, k, :], y2[:, u, k * P:(k + 1) * P],
                                         start=k == 0, stop=k == KC - 1)
                    last.then_inc(r_mm, 1)
                if has[1]:
                    pe.wait_ge(crT_made, 2 * s)
                    half(0, s, u)
                if has[0]:
                    pe.wait_ge(r_out, s + 1)
                    if later(s, 1):
                        pe.wait_ge(step, MS * (s - 1) + 2)
                    pe.transpose(pr[1][:, 0:R2 + E2], rT[:], K["ident"][0:R2 + E2, 0:R2 + E2]).then_inc(r_turned, 1)
                if has[1]:
                    half(1, s, u)
            stepped(pe, body, 2)


def phase_l3(nc, K, A, SC, out):
    with ExitStack() as ctx:
        s_ = Scope(nc, ctx)
        y3T = K["y3T"]
        TOK = NT * P
        acc = s_.sb("acc", [P, NT, D])
        NR = 4
        up = s_.sb("up_ring", [P, NR, D])
        dn = s_.sb("down_ring", [P, NR, D])
        hid = [s_.sb(f"hid{i}", [P, 2, TOK]) for i in range(2)]
        pu = s_.banks("pu", 4)
        pd = [s_.banks(f"pd{v}_", 2) for v in range(2)]
        up_loaded, dn_loaded = s_.slot_sems("up_loaded"), s_.slot_sems("down_loaded")
        up_mm, relu, hid_made, dn_mm, added, acc_set = s_.sems("up_mm relu hid_made down_mm added acc_zeroed")
        gT = hid[1][0:EG, 0, :]
        logits, top = s_.sb("gate_logits", [P, NT * EG]), s_.sb("gate_top", [P, NT, EG])
        gate_sum = s_.sb("gate_sum", [P, NT])
        g_mm, gT_made, g_turned, g_out, topped, g_summed = s_.sems("gate_mm gateT_made gate_turned gate_out gate_topped gate_summed")
        gamma = s_.sb("gamma", [P, D])
        sums = s_.sb("row_sums", [P, NT, 2])
        nmean, ssq, root, inv, shift = [s_.sb(n, [P, NT]) for n in ("neg_mean", "sum_sq", "root", "rstd", "shift")]
        eps = s_.sb("eps", [P, 1])
        gamma_loaded, eps_set, centred, squared, rooted, inverted, shifted, normed, scaled, out_made, out_stored = s_.sems(
            "gamma_loaded eps_set neg_mean_made sum_sq_made root_made rstd_made shift_made normed scaled out_made out_stored")
        x3b_loaded = s_.slot_sems("x3b_loaded", NR)
        block = s_.block()
        NB = TOK // HALF

        def steps(eng, body):
            body(0, 0, 1, True, False, False, False)
            with eng.Fori(0, HPAIR // 2 - 1) as i:
                body(2 * i + 1, 1, i + 1, True, True, False, False)
                body(2 * i + 2, 0, i + 2, True, True, False, False)
            body(HPAIR - 1, 1, HPAIR // 2, True, True, False, False)
            for j in range(HPAIR, NPAIR):
                body(j, j % 2, j // 2 + 1, True, True, True, j > HPAIR)
            body(NPAIR, NPAIR % 2, NPAIR // 2 + 1, False, True, True, True)

        @block.sync
        def _(sp):
            def body(j, u, use, front, back, lat, _):
                if not front:
                    return
                ups, downs, c = (SC["g2"], A["fc2"], 2 * j - NINT) if lat else (A["up"], A["down"], 2 * j)
                sp.wait_ge(up_mm, 2 * NB * j + 2 * NB)
                for i in range(2):
                    sp.dma_start(up[:, 2 * u + i, :], tile_of(ups, c + i)).then_inc(up_loaded[u], 16)
                sp.wait_ge(dn_mm, NT * j + NT)
                for i in range(2):
                    sp.dma_start(dn[:, 2 * u + i, :], tile_of(downs, c + i)).then_inc(dn_loaded[u], 16)
            sp.dma_start(gamma[:], A["L3_ffn_ln_gamma"].partition_broadcast(P)).then_inc(gamma_loaded, 16)
            steps(sp, body)
            for t in range(NT + NR):
                if t >= NR:
                    sp.wait_ge(out_made, t - NR + 1)
                    sp.dma_start(tile_of(out, t - NR), acc[:, t - NR, :]).then_inc(out_stored, 16)
                if t < NT:
                    if t < NR:
                        sp.wait_ge(up_mm, 2 * NB * (NPAIR + 1 + t // 2))
                    sp.dma_start(up[:, t % NR, :], tile_of(SC["x3b"], t)).then_inc(x3b_loaded[t % NR], 16)
            sp.wait_ge(out_stored, 16 * NT)

        @block.gpsimd
        def _(pool):
            for t in range(NT):
                pool.memset(acc[:, t, :], 0.0).then_inc(acc_set, 1)
            pool.memset(eps[:], LN_EPS).then_inc(eps_set, 1)
            for t in range(NT):
                pool.wait_ge(scaled, t + 1)
                pool.wait_ge(x3b_loaded[t % NR], 16 * (t // NR + 1))
                pool.tensor_tensor(acc[:, t, :], acc[:, t, :], up[:, t % NR, :], ALU.add).then_inc(out_made, 1)

        @block.scalar
        def _(act):
            def body(j, u, use, front, back, lat, _):
                if not front:
                    return
                for i in range(2):
                    for n in range(NB):
                        cols = slice(n * HALF, (n + 1) * HALF)
                        k = NB * i + n
                        act.wait_ge(up_mm, 2 * NB * (j + 2) + k + 1)
                        if k == 0:
                            act.wait_ge(dn_mm, NT * j + NT)
                        if lat:
                            act.copy(hid[u][:, i, cols], pu[n][:]).then_inc(hid_made, 1)
                        else:
                            act.activation(hid[u][:, i, cols], pu[n][:], ACT.Relu).then_inc(relu, 1)
                            act.wait_ge(relu, 2 * NB * j + k + 1)
                            act.activation(hid[u][:, i, cols], hid[u][:, i, cols], ACT.Square).then_inc(hid_made, 1)
            for n in range(NB):
                act.wait_ge(g_mm, n + 1)
                act.copy(gT[:, n * HALF:(n + 1) * HALF], pd[n // 2][n % 2][0:EG, :]).then_inc(gT_made, 1)
            steps(act, body)

            act.wait_ge(eps_set, 1)
            for t in range(NT + 1):
                if t < NT:
                    act.wait_ge(centred, t + 1)
                    if t:
                        act.wait_ge(squared, t)
                    act.activation(hid[0][:, 0, 0:D], acc[:, t, :], ACT.Square, bias=nmean[:, t:t + 1],
                                   accum_out=ssq[:, t:t + 1]).then_inc(squared, 1)
                if t:
                    act.wait_ge(shifted, t)
                    act.activation(acc[:, t - 1, :], acc[:, t - 1, :], ACT.Identity, bias=shift[:, t - 1:t],
                                   scale=inv[:, t - 1:t]).then_inc(normed, 1)
                if t < NT:
                    act.wait_ge(squared, t + 1)
                    act.activation(root[:, t:t + 1], ssq[:, t:t + 1], ACT.Sqrt, bias=eps[:], scale=1.0 / D).then_inc(rooted, 1)

        @block.vector
        def _(dve):
            dve.wait_ge(g_turned, 1)
            dve.tensor_copy(logits[:], pd[0][0][:, 0:NT * EG]).then_inc(g_out, 1)
            dve.wait_ge(g_out, 1)
            for t in range(NT):
                dve.max(out=top[:, t, :], in_=logits[:, t * EG:(t + 1) * EG]).then_inc(topped, 1)
            dve.wait_ge(topped, NT)
            dve.tensor_tensor(gate_sum[:].unsqueeze(2), top[:, :, 0:1], top[:, :, 1:2], ALU.add).then_inc(g_summed, 1)
            dve.wait_ge(g_summed, 1)
            dve.wait_ge(acc_set, NT)

            def body(j, u, use, front, back, _, lat):
                if not back:
                    return
                end = not front
                for t in range(NT):
                    dve.wait_ge(dn_mm, NT * (j + 1) + t + 1)
                    for h in range(2):
                        part = acc[:, t, h * HALF:(h + 1) * HALF]
                        if lat:
                            last = dve.scalar_tensor_tensor(out=part, in0=pd[t % 2][h][:], scalar=gate_sum[:, t:t + 1],
                                                            in1=part, op0=ALU.mult, op1=ALU.add,
                                                            accum_out=sums[:, t, h:h + 1] if end else None)
                        else:
                            last = dve.tensor_tensor(part, pd[t % 2][h][:], part, ALU.add)
                        last.then_inc(added, 1)
                    if end:
                        dve.wait_ge(added, 2 * (NT * (j - 1) + t + 3))
                        dve.tensor_scalar(nmean[:, t:t + 1], sums[:, t, 0:1], sums[:, t, 1:2], -1.0 / D,
                                          ALU.add, ALU.mult).then_inc(centred, 1)
                        if t >= 1:
                            scale(t - 1)
                        if t >= 2:
                            weigh(t - 2)

            def scale(t):
                dve.wait_ge(rooted, t + 1)
                dve.reciprocal(inv[:, t:t + 1], root[:, t:t + 1]).then_inc(inverted, 1)
                dve.wait_ge(inverted, t + 1)
                dve.tensor_tensor(shift[:, t:t + 1], nmean[:, t:t + 1], inv[:, t:t + 1], ALU.mult).then_inc(shifted, 1)

            def weigh(t):
                dve.wait_ge(normed, t + 1)
                if t == 0:
                    dve.wait_ge(gamma_loaded, 16)
                dve.tensor_tensor(acc[:, t, :], acc[:, t, :], gamma[:], ALU.mult).then_inc(scaled, 1)

            steps(dve, body)
            scale(NT - 1)
            weigh(NT - 2)
            weigh(NT - 1)

        @block.tensor
        def _(pe):
            pe.sem_inc(up_mm, 4 * NB)
            pe.sem_inc(dn_mm, 2 * NT)
            pe.sem_inc(added, 4)
            for n in range(NB):
                for k in range(KC):
                    last = pe.matmul(pd[n // 2][n % 2][0:EG, :], K["gate"][:, k, :], y3T[:, k, n * HALF:(n + 1) * HALF],
                                     start=k == 0, stop=k == KC - 1)
                last.then_inc(g_mm, 1)

            def body(j, u, use, front, back, lat, _):
                def upward(i, n):
                    if i == 0 and n == 0:
                        pe.wait_ge(up_loaded[u], 32 * use)
                    if i or later(j, 1):
                        pe.wait_ge(hid_made, 2 * NB * j + NB * (i - 1) + n + 1)
                    for k in range(KC):
                        last = pe.matmul(pu[n][:], up[:, 2 * u + i, k * P:(k + 1) * P],
                                         y3T[:, k, n * HALF:(n + 1) * HALF], start=k == 0, stop=k == KC - 1)
                    last.then_inc(up_mm, 1)

                def downward(t):
                    v = 1 - u
                    if t == 0:
                        pe.wait_ge(dn_loaded[v], 32 * back_use)
                        pe.wait_ge(hid_made, 2 * NB * j)
                    pe.wait_ge(added, 2 * (NT * (j - 1) + t + 1))
                    for h in range(2):
                        for i in range(2):
                            last = pe.matmul(pd[t % 2][h][:], hid[v][:, i, t * P:(t + 1) * P],
                                             dn[:, 2 * v + i, h * HALF:(h + 1) * HALF], start=i == 0, stop=i == 1)
                    last.then_inc(dn_mm, 1)

                if isinstance(j, int) and j == 0:
                    for n in range(NB):
                        upward(0, n)
                    pe.wait_ge(gT_made, NB)
                    for t in range(NT):
                        last = pe.transpose(pd[0][0][:, t * EG:(t + 1) * EG], gT[:, t * P:(t + 1) * P], K["ident"][0:EG, 0:EG])
                    last.then_inc(g_turned, 1)
                    for n in range(NB):
                        upward(1, n)
                    pe.wait_ge(g_out, 1)
                    return
                back_use = use if u == 1 else use - 1
                for i in range(2):
                    for n in range(NB):
                        if front:
                            upward(i, n)
                        if back:
                            downward(2 * (NB * i + n))
                            downward(2 * (NB * i + n) + 1)
            steps(pe, body)


def build(nc, A, out):
    SC = {}
    for name, shape in (("att0", (BATCH, NK)), ("att3", (BATCH, NK)), ("bias0", (BATCH, CH)), ("bias3", (BATCH, CH)),
                        ("ctx2", (BATCH, CH)), ("g", (NLAT, P, KC, P)), ("x1", (NT, P, D)), ("y1", (NT, P, D)),
                        ("x2", (NT, P, D)), ("y2T", (NT, P, D)), ("x3b", (NT, P, D))):
        SC[name] = nc.dram_tensor("scratch_" + name, shape, F32).ap()
    SC["g2"] = SC["g"].rearrange("c p k j -> c p (k j)")
    with ExitStack() as ctx:
        s = Scope(nc, ctx)
        K = dict(ident=s.sb("ident", [P, P]), ones=s.sb("ones", [P, P]), desc=s.sb("desc", [P, E2]),
                 gate=s.sb("gate", [P, KC, EG]))
        K["taps_loaded"], K["l0_loaded"], K["l2_loaded"] = s.sems("taps_loaded l0_weights_loaded l2_weights_loaded")
        y3T = s.sb("y3T", [P, KC, NT * P])
        room, taken = y3T[:].rearrange("p k t -> p (k t)"), 0

        def carve(*shape):
            nonlocal taken
            size = 1
            for n in shape:
                size *= n
            part, taken = room[:, taken:taken + size], taken + size
            assert taken <= KC * NT * P
            return part if len(shape) == 1 else part.rearrange("p (a b) -> p a b", b=shape[1])

        K["cbT"], K["scb_row"], K["cmax"] = carve(KC, D), carve(D), carve(HALF)
        K["ctx1"], K["ctx2"] = carve(2, NT), carve(NT * P)
        K["taps"] = [carve(SHIFTS, P) for _ in range(2)]
        K["bias0"] = carve(NT * P)
        with ExitStack() as c0:
            s0 = Scope(nc, c0)
            K["l2_base"], K["l2_B"] = s0.sb("l2_base", [P, KC, D]), s0.sb("l2_B", [P, KC, D])
            K["l2_war"] = s0.sb("l2_war", [P, KC, R2 + E2])
            K["att3"], K["kern3"] = s0.sb("att3", [P, NT, NK]), s0.sb("kern3", [P, CH, NK])
            K["bias3"] = s0.sb("bias3", [P, NT * P])
            with ExitStack() as c1:
                s1 = Scope(nc, c1)
                K["att0"], K["kern0"] = s1.sb("att0", [P, NT, NK]), s1.sb("kern0", [P, CH, NK])
                K["l0_wa"], K["l0_wb"] = s1.sb("l0_wa", [P, KC, P + E0]), s1.sb("l0_wb", [P, D])
                K["kept_loads"] = [(K["l0_wa"][:], A["l0_wa"], K["l0_loaded"]), (K["l0_wb"][:], A["l0_wb"], K["l0_loaded"]),
                                   (K["l2_war"][:], A["l2_war"], K["l2_loaded"]), (K["gate"][:], A["gate"], K["l2_loaded"]),
                                   (K["l2_base"][:], A["l2_base"], K["l2_loaded"]), (K["l2_B"][:], A["l2_B"], K["l2_loaded"])]
                phase_setup(nc, K, A, SC)
                phase_l0(nc, K, A, SC)
            phase_l1(nc, K, A, SC)
            K["y3T"] = y3T
            phase_l2(nc, K, A, SC)
        phase_l3(nc, K, A, SC, out)
    return SC


def lay_out(i):
    import numpy as np

    def c(a):
        return np.ascontiguousarray(a)

    def feat(a, axis=-1):
        a = np.moveaxis(np.asarray(a), axis, -1)
        a = a.reshape(a.shape[:-1] + (HALF, 2)).swapaxes(-1, -2).reshape(a.shape)
        return np.moveaxis(a, -1, axis)

    def chunks(a):
        return c(np.asarray(a).reshape(KC, P, -1).transpose(1, 0, 2))

    a = {}
    a["x"] = c(feat(i["x"])).reshape(NT, P, D)
    a["condT"] = c(np.asarray(i["cond_128"]).T)
    a["fside_S_0"] = c(i["fside_S_0"])
    a["L1_ffn_weight"] = c(feat(feat(i["L1_ffn_weight"], 0), 1))
    for n in ("L1_ffn_bias", "L2_ffn_base_b", "L3_ffn_ln_gamma", "L3_ffn_ln_beta"):
        a[n] = c(feat(i[n]))
    for L in "03":
        for n in ("W0", "b0", "W1", "b1", "W2", "b2", "bias_k"):
            a[f"L{L}_cond_{n}"] = c(i[f"L{L}_cond_{n}"])
        a[f"L{L}_cond_kernels"] = c(np.asarray(i[f"L{L}_cond_weight"])[..., 0].transpose(2, 1, 0)).reshape(CH, NK * CH)
    for L in "12":
        a[f"L{L}_cond_c_weight_T"] = c(np.asarray(i[f"L{L}_cond_c_weight"]).T)
        w = np.asarray(i[f"L{L}_cond_weight"]).reshape(GROUPS, GI, GI, TAPS)
        a[f"L{L}_cond_taps"] = c(w.transpose(0, 2, 3, 1)).reshape(GROUPS, GI, TAPS * GI)
    wa = np.concatenate([np.asarray(i["L0_ffn_A"]).reshape(E0 * R0, D), np.asarray(i["L0_ffn_route_w"])])
    a["l0_wa"] = chunks(feat(wa).T)
    a["l0_wb"] = c(feat(np.asarray(i["L0_ffn_Bw"]).transpose(0, 2, 1))).reshape(P, D)
    war = np.concatenate([np.asarray(i["L2_ffn_A"]), np.asarray(i["L2_ffn_router_w"])])
    a["l2_war"] = chunks(feat(war).T)
    a["l2_base"] = chunks(feat(feat(i["L2_ffn_base_w"], 0), 1).T)
    a["l2_B"] = chunks(feat(np.asarray(i["L2_ffn_B"]).transpose(0, 2, 1)).reshape(D, D))
    a["gate"] = chunks(feat(i["L3_ffn_gate_w"], 0))
    up = feat(i["L3_ffn_up_w"], 0)
    a["up"] = c(up.reshape(KC, P, NINT, P).transpose(2, 1, 0, 3)).reshape(NINT, P, D)
    a["down"] = c(feat(i["L3_ffn_down_w"])).reshape(NINT, P, D)
    a["fc1T"] = c(feat(i["L3_ffn_fc1_w"], 0).T)
    a["L3_ffn_expert_w"] = c(i["L3_ffn_expert_w"])
    a["fc2"] = c(feat(i["L3_ffn_fc2_w"])).reshape(NLAT, P, D)
    return a


def kernel(**inputs):
    import numpy as np
    import concourse.bacc as bacc
    from concourse.bass_utils import run_bass_kernel_spmd as run

    nc = bacc.Bacc("TRN2", target_bir_lowering=False, num_devices=1)
    arrays, aps = {}, {}
    for name, a in lay_out(inputs).items():
        arrays["in_" + name] = a
        aps[name] = nc.dram_tensor("in_" + name, a.shape, F32, kind="ExternalInput").ap()
    out = nc.dram_tensor("out", (NT, P, D), F32, kind="ExternalOutput").ap()
    build(nc, aps, out)
    result = run(nc, [arrays], core_ids=[0]).results[0]["out"]
    return np.asarray(result).reshape(BATCH, CH, 2, HALF).transpose(0, 1, 3, 2).reshape(BATCH, CH, D)
```

```python
from contextlib import ExitStack

import concourse.bass as bass
from concourse import mybir

F32 = mybir.dt.float32
F32R = mybir.dt.float32r
ALU = mybir.AluOpType
ACT = mybir.ActivationFunctionType
AX = mybir.AxisListType

P = 128
BATCH, CH, D = 32, 64, 1024
NT = BATCH * CH // P
KC = D // P
HALF = D // 2
QC = HALF // P
COND = 128
NK = 8
TAPS, PAD, GROUPS = 9, 4, 4
GI = CH // GROUPS
SHIFTS = 5
HP = PAD // 2
E0, R0 = 8, 16
E2, R2 = 16, 64
NINT, NLAT = 16, 4
NPAIR, HPAIR = (NINT + NLAT) // 2, NINT // 2
EG = 8
ROUND = 1.5 * 2.0 ** 23
THRESHOLD = 6.0
LN_EPS = 1e-5
BIG = 3.0e38



def stepped(eng, body, depth):
    def peeled(s):
        uses = [max(s - k, 0) // 2 + 1 for k in range(depth + 1)]
        body(s, s % 2, uses, [0 <= s - k < NT for k in range(depth + 1)])

    pairs = (NT - depth) // 2
    for s in range(depth):
        peeled(s)
    with eng.Fori(0, pairs) as j:
        for r in range(2):
            s0 = depth + r
            body(2 * j + s0, s0 % 2, [j + (s0 - k) // 2 + 1 for k in range(depth + 1)], [True] * (depth + 1))
    for s in range(depth + 2 * pairs, NT + depth):
        peeled(s)


def later(s, n):
    return not isinstance(s, int) or s >= n


class Scope:

    def __init__(self, nc, ctx):
        self.nc, self.ctx, self.owned = nc, ctx, []

    def sb(self, name, shape, dt=F32):
        return self.ctx.enter_context(self.nc.sbuf_tensor(name, shape, dt))

    def split(self, name, shape):
        return self.sb(name + "_hi", shape, F32R), self.sb(name + "_lo", shape, F32R)

    def banks(self, name, n):
        return [self.ctx.enter_context(self.nc.psum_tensor(f"{name}{i}", [P, HALF], F32)) for i in range(n)]

    def semaphore(self, name):
        self.owned.append(self.ctx.enter_context(self.nc.semaphore(name)))
        return self.owned[-1]

    def sems(self, names):
        return [self.semaphore(n) for n in names.split()]

    def slot_sems(self, name, slots=2):
        return [self.semaphore(f"{name}{i}") for i in range(slots)]

    def block(self):
        self.ctx.callback(self.clear)
        return self.ctx.enter_context(self.nc.Block())

    def clear(self):
        numbers = sorted(sem.num for sem in self.owned)
        with self.nc.Block() as block:
            @block.gpsimd
            def _(pool):
                first = 0
                for n in range(1, len(numbers) + 1):
                    if n == len(numbers) or numbers[n] != numbers[n - 1] + 1:
                        pool.sem_clear(range(numbers[first], numbers[n - 1] + 1))
                        first = n


def tile_of(ap, t):
    return ap[bass.ds(t, 1), :, :].rearrange("a p d -> (a p) d")


def parity_store(eng, dram, t, src, sem):
    view = dram.rearrange("t (b o) (q k) -> t q o b k", b=2, q=2)
    for q in range(2):
        dst = view[bass.ds(t, 1), q, :, :, :].rearrange("a o b k -> (a o) b k")
        eng.dma_start(dst, src[q * CH:(q + 1) * CH, :, :]).then_inc(sem, 16)


def parity_load(eng, dram, t, dst, sem):
    view = dram.rearrange("t (b o) (q k) -> t q o b k", b=2, q=2)
    for q in range(2):
        src = view[bass.ds(t, 1), q, :, :, :].rearrange("a o b k -> (a o) b k")
        eng.dma_start(dst[q * CH:(q + 1) * CH, :, :], src).then_inc(sem, 16)


def exact_quotient(dve, order, at, out, den, tmp):
    q, dh, dl, qh, ql, r, rec = [tmp[:, i:i + 1] for i in range(7)]
    steps = [
        lambda: dve.reciprocal(rec, den),
        lambda: dve.tensor_scalar(q, rec, 127.0, None, ALU.mult),
        lambda: dve.tensor_scalar(qh, q, 4097.0, None, ALU.mult),
        lambda: dve.tensor_tensor(ql, qh, q, ALU.subtract),
        lambda: dve.tensor_tensor(qh, qh, ql, ALU.subtract),
        lambda: dve.tensor_tensor(ql, q, qh, ALU.subtract),
        lambda: dve.tensor_scalar(dh, den, 4097.0, None, ALU.mult),
        lambda: dve.tensor_tensor(dl, dh, den, ALU.subtract),
        lambda: dve.tensor_tensor(dh, dh, dl, ALU.subtract),
        lambda: dve.tensor_tensor(dl, den, dh, ALU.subtract),
        lambda: dve.tensor_scalar(r, qh, dh, 127.0, ALU.mult, ALU.subtract),
        lambda: dve.scalar_tensor_tensor(out=r, in0=dh, scalar=ql, in1=r, op0=ALU.mult, op1=ALU.add),
        lambda: dve.scalar_tensor_tensor(out=r, in0=qh, scalar=dl, in1=r, op0=ALU.mult, op1=ALU.add),
        lambda: dve.scalar_tensor_tensor(out=r, in0=ql, scalar=dl, in1=r, op0=ALU.mult, op1=ALU.add),
        lambda: dve.tensor_tensor(r, r, rec, ALU.mult),
        lambda: dve.tensor_tensor(out, q, r, ALU.subtract),
    ]
    assert len(steps) == QUOT
    for n, step in enumerate(steps):
        step().then_inc(order, 1)
        dve.wait_ge(order, at + n + 1)
    return at + QUOT


QUOT = 16


def first_of_largest(dve, order, at, lg, desc, m, key, kmax, mask):
    dve.tensor_reduce(m, lg, AX.X, ALU.max).then_inc(order, 1)
    dve.wait_ge(order, at + 1)
    dve.scalar_tensor_tensor(out=key, in0=lg, scalar=m, in1=desc, op0=ALU.is_ge, op1=ALU.mult).then_inc(order, 1)
    dve.wait_ge(order, at + 2)
    dve.tensor_reduce(kmax, key, AX.X, ALU.max).then_inc(order, 1)
    dve.wait_ge(order, at + 3)
    dve.tensor_scalar(mask, key, kmax, None, ALU.is_equal).then_inc(order, 1)
    dve.wait_ge(order, at + 4)
    return at + 4


class Mixer:

    def __init__(self, s, tag, att, kern):
        self.att, self.kern = att, kern
        self.prod = s.sb(f"{tag}_prod", [P, CH, NK])
        self.acc = s.sb(f"{tag}_acc", [P, CH])
        self.mats = s.sb(f"{tag}_mats", [P, 2, P])
        self.weighted, self.summed, self.placed, self.zeroed = s.sems(
            f"{tag}_weighted {tag}_summed {tag}_placed {tag}_zeroed")

    def weigh(self, pool, t):
        pool.wait_ge(self.summed, t + 1)
        pool.tensor_tensor(self.prod[:], self.kern[:],
                           self.att[:, bass.ds(t, 1), :].to_broadcast([P, CH, NK]), ALU.mult).then_inc(self.weighted, 1)

    def sum(self, dve, t):
        dve.wait_ge(self.weighted, t + 1)
        dve.wait_ge(self.placed, 2 * t + 2)
        dve.tensor_reduce(self.acc[:].unsqueeze(2), self.prod[:], AX.X, ALU.add).then_inc(self.summed, 1)

    def place(self, act, t, slot):
        act.wait_ge(self.summed, t + 2)
        for b in range(2):
            rows = slice(b * CH, (b + 1) * CH)
            act.copy(self.mats[rows, slot, b * CH:(b + 1) * CH], self.acc[rows, :]).then_inc(self.placed, 1)

    def start(self, dve):
        dve.memset(self.mats[:], 0.0).then_inc(self.zeroed, 1)
        dve.sem_inc(self.summed, 1)
        dve.sem_inc(self.placed, 2)

    def multiply(self, pe, t, slot, x, out):
        pe.wait_ge(self.placed, 2 * t + 4)
        for h in range(2):
            for c in range(4):
                last = pe.matmul(out[h][:, c * P:(c + 1) * P], x[:, (4 * h + c) * P:(4 * h + c + 1) * P],
                                 self.mats[:, slot, :], start=True, stop=True)
            yield h, last


def phase_setup(nc, K, A, SC):
    with ExitStack() as ctx:
        s = Scope(nc, ctx)
        cT = s.sb("cT", [COND, BATCH])
        W = {}
        for L in "03":
            W[L] = dict(w0=s.sb(f"w0_{L}", [COND, P]), w1=s.sb(f"w1_{L}", [P, P]), w2=s.sb(f"w2_{L}", [P, NK]),
                        b0=s.sb(f"b0_{L}", [P, 1]), b1=s.sb(f"b1_{L}", [P, 1]), b2=s.sb(f"b2_{L}", [BATCH, NK]),
                        bk=s.sb(f"bk_{L}", [NK, CH]), h0=s.sb(f"h0_{L}", [P, BATCH]), h1=s.sb(f"h1_{L}", [P, BATCH]),
                        lg=s.sb(f"lg_{L}", [BATCH, NK]), m=s.sb(f"m_{L}", [BATCH, 1]), nm=s.sb(f"nm_{L}", [BATCH, 1]),
                        ex=s.sb(f"ex_{L}", [BATCH, NK]), z=s.sb(f"z_{L}", [BATCH, 1]), rz=s.sb(f"rz_{L}", [BATCH, 1]),
                        att=s.sb(f"att_{L}", [BATCH, NK]), attT=s.sb(f"attT_{L}", [NK, BATCH]),
                        bias=s.sb(f"bias_{L}", [BATCH, CH]))
        cw1 = s.sb("cw1", [COND, 2, CH])
        cw2 = s.sb("cw2", [COND, CH])
        fside_col = s.sb("fside_col", [P, 1])
        fside_row = s.sb("fside_row", [BATCH, CH])
        ctx2 = s.sb("ctx2_out", [BATCH, CH])
        raw = s.sb("qw_raw", [P, 2, D])
        cb = s.sb("qw_cb", [P, D])
        col = s.sb("qw_col", [P, 4])
        tmp = s.sb("qw_tmp", [P, 8])
        diag = s.sb("qw_diag", [P, P])
        fc1 = s.sb("fc1_raw", [P, NLAT, D])
        exp = s.sb("exp_raw", [P, NLAT, NLAT * P])
        gout = s.sb("g_out", [P, 2, NLAT * P])
        (pm,) = s.banks("pm", 1)
        (px,) = s.banks("px", 1)
        tp = s.banks("qw_tp", 2)
        (bc,) = s.banks("qw_bc", 1)
        pg = s.banks("pg", 2)
        (ident_zeroed, ident_made, desc_made, taps_zeroed, cond_loaded, mlp, gelus, mlp_step, ctx_mm, ctx_out,
         order, rounded, turned, taken, diag_made, spread, spread_out, fc_loaded, g_mm, g_out, bias_stored, att_turned,
         kept, exps) = s.sems(
            "ident_zeroed ident_made desc_made taps_zeroed cond_loaded mlp_mm gelus mlp_step ctx_mm ctx_out "
            "qw_step cb_rounded cb_turned cb_taken scb_diag scb_spread scb_row_out fc_loaded g_mm g_out_ready bias_stored "
            "att_turned setup_kept exps")
        att_stored = s.slot_sems("att_stored")
        qw_loaded, g_stored = K["qw_loaded"], K["g_stored"]
        per = QUOT + 4
        block = s.block()

        loads = [(cT[:], A["condT"])]
        for L in "03":
            w = W[L]
            loads += [(w["w0"][:], A[f"L{L}_cond_W0"]), (w["b0"][:], A[f"L{L}_cond_b0"].rearrange("(p a) -> p a", a=1)),
                      (w["w1"][:], A[f"L{L}_cond_W1"]), (w["b1"][:], A[f"L{L}_cond_b1"].rearrange("(p a) -> p a", a=1)),
                      (w["w2"][:], A[f"L{L}_cond_W2"]), (w["b2"][:], A[f"L{L}_cond_b2"].partition_broadcast(BATCH)),
                      (w["bk"][:], A[f"L{L}_cond_bias_k"])]
        fcol = A["fside_S_0"].rearrange("(p a) -> p a", a=1)
        loads += [(cw1[:, 0, :], A["L1_cond_c_weight_T"]), (cw1[:, 1, :], A["L1_cond_c_weight_T"]),
                  (cw2[:], A["L2_cond_c_weight_T"]), (fside_row[:], A["fside_S_0"].partition_broadcast(BATCH)),
                  (fside_col[0:CH, :], fcol), (fside_col[CH:P, :], fcol)]
        all_loaded = 16 * len(loads)

        tap_loads = []
        for dst, name in zip(K["taps"], ("L1_cond_taps", "L2_cond_taps")):
            taps = A[name].rearrange("g i (k o) -> g i k o", k=TAPS)
            for p in range(2):
                for q in range(2):
                    js = [j for j in range(SHIFTS) if 0 <= 2 * j + p - q < TAPS]
                    k0 = 2 * js[0] + p - q
                    for g in range(GROUPS):
                        tap_loads.append((dst[p * CH + g * GI:p * CH + (g + 1) * GI, js[0]:js[-1] + 1,
                                              q * CH + g * GI:q * CH + (g + 1) * GI],
                                          taps[g][:, k0:k0 + 2 * len(js) - 1:2, :]))

        @block.sync
        def _(sp):
            for dst, src in loads:
                sp.dma_start(dst, src).then_inc(cond_loaded, 16)
            sp.dma_start(fc1[:], A["fc1T"].rearrange("(l p) h -> p l h", p=P)).then_inc(fc_loaded, 16)
            sp.dma_start(exp[:], A["L3_ffn_expert_w"].rearrange("(l p) m -> p l m", p=P)).then_inc(fc_loaded, 16)
            for n, L in enumerate("03"):
                sp.wait_ge(mlp_step, 6 * n + 5)
                sp.dma_start(SC[f"att{L}"], W[L]["att"][:]).then_inc(att_stored[n], 16)
                sp.wait_ge(att_stored[n], 16)
                src = SC[f"att{L}"].rearrange("(t b) k -> b t k", b=2)
                for b in range(2):
                    sp.dma_start(K[f"att{L}"][b * CH:(b + 1) * CH, :, :], src[b].partition_broadcast(CH)).then_inc(kept, 16)
                    sp.dma_start(K[f"kern{L}"][b * CH:(b + 1) * CH, :, :],
                                 A[f"L{L}_cond_kernels"].rearrange("i (o k) -> i o k", k=NK)).then_inc(kept, 16)
                sp.wait_ge(mlp_step, 6 * n + 6)
                sp.dma_start(SC[f"bias{L}"], W[L]["bias"][:]).then_inc(bias_stored, 16)
                sp.wait_ge(bias_stored, 16 * (2 * n + 1))
                sp.dma_start(K[f"bias{L}"][:], SC[f"bias{L}"].rearrange("b o -> (b o)").partition_broadcast(P)).then_inc(kept, 16)
                if n == 0:
                    sp.wait_ge(ctx_out, 3)
                    sp.dma_start(SC["ctx2"], ctx2[:]).then_inc(bias_stored, 16)
                    sp.wait_ge(bias_stored, 32)
                    sp.dma_start(K["ctx2"][:], SC["ctx2"].rearrange("b o -> (b o)").partition_broadcast(P)).then_inc(kept, 16)
            sp.wait_ge(kept, 16 * 11)

        @block.gpsimd
        def _(pool):
            for c in range(2):
                pool.dma_start(raw[:, c, :], A["L1_ffn_weight"][c * P:(c + 1) * P, :]).then_inc(qw_loaded[c], 16)
            pool.memset(K["ident"][:], 0.0).then_inc(ident_zeroed, 1)
            pool.memset(K["ones"][:], 1.0).then_inc(ident_made, 1)
            pool.wait_ge(ident_zeroed, 1)
            pool.affine_select(out=K["ident"][:], in_=K["ident"][:], compare_op=ALU.not_equal, fill=1.0,
                               base=0, pattern=[[-1, P]], channel_multiplier=1).then_inc(ident_made, 1)
            for e in range(E2):
                pool.memset(K["desc"][:, e:e + 1], float(E2 - e)).then_inc(desc_made, 1)
            pool.wait_ge(taps_zeroed, 2)
            for dst, src in tap_loads:
                pool.dma_start(dst, src).then_inc(K["taps_loaded"], 16)
            for k in range(KC):
                c = k + 2
                if c < KC:
                    pool.wait_ge(rounded, c - 1)
                    pool.dma_start(raw[:, c % 2, :], A["L1_ffn_weight"][c * P:(c + 1) * P, :]).then_inc(qw_loaded[c % 2], 16)
                pool.wait_ge(g_out, k + 1)
                pool.dma_start(SC["g"][:, :, k, :].rearrange("c p j -> p c j"),
                               gout[:, k % 2, :].rearrange("p (c j) -> p c j", c=NLAT)).then_inc(g_stored[k % 2], 16)
            for slot in g_stored:
                pool.wait_ge(slot, 16 * KC // 2)

        @block.tensor
        def _(pe):
            def mlp_layer(n, L):
                w = W[L]
                if n:
                    pe.wait_ge(mlp_step, 6)
                pe.matmul(pm[:, 0:BATCH], w["w0"][:], cT[:], start=True, stop=True).then_inc(mlp, 1)
                yield
                pe.wait_ge(gelus, 2 * n + 1)
                pe.matmul(pm[:, 0:BATCH], w["w1"][:], w["h0"][:], start=True, stop=True).then_inc(mlp, 1)
                yield
                pe.wait_ge(gelus, 2 * n + 2)
                pe.matmul(pm[0:BATCH, 0:NK], w["h1"][:], w["w2"][:], start=True, stop=True).then_inc(mlp, 1)
                yield
                pe.wait_ge(mlp_step, 6 * n + 5)
                pe.transpose(pm[0:NK, 0:BATCH], w["att"][:], K["ident"][0:BATCH, 0:BATCH]).then_inc(mlp, 1)
                yield
                pe.wait_ge(att_turned, n + 1)
                pe.matmul(pm[0:BATCH, 0:CH], w["attT"][:], w["bk"][:], start=True, stop=True).then_inc(mlp, 1)
                yield

            def latent(k):
                if k == 0:
                    pe.wait_ge(fc_loaded, 32)
                if k >= 2:
                    pe.wait_ge(g_out, k - 1)
                for l in range(NLAT):
                    last = pe.matmul(pg[k % 2][:], fc1[:, l, k * P:(k + 1) * P], exp[:, l, :], start=l == 0, stop=l == NLAT - 1)
                last.then_inc(g_mm, 1)

            def weight(c):
                pe.wait_ge(rounded, c + 1)
                for h in range(2):
                    if c:
                        pe.wait_ge(taken, 2 * (c - 1) + h + 1)
                    for j in range(4):
                        k = 4 * h + j
                        last = pe.transpose(tp[h][:, j * P:(j + 1) * P], cb[:, k * P:(k + 1) * P], K["ident"][:])
                    last.then_inc(turned, 1)
                pe.wait_ge(diag_made, c + 1)
                if c:
                    pe.wait_ge(spread_out, c)
                pe.matmul(bc[:, 0:P], K["ones"][:], diag[:], start=True, stop=True).then_inc(spread, 1)

            pe.wait_ge(cond_loaded, all_loaded)
            pe.wait_ge(ident_made, 2)
            pe.matmul(px[:, 0:BATCH], cw1[:].rearrange("d b o -> d (b o)"), cT[:], start=True, stop=True).then_inc(ctx_mm, 1)
            pe.matmul(px[0:BATCH, 2 * CH:3 * CH], cT[:], cw2[:], start=True, stop=True).then_inc(ctx_mm, 1)
            for n, L in enumerate("03"):
                for _ in mlp_layer(n, L):
                    pass
            for k in range(KC):
                weight(k)
                latent(k)

        @block.scalar
        def _(act):
            for dst, src, sem in K["kept_loads"]:
                act.dma_start(dst, src).then_inc(sem, 16)
            act.wait_ge(cond_loaded, all_loaded)
            for n, L in enumerate("03"):
                w = W[L]
                act.wait_ge(mlp, 5 * n + 1)
                act.activation(w["h0"][:], pm[:, 0:BATCH], ACT.Gelu, bias=w["b0"][:]).then_inc(gelus, 1)
                act.wait_ge(mlp, 5 * n + 2)
                act.activation(w["h1"][:], pm[:, 0:BATCH], ACT.Gelu, bias=w["b1"][:]).then_inc(gelus, 1)
                act.wait_ge(mlp_step, 6 * n + 3)
                act.activation(w["ex"][:], w["lg"][:], ACT.Exp, bias=w["nm"][:], accum_out=w["z"][:]).then_inc(exps, 1)
                act.wait_ge(mlp, 5 * n + 4)
                act.copy(w["attT"][:], pm[0:NK, 0:BATCH]).then_inc(att_turned, 1)
            for c in range(KC):
                for h in range(2):
                    act.wait_ge(turned, 2 * c + h + 1)
                    act.copy(K["cbT"][:, 4 * h:4 * h + 4, c * P:(c + 1) * P],
                             tp[h][:].rearrange("p (k o) -> p k o", k=4)).then_inc(taken, 1)
                act.wait_ge(g_mm, c + 1)
                if c >= 2:
                    act.wait_ge(g_stored[c % 2], 16 * (c // 2))
                act.copy(gout[:, c % 2, :], pg[c % 2][:]).then_inc(g_out, 1)

        @block.vector
        def _(dve):
            for taps in K["taps"]:
                dve.memset(taps[:], 0.0).then_inc(taps_zeroed, 1)
            dve.wait_ge(ctx_mm, 2)
            dve.wait_ge(cond_loaded, all_loaded)
            pcv = px[:, 0:BATCH].rearrange("p (t b) -> p b t", b=2)
            for b in range(2):
                dve.tensor_scalar(K["ctx1"][:, b, :], pcv[:, b, :], fside_col[:], None, ALU.add).then_inc(ctx_out, 1)
            dve.tensor_tensor(ctx2[:], px[0:BATCH, 2 * CH:3 * CH], fside_row[:], ALU.add).then_inc(ctx_out, 1)
            for n, L in enumerate("03"):
                w, base = W[L], 6 * n
                dve.wait_ge(mlp, 5 * n + 3)
                dve.tensor_tensor(w["lg"][:], pm[0:BATCH, 0:NK], w["b2"][:], ALU.add).then_inc(mlp_step, 1)
                dve.wait_ge(mlp_step, base + 1)
                dve.tensor_reduce(w["m"][:], w["lg"][:], AX.X, ALU.max).then_inc(mlp_step, 1)
                dve.wait_ge(mlp_step, base + 2)
                dve.tensor_scalar(w["nm"][:], w["m"][:], -1.0, None, ALU.mult).then_inc(mlp_step, 1)
                dve.wait_ge(exps, n + 1)
                dve.reciprocal(w["rz"][:], w["z"][:]).then_inc(mlp_step, 1)
                dve.wait_ge(mlp_step, base + 4)
                dve.tensor_scalar(w["att"][:], w["ex"][:], w["rz"][:], None, ALU.mult).then_inc(mlp_step, 1)
                dve.wait_ge(mlp, 5 * n + 5)
                dve.tensor_copy(w["bias"][:], pm[0:BATCH, 0:CH]).then_inc(mlp_step, 1)
            dve.wait_ge(ident_made, 2)
            for c in range(KC):
                at, w = per * c, raw[:, c % 2, :]
                dve.wait_ge(qw_loaded[c % 2], 16 * (c // 2 + 1))
                dve.tensor_reduce(col[:, 0:1], w, AX.X, ALU.max, apply_absolute_value=True).then_inc(order, 1)
                dve.wait_ge(order, at + 1)
                dve.tensor_scalar(col[:, 1:2], col[:, 0:1], 1e-8, None, ALU.max).then_inc(order, 1)
                dve.wait_ge(order, at + 2)
                at = exact_quotient(dve, order, at + 2, col[:, 2:3], col[:, 1:2], tmp)
                dve.tensor_scalar(col[:, 3:4], col[:, 0:1], 1.0 / 127.0, None, ALU.mult).then_inc(order, 1)
                dve.tensor_scalar(w, w, col[:, 2:3], ROUND, ALU.mult, ALU.add).then_inc(order, 1)
                dve.wait_ge(order, at + 2)
                if c:
                    dve.wait_ge(turned, 2 * c)
                    dve.wait_ge(spread, c)
                dve.tensor_scalar(cb[:], w, ROUND, None, ALU.subtract).then_inc(rounded, 1)
                dve.tensor_scalar(diag[:], K["ident"][:], col[:, 3:4], None, ALU.mult).then_inc(diag_made, 1)
                dve.wait_ge(spread, c + 1)
                dve.tensor_copy(K["scb_row"][:, c * P:(c + 1) * P], bc[:, 0:P]).then_inc(spread_out, 1)
            dve.wait_ge(desc_made, E2)


def phase_l0(nc, K, A, SC):
    with ExitStack() as ctx:
        s_ = Scope(nc, ctx)
        mix = Mixer(s_, "mix0", K["att0"], K["kern0"])
        wa, wb = K["l0_wa"], K["l0_wb"]
        x = s_.sb("x_in", [P, 2, D])
        yT = s_.sb("y0T", [P, D])
        wh = s_.sb("wh", [P, P])
        whT = s_.sb("whT", [P, P])
        x1 = [s_.sb(f"x1_{i}", [P, 2, HALF + PAD]) for i in range(2)]
        y1 = s_.sb("y1", [P, 2, 2, HALF])
        mag = s_.sb("y1_mag", [P, 2, HALF])
        xmov = s_.sb("x_moved", [P, HALF])
        small = s_.sb("l0_small", [P, 32])
        m, kmax = small[:, 0:1], small[:, 1:2]
        lg, key, mask = small[:, 8:16], small[:, 16:24], small[:, 24:32]
        py = s_.banks("py", 2)
        (ph,) = s_.banks("ph", 1)
        (pt,) = s_.banks("pt", 1)
        po = s_.banks("po", 2)
        pv = s_.banks("pv", 2)
        ctx_col = s_.sb("ctx_col", [P, 2, 2])
        x_loaded, y1_stored, x1_stored = [s_.slot_sems(n) for n in ("x_loaded", "y1_stored", "x1_stored")]
        conv_done, y1_made, mag_made, seen = [s_.slot_sems(n) for n in ("conv_done_b", "y1_made_b", "mag_made_b", "mag_seen_b")]
        (x_free, y_mm, y_made, h_mm, route, wh_made, wh_turned, whT_made, o_mm, x1_b0, x1_b1_moved, x1_b1, edge, cmax_set,
         ctx_placed) = s_.sems(
            "x_read y0_mm y0_made h_mm route_step wh_made wh_turned whT_made o_mm x1_b0_made x1_b1_moved x1_b1_made "
            "x1_edges cmax_zeroed ctx_placed")
        block = s_.block()
        cmax = K["cmax"]
        inner = slice(HP, HP + HALF)

        @block.sync
        def _(sp):
            def body(s, u, uses, has):
                if has[0]:
                    sp.wait_ge(x_free, s + 1)
                    sp.dma_start(x[:, u, :], tile_of(A["x"], s)).then_inc(x_loaded[u], 16)
                if has[1]:
                    sp.wait_ge(x1_b0, 2 * s)
                    sp.wait_ge(x1_b1, s)
                    parity_store(sp, SC["x1"], s - 1, x1[1 - u][:, :, inner], x1_stored[1 - u])
                if has[2]:
                    for b in range(2):
                        sp.wait_ge(y1_made[b], s - 1)
                    parity_store(sp, SC["y1"], s - 2, y1[:, u, :, :], y1_stored[u])
            stepped(sp, body, 2)
            for slot in x1_stored + y1_stored:
                sp.wait_ge(slot, 32 * (NT // 2) + 32)

        @block.gpsimd
        def _(pool):
            def body(s, u, uses, has):
                if has[0]:
                    mix.weigh(pool, s)
                if has[1]:
                    if later(s, 3):
                        pool.wait_ge(mag_made[1], s - 2)
                    pool.tensor_copy(ctx_col[:, 1 - u, :].unsqueeze(2),
                                     K["ctx1"][:, :, bass.ds(s - 1, 1)]).then_inc(ctx_placed, 1)
                    pool.wait_ge(x1_b1_moved, 4 * s)
                    pool.tensor_tensor(x1[1 - u][:, 1, inner], x1[1 - u][:, 1, inner], xmov[:], ALU.add).then_inc(x1_b1, 1)
            stepped(pool, body, 2)

        @block.scalar
        def _(act):
            act.wait_ge(mix.zeroed, 1)
            act.wait_ge(edge, 4)

            def conv_out(b, slot, tile, use):
                act.wait_ge(conv_done[b], tile + 1)
                if b == 0:
                    act.wait_ge(y1_stored[slot], 32 * use)
                act.wait_ge(ctx_placed, tile + 1)
                bias = ctx_col[:, slot, b:b + 1]
                act.activation(y1[:, slot, b, :], pv[b][:], ACT.Identity, bias=bias).then_inc(y1_made[b], 1)
                act.wait_ge(seen[b], tile + 1)
                act.activation(mag[:, b, :], pv[b][:], ACT.Abs, bias=bias).then_inc(mag_made[b], 1)

            def body(s, u, uses, has):
                if has[0]:
                    if later(s, 2):
                        act.wait_ge(y_mm, 2 * (s - 1))
                    mix.place(act, s, u)
                if has[1]:
                    act.wait_ge(o_mm, 2 * s)
                    act.wait_ge(x1_stored[1 - u], 32 * uses[1])
                    if later(s, 3):
                        act.wait_ge(conv_done[1], s - 2)
                    if later(s, 2):
                        act.wait_ge(x1_b1, s - 1)
                    for q in range(2):
                        act.copy(x1[1 - u][q * CH:(q + 1) * CH, 1, inner], po[q][CH:P, :]).then_inc(x1_b1_moved, 1)
                        act.copy(xmov[q * CH:(q + 1) * CH, :], x[CH:P, 1 - u, q * HALF:(q + 1) * HALF]).then_inc(x1_b1_moved, 1)
                if has[2]:
                    conv_out(1, u, s - 2, uses[2])
                if has[1]:
                    conv_out(0, 1 - u, s - 1, uses[1])
                if has[0]:
                    act.wait_ge(wh_turned, s + 1)
                    act.copy(whT[:], pt[:, 0:P]).then_inc(whT_made, 1)
            stepped(act, body, 2)

        @block.vector
        def _(dve):
            mix.start(dve)
            for tiles in x1:
                dve.memset(tiles[:, :, 0:HP], 0.0).then_inc(edge, 1)
                dve.memset(tiles[:, :, HP + HALF:], 0.0).then_inc(edge, 1)
            dve.memset(cmax[:], 0.0).then_inc(cmax_set, 1)
            dve.wait_ge(cmax_set, 1)
            dve.wait_ge(edge, 4)
            dve.sem_inc(x_free, 2)
            for sem in seen:
                dve.sem_inc(sem, 1)
            for sem in y1_stored + x1_stored:
                dve.sem_inc(sem, 32)

            def see(b, tile):
                dve.wait_ge(mag_made[b], tile + 1)
                dve.tensor_tensor(cmax[:], mag[:, b, :], cmax[:], ALU.max).then_inc(seen[b], 1)
                dve.wait_ge(seen[b], tile + 2)

            def body(s, u, uses, has):
                if has[0]:
                    mix.sum(dve, s)
                if has[1]:
                    dve.wait_ge(o_mm, 2 * s)
                    dve.wait_ge(x1_stored[1 - u], 32 * uses[1])
                    if later(s, 3):
                        dve.wait_ge(conv_done[0], s - 2)
                    for q in range(2):
                        dve.tensor_tensor(x1[1 - u][q * CH:(q + 1) * CH, 0, inner], po[q][0:CH, :],
                                          x[0:CH, 1 - u, q * HALF:(q + 1) * HALF], ALU.add).then_inc(x1_b0, 1)
                    dve.wait_ge(x1_b0, 2 * s)
                    dve.wait_ge(x1_b1_moved, 4 * s)
                    dve.sem_inc(x_free, 1)
                if has[0]:
                    if later(s, 1):
                        dve.wait_ge(h_mm, s)
                    for h in range(2):
                        dve.wait_ge(y_mm, 2 * s + h + 1)
                        dve.tensor_tensor(yT[:, h * HALF:(h + 1) * HALF].rearrange("p (c k) -> p c k", c=4),
                                          py[h][:].rearrange("p (c k) -> p c k", c=4),
                                          K["bias0"][:, bass.ds(s * P, P)].unsqueeze(1).to_broadcast([P, 4, P]),
                                          ALU.add).then_inc(y_made, 1)
                if has[2]:
                    see(1, s - 2)
                if has[0]:
                    at = 6 * s
                    dve.wait_ge(h_mm, s + 1)
                    dve.tensor_copy(lg, ph[:, P:P + E0]).then_inc(route, 1)
                    dve.wait_ge(route, at + 1)
                    at = first_of_largest(dve, route, at + 1, lg, K["desc"][:, E2 - E0:E2], m, key, kmax, mask)
                    dve.tensor_scalar(key, mask, m, None, ALU.mult).then_inc(route, 1)
                    dve.wait_ge(route, at + 1)
                    if later(s, 1):
                        dve.wait_ge(wh_turned, s)
                    dve.tensor_tensor(wh[:].rearrange("p (e r) -> p e r", e=E0),
                                      ph[:, 0:P].rearrange("p (e r) -> p e r", e=E0),
                                      key.unsqueeze(2).to_broadcast([P, E0, R0]), ALU.mult).then_inc(wh_made, 1)
                if has[1]:
                    see(0, s - 1)
            stepped(dve, body, 2)

        @block.tensor
        def _(pe):
            pe.wait_ge(K["l0_loaded"], 32)
            pe.wait_ge(K["taps_loaded"], 16 * 2 * 4 * GROUPS)

            def conv(b, slot, tile, n0, n1):
                for n in range(n0, n1):
                    last = pe.matmul(pv[b][:], K["taps"][0][:, n, :], x1[slot][:, b, n:n + HALF],
                                     start=n == 0, stop=n == SHIFTS - 1)
                if n1 == SHIFTS:
                    last.then_inc(conv_done[b], 1)

            def body(s, u, uses, has):
                if has[1]:
                    pe.wait_ge(whT_made, s)
                    if later(s, 2):
                        pe.wait_ge(x1_b0, 2 * (s - 1))
                        pe.wait_ge(x1_b1_moved, 4 * (s - 1))
                    for q in range(2):
                        pe.matmul(po[q][:], whT[:], wb[:, q * HALF:(q + 1) * HALF], start=True, stop=True).then_inc(o_mm, 1)
                if has[0]:
                    pe.wait_ge(x_loaded[u], 16 * uses[0])
                    if later(s, 1):
                        pe.wait_ge(y_made, 2 * s)
                    for h, last in mix.multiply(pe, s, u, x[:, u, :], py):
                        last.then_inc(y_mm, 1)
                if has[2]:
                    pe.wait_ge(x1_b1, s - 1)
                    if later(s, 3):
                        pe.wait_ge(mag_made[1], s - 2)
                    conv(1, u, s - 2, 0, SHIFTS)
                if has[0]:
                    pe.wait_ge(y_made, 2 * s + 2)
                    if later(s, 1):
                        pe.wait_ge(wh_made, s)
                    for k in range(KC):
                        last = pe.matmul(ph[:, 0:P + E0], yT[:, k * P:(k + 1) * P], wa[:, k, :], start=k == 0, stop=k == KC - 1)
                    last.then_inc(h_mm, 1)
                if has[1]:
                    pe.wait_ge(x1_b0, 2 * s)
                    if later(s, 2):
                        pe.wait_ge(mag_made[0], s - 1)
                    conv(0, 1 - u, s - 1, 0, 4)
                if has[0]:
                    pe.wait_ge(wh_made, s + 1)
                    if later(s, 1):
                        pe.wait_ge(whT_made, s)
                    pe.transpose(pt[:, 0:P], wh[:], K["ident"][:]).then_inc(wh_turned, 1)
                if has[1]:
                    conv(0, 1 - u, s - 1, 4, SHIFTS)
            stepped(pe, body, 2)


def phase_l1(nc, K, A, SC):
    with ExitStack() as ctx:
        s_ = Scope(nc, ctx)
        y1 = s_.sb("l1_y1", [P, 2, D])
        x1 = s_.sb("l1_x1", [P, 2, 2, HALF])
        bias = s_.sb("l1_bias", [P, HALF])
        keep_row = s_.sb("keep_row", [P, D])
        yi = s_.sb("yi", [P, D])
        z = s_.sb("z", [P, D])
        zT = [s_.split(f"zT{i}", [P, D]) for i in range(2)]
        x2 = [s_.sb(f"x2_{i}", [P, 2, HALF + PAD]) for i in range(2)]
        y2 = s_.sb("y2", [P, 2, D])
        col = s_.sb("l1_col", [P, 4])
        tmp = s_.sb("l1_tmp", [P, 8])
        top = s_.sb("col_top", [P, QC, 2])
        keep = s_.sb("col_keep", [P, QC, 2])
        diag = s_.sb("keep_diag", [P, 2, P])
        pz = s_.banks("pz", 2)
        pf = s_.banks("pf", 2)
        pv = s_.banks("pw", 2)
        y_loaded, x_loaded, y2_stored, x2_stored = [
            s_.slot_sems(n) for n in ("l1_y_loaded", "l1_x_loaded", "y2_stored", "x2_stored")]
        conv_done, y2_made = [s_.slot_sems(n) for n in ("conv2_done_b", "y2_made_b")]
        (x_free, bias_loaded, q, rest, rounded, z_made, z_turned, zT_hi, zT_lo, f_mm, xb, x2_scaled, x2_made, edge,
         turned, topped, kept, diag_made, spread, keep_out, y2_half) = s_.sems(
            "l1_x_read l1_bias_loaded quant_step outlier_part row_rounded z_made z_turned zT_hi zT_lo f_mm xb_made "
            "x2_scaled x2_made x2_edges cmax_turned col_topped col_kept keep_diag_made keep_spread keep_row_out y2_half_made")
        QS = 4 + QUOT
        block = s_.block()
        inner = slice(HP, HP + HALF)

        @block.sync
        def _(sp):
            for q_ in range(2):
                sp.dma_start(bias[q_ * CH:(q_ + 1) * CH, :],
                             A["L1_ffn_bias"][q_ * HALF:(q_ + 1) * HALF].partition_broadcast(CH)).then_inc(bias_loaded, 16)

            def body(s, u, uses, has):
                if has[0]:
                    sp.wait_ge(z_made, s + 1)
                    sp.dma_start(y1[:, u, :], tile_of(SC["y1"], s)).then_inc(y_loaded[u], 16)
                    sp.wait_ge(x_free, s + 1)
                    parity_load(sp, SC["x1"], s, x1[:, u, :, :], x_loaded[u])
                if has[1]:
                    sp.wait_ge(x2_made, s)
                    parity_store(sp, SC["x2"], s - 1, x2[1 - u][:, :, inner], x2_stored[1 - u])
                if has[2]:
                    for b in range(2):
                        sp.wait_ge(y2_made[b], s - 1)
                    sp.dma_start(tile_of(SC["y2T"], s - 2), y2[:, u, :]).then_inc(y2_stored[u], 16)
            stepped(sp, body, 2)
            for slot in x2_stored:
                sp.wait_ge(slot, 32 * (NT // 2) + 32)
            for slot in y2_stored:
                sp.wait_ge(slot, 16 * (NT // 2) + 16)

        @block.gpsimd
        def _(pool):
            pool.wait_ge(bias_loaded, 32)

            def body(s, u, uses, has):
                if has[0]:
                    pool.wait_ge(q, QS * s + 1)
                    pool.tensor_tensor(y1[:, u, :], y1[:, u, :], yi[:], ALU.subtract).then_inc(rest, 1)
                    pool.wait_ge(x_loaded[u], 32 * uses[0])
                    pool.tensor_tensor(x1[:, u, :, :], x1[:, u, :, :], bias[:].unsqueeze(1).to_broadcast([P, 2, HALF]),
                                       ALU.add).then_inc(xb, 1)
                if has[1]:
                    pool.wait_ge(x2_scaled, 4 * s)
                    pool.wait_ge(xb, s)
                    pool.tensor_tensor(x2[1 - u][:, :, inner], x2[1 - u][:, :, inner], x1[:, 1 - u, :, :],
                                       ALU.add).then_inc(x2_made, 1)
                    pool.wait_ge(x2_made, s)
                    pool.sem_inc(x_free, 1)
            pool.sem_inc(x_free, 2)
            stepped(pool, body, 2)

        @block.scalar
        def _(act):
            def body(s, u, uses, has):
                if has[0]:
                    for h in range(2):
                        act.wait_ge(z_turned, 2 * s + h + 1)
                        if h == 0 and later(s, 2):
                            act.wait_ge(f_mm, 2 * (s - 1))
                        act.copy(zT[u][0][:, h * HALF:(h + 1) * HALF], pz[h][:]).then_inc(zT_hi, 1)
            stepped(act, body, 2)

        @block.vector
        def _(dve):
            for tiles in x2:
                dve.memset(tiles[:, :, 0:HP], 0.0).then_inc(edge, 1)
                dve.memset(tiles[:, :, HP + HALF:], 0.0).then_inc(edge, 1)
            dve.wait_ge(edge, 4)
            dve.sem_inc(z_made, 2)
            for sem in x2_stored:
                dve.sem_inc(sem, 32)
            for sem in y2_stored:
                dve.sem_inc(sem, 16)
            dve.wait_ge(turned, 1)
            dve.tensor_reduce(top[:].rearrange("p c q -> p (c q)").unsqueeze(2),
                              pz[0][:].rearrange("p (a o) -> p a o", o=CH), AX.X, ALU.max).then_inc(topped, 1)
            dve.wait_ge(topped, 1)
            dve.tensor_scalar(keep[:], top[:], THRESHOLD, None, ALU.is_le).then_inc(kept, 1)
            dve.wait_ge(kept, 1)
            for n in range(KC):
                if n >= 2:
                    dve.wait_ge(spread, n - 1)
                dve.tensor_scalar(diag[:, n % 2, :], K["ident"][:], keep[:, n % QC, n // QC:n // QC + 1], None,
                                  ALU.mult).then_inc(diag_made, 1)
            dve.wait_ge(spread, KC)
            for h in range(2):
                dve.tensor_copy(keep_row[:, h * HALF:(h + 1) * HALF], pf[h][:]).then_inc(keep_out, 1)
            dve.wait_ge(keep_out, 2)

            def conv_out(b, s, u, use):
                dve.wait_ge(conv_done[b], s - 1)
                if b == 0:
                    dve.wait_ge(y2_stored[u], 16 * use)
                out = y2[:, u, :].rearrange("p (q c b o) -> p b c q o", q=2, c=QC, b=2)[:, b]
                row = K["ctx2"][:, bass.ds((s - 2) * P + b * CH, CH)]
                for q_ in range(2):
                    dve.tensor_tensor(out[:, :, q_, :], pv[b][:].rearrange("p (c q o) -> p c q o", c=QC, q=2)[:, :, q_, :],
                                      row.unsqueeze(1).to_broadcast([P, QC, CH]), ALU.add).then_inc(y2_half, 1)
                dve.wait_ge(y2_half, 4 * (s - 2) + 2 * b + 2)
                dve.sem_inc(y2_made[b], 1)

            def scale(h, s, u):
                dve.wait_ge(f_mm, 2 * (s - 1) + h + 1)
                for b in range(2):
                    dve.tensor_tensor(x2[1 - u][h * CH:(h + 1) * CH, b, inner], pf[h][b * CH:(b + 1) * CH, :],
                                      K["scb_row"][b * CH:(b + 1) * CH, h * HALF:(h + 1) * HALF], ALU.mult).then_inc(x2_scaled, 1)

            def body(s, u, uses, has):
                if has[0]:
                    at, y = QS * s, y1[:, u, :]
                    dve.wait_ge(y_loaded[u], 16 * uses[0])
                    if later(s, 1):
                        dve.wait_ge(rest, s)
                    dve.tensor_tensor(yi[:], y, keep_row[:], ALU.mult).then_inc(q, 1)
                    dve.wait_ge(q, at + 1)
                    dve.tensor_reduce(col[:, 0:1], yi[:], AX.X, ALU.max, apply_absolute_value=True).then_inc(q, 1)
                    dve.wait_ge(q, at + 2)
                    dve.tensor_scalar(col[:, 1:2], col[:, 0:1], 1e-8, None, ALU.max).then_inc(q, 1)
                    dve.wait_ge(q, at + 3)
                    at = exact_quotient(dve, q, at + 3, col[:, 2:3], col[:, 1:2], tmp)
                    dve.tensor_scalar(col[:, 3:4], col[:, 1:2], 1.0 / 127.0, None, ALU.mult).then_inc(q, 1)
                    dve.wait_ge(rest, s + 1)
                    dve.tensor_scalar(yi[:], yi[:], col[:, 2:3], ROUND, ALU.mult, ALU.add).then_inc(rounded, 1)
                    dve.wait_ge(rounded, 2 * s + 1)
                    dve.tensor_scalar(yi[:], yi[:], ROUND, None, ALU.subtract).then_inc(rounded, 1)
                    dve.wait_ge(rounded, 2 * s + 2)
                    dve.wait_ge(q, at + 1)
                    if later(s, 1):
                        dve.wait_ge(z_turned, 2 * s)
                    dve.scalar_tensor_tensor(out=z[:], in0=yi[:], scalar=col[:, 3:4], in1=y, op0=ALU.mult,
                                             op1=ALU.add).then_inc(z_made, 1)
                    dve.wait_ge(z_made, s + 3)
                if has[1]:
                    dve.wait_ge(x2_stored[1 - u], 32 * uses[1])
                    if later(s, 3):
                        for b in range(2):
                            dve.wait_ge(conv_done[b], s - 2)
                    scale(0, s, u)
                    scale(1, s, u)
                if has[2]:
                    conv_out(0, s, u, uses[2])
                if has[0]:
                    for h in range(2):
                        cols = slice(h * HALF, (h + 1) * HALF)
                        dve.wait_ge(zT_hi, 2 * s + h + 1)
                        dve.tensor_tensor(zT[u][1][:, cols], pz[h][:], zT[u][0][:, cols].bitcast(F32),
                                          ALU.subtract).then_inc(zT_lo, 1)
                if has[2]:
                    conv_out(1, s, u, uses[2])
            stepped(dve, body, 2)

        @block.tensor
        def _(pe):
            for c in range(QC):
                last = pe.transpose(pz[0][:, c * P:(c + 1) * P], K["cmax"][:, c * P:(c + 1) * P], K["ident"][:])
            last.then_inc(turned, 1)
            for n in range(KC):
                pe.wait_ge(diag_made, n + 1)
                pe.matmul(pf[n // QC][:, (n % QC) * P:(n % QC + 1) * P], K["ones"][:], diag[:, n % 2, :],
                          start=True, stop=True).then_inc(spread, 1)

            def product(h, s, u):
                if later(s, 2):
                    pe.wait_ge(x2_scaled, 4 * (s - 2) + 2 * h + 2)
                else:
                    pe.wait_ge(keep_out, 2)
                for k in range(KC):
                    last = split_product(pe, pf[h][:], [v[:, k * P:(k + 1) * P] for v in zT[1 - u]],
                                         [K["cbT"][:, k, h * HALF:(h + 1) * HALF]], k == 0, k == KC - 1)
                last.then_inc(f_mm, 1)

            def conv(b, s, u):
                if later(s, 3):
                    pe.wait_ge(y2_made[b], s - 2)
                for c in range(QC):
                    for n in range(SHIFTS):
                        last = pe.matmul(pv[b][:, c * P:(c + 1) * P], x2[u][:, b, c * P + n:(c + 1) * P + n],
                                         K["taps"][1][:, n, :], start=n == 0, stop=n == SHIFTS - 1)
                last.then_inc(conv_done[b], 1)

            def body(s, u, uses, has):
                if has[1]:
                    pe.wait_ge(zT_lo, 2 * s)
                    product(0, s, u)
                    product(1, s, u)
                if has[2]:
                    pe.wait_ge(x2_made, s - 1)
                    conv(0, s, u)
                if has[0]:
                    pe.wait_ge(z_made, s + 3)
                    for h in range(2):
                        if later(s, 1):
                            pe.wait_ge(zT_lo, 2 * s)
                        else:
                            pe.wait_ge(topped, 1)
                        for j in range(4):
                            k = 4 * h + j
                            last = pe.transpose(pz[h][:, j * P:(j + 1) * P], z[:, k * P:(k + 1) * P], K["ident"][:])
                        last.then_inc(z_turned, 1)
                if has[2]:
                    conv(1, s, u)
            stepped(pe, body, 2)


def phase_l2(nc, K, A, SC):
    with ExitStack() as ctx:
        s_ = Scope(nc, ctx)
        mix = Mixer(s_, "mix3", K["att3"], K["kern3"])
        base, low, war = K["l2_base"], K["l2_B"], K["l2_war"]
        y2 = s_.sb("l2_y2", [P, 2, D])
        x2 = s_.sb("l2_x2", [P, 2, D])
        bias = s_.sb("l2_bias", [P, D])
        beta = s_.sb("l2_beta", [P, D])
        cr = s_.sb("cr", [P, D])
        crT = s_.sb("crT", [P, D])
        x3 = s_.sb("x3", [P, 2, D])
        x3b = s_.sb("x3b", [P, D])
        y3 = s_.sb("y3", [P, D])
        y3s = s_.split("y3_out", [P, D])
        rT = s_.sb("rT", [R2 + E2, P])
        sm = s_.sb("l2_small", [P, 8, E2])
        res = s_.sb("l2_res", [P, R2])
        m, nm, kmax, z, tot, m2 = [sm[:, 0, i:i + 1] for i in range(6)]
        lg, key, one, two, ex, lg2 = [sm[:, i, :] for i in range(1, 7)]
        pr = s_.banks("pr", 2)
        pc = s_.banks("pc", 2)
        po = s_.banks("po2_", 2)
        py = s_.banks("py3_", 2)
        y_loaded, x_loaded = s_.slot_sems("l2_y_loaded"), s_.slot_sems("l2_x_loaded")
        (bias_loaded, beta_loaded, x_free, r_mm, r_out, r_turned, step, e_done, cr_made, cr_turned, crT_made, o_mm, xb,
         x3_made, x3b_made, x3b_stored, y_mm, y3_made, y3_hi, y3_lo, y3_stored) = s_.sems(
            "l2_bias_loaded beta_loaded l2_x_read r_mm r_out r_turned mix_step exp_done cr_made cr_turned crT_made l2_o_mm "
            "l2_xb_made x3_made x3b_made x3b_stored y3_mm y3_made y3_hi y3_lo y3_stored")
        MS = 18
        block = s_.block()

        @block.sync
        def _(sp):
            sp.dma_start(bias[:], A["L2_ffn_base_b"].partition_broadcast(P)).then_inc(bias_loaded, 16)
            sp.dma_start(beta[:], A["L3_ffn_ln_beta"].partition_broadcast(P)).then_inc(beta_loaded, 16)

            def body(s, u, uses, has):
                if has[0]:
                    sp.wait_ge(o_mm, 2 * s + 2)
                    sp.dma_start(y2[:, u, :], tile_of(SC["y2T"], s)).then_inc(y_loaded[u], 16)
                    sp.wait_ge(x_free, s + 1)
                    sp.dma_start(x2[:, u, :], tile_of(SC["x2"], s)).then_inc(x_loaded[u], 16)
                if has[1]:
                    sp.wait_ge(x3b_made, s)
                    sp.dma_start(tile_of(SC["x3b"], s - 1), x3b[:]).then_inc(x3b_stored, 16)
                if has[2]:
                    t = s - 2
                    sp.wait_ge(y3_lo, s - 1)
                    for part in range(2):
                        sp.dma_start(SC["y3s"][part][:, :, bass.ds(t * P, P)],
                                     y3s[part][:].bitcast(F32).rearrange("p (k j) -> p k j", k=KC)).then_inc(y3_stored, 16)
            stepped(sp, body, 2)
            sp.wait_ge(x3b_stored, 16 * (NT + 1))
            sp.wait_ge(y3_stored, 32 * (NT + 1))

        @block.gpsimd
        def _(pool):
            pool.wait_ge(bias_loaded, 16)
            pool.wait_ge(beta_loaded, 16)
            pool.sem_inc(y3_stored, 32)

            def body(s, u, uses, has):
                if has[0]:
                    mix.weigh(pool, s)
                    pool.wait_ge(x_loaded[u], 16 * uses[0])
                    pool.tensor_tensor(x2[:, u, :], x2[:, u, :], bias[:], ALU.add).then_inc(xb, 1)
                if has[1]:
                    pool.wait_ge(x3_made, 2 * s)
                    pool.wait_ge(x3b_stored, 16 * s)
                    pool.tensor_tensor(x3b[:], x3[:, 1 - u, :], beta[:], ALU.add).then_inc(x3b_made, 1)
                if has[2]:
                    pool.wait_ge(y3_hi, s - 1)
                    pool.tensor_tensor(y3s[1][:], y3[:], y3s[0][:].bitcast(F32), ALU.subtract).then_inc(y3_lo, 1)
            stepped(pool, body, 2)

        @block.scalar
        def _(act):
            act.wait_ge(mix.zeroed, 1)

            def body(s, u, uses, has):
                if has[1]:
                    for h in range(2):
                        act.wait_ge(cr_turned, 2 * (s - 1) + h + 1)
                        if later(s, 2):
                            act.wait_ge(o_mm, 2 * (s - 2) + 6)
                        act.copy(crT[:, h * HALF:(h + 1) * HALF], pc[h][:]).then_inc(crT_made, 1)
                if has[0]:
                    if later(s, 2):
                        act.wait_ge(y_mm, 2 * (s - 1))
                    mix.place(act, s, u)
                    act.wait_ge(r_mm, s + 1)
                    act.copy(rT[:], pr[0][0:R2 + E2, 0:P]).then_inc(r_out, 1)
                if has[0]:
                    act.wait_ge(step, MS * s + 7)
                    act.activation(ex, lg, ACT.Exp, bias=nm, accum_out=z).then_inc(e_done, 1)
                if has[2]:
                    act.wait_ge(y3_made, 2 * (s - 1))
                    act.wait_ge(y3_stored, 32 * (s - 1))
                    act.copy(y3s[0][:], y3[:]).then_inc(y3_hi, 1)
            stepped(act, body, 2)

        @block.vector
        def _(dve):
            mix.start(dve)
            dve.sem_inc(x_free, 2)
            dve.sem_inc(x3b_stored, 16)
            dve.sem_inc(o_mm, 4)

            def body(s, u, uses, has):
                if has[0]:
                    mix.sum(dve, s)
                if has[2]:
                    for h in range(2):
                        dve.wait_ge(y_mm, 2 * (s - 2) + h + 1)
                        if later(s, 3):
                            dve.wait_ge(y3_lo, s - 2)
                        dve.tensor_tensor(y3[:, h * HALF:(h + 1) * HALF].rearrange("p (c k) -> p c k", c=4),
                                          py[h][:].rearrange("p (c k) -> p c k", c=4),
                                          K["bias3"][:, bass.ds((s - 2) * P, P)].unsqueeze(1).to_broadcast([P, 4, P]),
                                          ALU.add).then_inc(y3_made, 1)
                if has[0]:
                    at = MS * s
                    dve.wait_ge(r_turned, s + 1)
                    dve.tensor_copy(lg, pr[1][:, R2:R2 + E2]).then_inc(step, 1)
                    if later(s, 1):
                        dve.wait_ge(cr_made, s)
                    dve.tensor_copy(res[:], pr[1][:, 0:R2]).then_inc(step, 1)
                    dve.wait_ge(step, at + 2)
                    at = first_of_largest(dve, step, at + 2, lg, K["desc"][:], m, key, kmax, one)
                    dve.tensor_scalar(nm, m, -1.0, None, ALU.mult).then_inc(step, 1)
                    dve.scalar_tensor_tensor(out=lg2, in0=one, scalar=-BIG, in1=lg, op0=ALU.mult, op1=ALU.add).then_inc(step, 1)
                    dve.wait_ge(step, at + 2)
                    at = first_of_largest(dve, step, at + 2, lg2, K["desc"][:], m2, key, kmax, two)
                    dve.tensor_tensor(one, one, two, ALU.add).then_inc(step, 1)
                    dve.wait_ge(step, at + 1)
                    dve.wait_ge(e_done, s + 1)
                    dve.tensor_tensor(key, ex, one, ALU.mult).then_inc(step, 1)
                    dve.wait_ge(step, at + 2)
                    dve.tensor_reduce(tot, key, AX.X, ALU.add).then_inc(step, 1)
                    dve.wait_ge(step, at + 3)
                    dve.scalar_tensor_tensor(out=tot, in0=z, scalar=1e-6, in1=tot, op0=ALU.mult, op1=ALU.add).then_inc(step, 1)
                    dve.wait_ge(step, at + 4)
                    dve.reciprocal(kmax, tot).then_inc(step, 1)
                    dve.wait_ge(step, at + 5)
                    dve.tensor_scalar(key, key, kmax, 0.5, ALU.mult, ALU.mult).then_inc(step, 1)
                    dve.wait_ge(step, at + 6)
                    if isinstance(s, int):
                        assert at + 6 == MS * (s + 1), at + 6 - MS * s
                if has[1]:
                    for h in range(2):
                        cols = slice(h * HALF, (h + 1) * HALF)
                        dve.wait_ge(o_mm, 2 * (s - 1) + h + 5)
                        if h == 0:
                            dve.wait_ge(xb, s)
                            if later(s, 3):
                                dve.wait_ge(y_mm, 2 * (s - 2))
                                dve.wait_ge(x3b_made, s - 2)
                        dve.tensor_tensor(x3[:, 1 - u, cols], po[h][:], x2[:, 1 - u, cols], ALU.add).then_inc(x3_made, 1)
                    dve.wait_ge(x3_made, 2 * s)
                    dve.sem_inc(x_free, 1)
                if has[0]:
                    if later(s, 1):
                        dve.wait_ge(cr_turned, 2 * s)
                    dve.tensor_tensor(cr[:].rearrange("p (e r) -> p e r", e=E2),
                                      key.unsqueeze(2).to_broadcast([P, E2, R2]),
                                      res[:].unsqueeze(1).to_broadcast([P, E2, R2]), ALU.mult).then_inc(cr_made, 1)
            stepped(dve, body, 2)

        @block.tensor
        def _(pe):
            pe.wait_ge(K["l2_loaded"], 16 * 4)

            def half(h, s, u):
                for k in range(KC):
                    last = pe.matmul(po[h][:], crT[:, k * P:(k + 1) * P], low[:, k, h * HALF:(h + 1) * HALF],
                                     start=False, stop=k == KC - 1)
                last.then_inc(o_mm, 1)

            def body(s, u, uses, has):
                if has[1]:
                    pe.wait_ge(cr_made, s)
                    for h in range(2):
                        if later(s, 2):
                            pe.wait_ge(crT_made, 2 * (s - 1))
                        for j in range(4):
                            k = 4 * h + j
                            last = pe.transpose(pc[h][:, j * P:(j + 1) * P], cr[:, k * P:(k + 1) * P], K["ident"][:])
                        last.then_inc(cr_turned, 1)
                    for h in range(2):
                        if later(s, 2):
                            pe.wait_ge(x3_made, 2 * (s - 2) + h + 1)
                        for k in range(KC):
                            pe.matmul(po[h][:], y2[:, 1 - u, k * P:(k + 1) * P], base[:, k, h * HALF:(h + 1) * HALF],
                                      start=k == 0, stop=False)
                if has[2]:
                    if later(s, 3):
                        pe.wait_ge(y3_made, 2 * (s - 2))
                    pe.wait_ge(x3_made, 2 * (s - 1))
                    for h, last in mix.multiply(pe, s - 2, u, x3[:, u, :], py):
                        last.then_inc(y_mm, 1)
                if has[0]:
                    pe.wait_ge(y_loaded[u], 16 * uses[0])
                    if later(s, 1):
                        pe.wait_ge(r_out, s)
                    for k in range(KC):
                        last = pe.matmul(pr[0][0:R2 + E2, 0:P], war[:, k, :], y2[:, u, k * P:(k + 1) * P],
                                         start=k == 0, stop=k == KC - 1)
                    last.then_inc(r_mm, 1)
                if has[1]:
                    pe.wait_ge(crT_made, 2 * s)
                    half(0, s, u)
                if has[0]:
                    pe.wait_ge(r_out, s + 1)
                    if later(s, 1):
                        pe.wait_ge(step, MS * (s - 1) + 2)
                    pe.transpose(pr[1][:, 0:R2 + E2], rT[:], K["ident"][0:R2 + E2, 0:R2 + E2]).then_inc(r_turned, 1)
                if has[1]:
                    half(1, s, u)
            stepped(pe, body, 2)


def split_product(pe, out, lhs, rhs, first, last):
    pairs = [(0, 0)] + [(0, 1)] * (len(rhs) > 1) + [(1, 0)] * (len(lhs) > 1)
    for n, (a, b) in enumerate(pairs):
        mm = pe.matmul(out, lhs[a], rhs[b], start=first and n == 0, stop=last and n == len(pairs) - 1)
    return mm


def phase_l3(nc, K, A, SC, out):
    with ExitStack() as ctx:
        s_ = Scope(nc, ctx)
        HT = NT // 2
        TOK = HT * P
        NB = TOK // HALF
        y = s_.split("y3", [P, KC, TOK])
        acc = s_.sb("acc", [P, HT, D])
        raw = s_.sb("raw", [P, 2, D])
        up = [s_.split(f"up{i}", [P, D]) for i in range(2)]
        dn = [[s_.split(f"down{v}{i}", [P, D]) for i in range(2)] for v in range(2)]
        act_f = s_.sb("hidden", [P, 2, HALF])
        hid = [s_.split(f"hid{v}", [P, 2, TOK]) for v in range(2)]
        gate = s_.split("gate", [P, KC, EG])
        gamma = s_.sb("gamma", [P, D])
        x3b = s_.sb("l3_x3b", [P, 2, D])
        scratch = s_.sb("scratch", [P, D])
        gT = scratch[0:EG, :]
        logits, top = s_.sb("gate_logits", [P, HT * EG]), s_.sb("gate_top", [P, HT, EG])
        gate_sum = s_.sb("gate_sum", [P, NT])
        sums = s_.sb("row_sums", [P, NT, 2])
        nmean, ssq, root, inv, shift = [s_.sb(n, [P, NT]) for n in ("neg_mean", "sum_sq", "root", "rstd", "shift")]
        eps = s_.sb("eps", [P, 1])
        pu = s_.banks("pu", 2 * NB)
        pd = [s_.banks(f"pd{v}_", 2) for v in range(2)]
        up_loaded = s_.slot_sems("up_loaded")
        y_loaded, x3b_loaded, out_stored = K["y3_loaded"], K["x3b_loaded"], K["out_stored"]
        dn_loaded = [s_.slot_sems(f"down_loaded{v}") for v in range(2)]
        up_hi, up_lo, dn_hi, dn_lo, up_mm, relu, squared, h_hi, h_lo, dn_mm, added = s_.sems(
            "up_hi up_lo down_hi down_lo up_mm relu squared hid_hi hid_lo down_mm added")
        gate_hi, gate_lo, g_mm, gT_made, g_turned, g_out, topped, g_summed = s_.sems(
            "gate_hi gate_lo gate_mm gateT_made gate_turned gate_out gate_topped gate_summed")
        gamma_loaded, eps_set, centred, ssq_made, rooted, inverted, shifted, normed, scaled, out_made = s_.sems(
            "gamma_loaded eps_set neg_mean_made sum_sq_made root_made rstd_made shift_made normed scaled out_made")
        block = s_.block()
        Q = 2 * NB

        def steps(body):
            def fori(eng):
                for half in range(2):
                    b = NPAIR * half
                    body(b, 0, b // 2 + 1, half, True, half == 1, lat_back=half == 1, end=half == 1)
                    body(b + 1, 1, b // 2 + 1, half, True, True, first=True)
                    with eng.Fori(0, (HPAIR - 2) // 2) as i:
                        for r in range(2):
                            body(b + 2 + r + 2 * i, r, b // 2 + 2 + i, half, True, True)
                    body(b + HPAIR, 0, (b + HPAIR) // 2 + 1, half, True, True, lat=True)
                    body(b + HPAIR + 1, 1, (b + HPAIR) // 2 + 1, half, True, True, lat=True, lat_back=True)
                body(2 * NPAIR, 0, NPAIR + 1, 2, False, True, lat_back=True, end=True)
            return fori

        @block.sync
        def _(sp):
            sp.dma_start(gamma[:], A["L3_ffn_ln_gamma"].partition_broadcast(P)).then_inc(gamma_loaded, 16)

            def pair(g, j, u, lat):
                ups, downs, c = (SC["g2"], A["fc2"], 2 * j - NINT) if lat else (A["up"], A["down"], 2 * j)
                for i in range(2):
                    sp.wait_ge(dn_lo, 2 * g + i + 1)
                    sp.dma_start(raw[:, i, :], tile_of(ups, c + i)).then_inc(up_loaded[i], 16)
                for i in range(2):
                    sp.wait_ge(up_lo, 2 * g + i + 1)
                    sp.dma_start(raw[:, i, :], tile_of(downs, c + i)).then_inc(dn_loaded[u][i], 16)

            for half in range(2):
                with sp.Fori(0, HPAIR // 2) as n:
                    for r in range(2):
                        pair(NPAIR * half + 2 * n + r, 2 * n + r, r, False)
                for j in range(HPAIR, NPAIR):
                    pair(NPAIR * half + j, j, j % 2, True)

        @block.gpsimd
        def _(pool):
            pool.memset(eps[:], LN_EPS).then_inc(eps_set, 1)

            def load(T):
                pool.dma_start(x3b[:, T % 2, :], tile_of(SC["x3b"], T)).then_inc(x3b_loaded[T % 2], 16)

            def load_y(half):
                for n in range(NB):
                    for part in range(2):
                        cols = half * TOK + n * HALF
                        pool.dma_start(y[part][:, :, n * HALF:(n + 1) * HALF],
                                       SC["y3s"][part][:, :, cols:cols + HALF]).then_inc(y_loaded[n], 16)

            load_y(0)

            def body(g, u, use, half, front, back, lat=False, lat_back=False, first=False, end=False):
                if end and front:
                    pool.wait_ge(up_mm, Q * (g + 1))
                    load_y(half)
                if end:
                    for t in range(HT):
                        T = HT * (half - 1) + t
                        if t == 0:
                            load(T)
                            load(T + 1)
                        pool.wait_ge(scaled, T + 1)
                        pool.wait_ge(x3b_loaded[T % 2], 16 * (T // 2 + 1))
                        pool.tensor_tensor(acc[:, t, :], acc[:, t, :], x3b[:, T % 2, :], ALU.add).then_inc(out_made, 1)
                        pool.wait_ge(out_made, T + 1)
                        pool.dma_start(tile_of(out, T), acc[:, t, :]).then_inc(out_stored, 16)
                        if t + 2 < HT:
                            load(T + 2)
                if front:
                    for i in range(2):
                        pool.wait_ge(dn_hi, 2 * g + i + 1)
                        pool.tensor_tensor(dn[u][i][1][:], raw[:, i, :], dn[u][i][0][:].bitcast(F32), ALU.subtract).then_inc(dn_lo, 1)
            steps(body)(pool)
            pool.wait_ge(out_stored, 16 * NT)

        @block.scalar
        def _(act):
            def up_part(g, i):
                act.wait_ge(up_loaded[i], 16 * (g + 1))
                act.wait_ge(up_mm, Q * g + NB * (i + 1))
                act.copy(up[i][0][:], raw[:, i, :]).then_inc(up_hi, 1)

            def dn_part(u, use, i):
                act.wait_ge(dn_loaded[u][i], 16 * use)
                act.copy(dn[u][i][0][:], raw[:, i, :]).then_inc(dn_hi, 1)

            act.copy(gate[0][:], K["gate"][:]).then_inc(gate_hi, 1)
            act.wait_ge(eps_set, 1)
            up_part(0, 0)

            def norm(half):
                for t in range(HT + 1):
                    T = HT * half + t
                    if t < HT:
                        act.wait_ge(centred, T + 1)
                        if T:
                            act.wait_ge(ssq_made, T)
                        act.activation(scratch[:], acc[:, t, :], ACT.Square, bias=nmean[:, T:T + 1],
                                       accum_out=ssq[:, T:T + 1]).then_inc(ssq_made, 1)
                    if t:
                        act.wait_ge(shifted, T)
                        act.activation(acc[:, t - 1, :], acc[:, t - 1, :], ACT.Identity, bias=shift[:, T - 1:T],
                                       scale=inv[:, T - 1:T]).then_inc(normed, 1)
                    if t < HT:
                        act.wait_ge(ssq_made, T + 1)
                        act.activation(root[:, T:T + 1], ssq[:, T:T + 1], ACT.Sqrt, bias=eps[:], scale=1.0 / D).then_inc(rooted, 1)

            def body(g, u, use, half, front, back, lat=False, lat_back=False, first=False, end=False):
                if end:
                    norm(half - 1)
                if not front:
                    return
                if isinstance(g, int) and g % NPAIR == 0:
                    for n in range(NB):
                        act.wait_ge(g_mm, NB * half + n + 1)
                        if end:
                            act.wait_ge(ssq_made, HT * half)
                        act.copy(gT[:, n * HALF:(n + 1) * HALF], pd[n][0][0:EG, :]).then_inc(gT_made, 1)
                for q in range(Q):
                    i, cols = q // NB, slice((q % NB) * HALF, (q % NB + 1) * HALF)
                    act.wait_ge(up_mm, Q * (g + 1) + q + 1)
                    if q == 0:
                        act.wait_ge(dn_mm, HT * (g + 1))
                    if lat:
                        act.copy(hid[u][0][:, i, cols], pu[q][:]).then_inc(h_hi, 1)
                    else:
                        act.wait_ge(h_lo, Q * (g + 1) + q - 1)
                        act.activation(act_f[:, q % 2, :], pu[q][:], ACT.Relu).then_inc(relu, 1)
                        n = Q * (g - (NPAIR - HPAIR) * half) + q + 1
                        act.wait_ge(relu, n)
                        act.activation(act_f[:, q % 2, :], act_f[:, q % 2, :], ACT.Square).then_inc(squared, 1)
                        act.wait_ge(squared, n)
                        act.copy(hid[u][0][:, i, cols], act_f[:, q % 2, :]).then_inc(h_hi, 1)
                    if q == 0:
                        up_part(g, 1)
                        dn_part(u, use, 0)
                    if q == 2:
                        dn_part(u, use, 1)
                    if q == 3 and not (lat and half == 1 and u == 1):
                        up_part(g + 1, 0)
            steps(body)(act)

        @block.vector
        def _(dve):
            def up_rest(g, i):
                dve.wait_ge(up_hi, 2 * g + i + 1)
                dve.tensor_tensor(up[i][1][:], raw[:, i, :], up[i][0][:].bitcast(F32), ALU.subtract).then_inc(up_lo, 1)

            dve.wait_ge(gate_hi, 1)
            dve.tensor_tensor(gate[1][:], K["gate"][:], gate[0][:].bitcast(F32), ALU.subtract).then_inc(gate_lo, 1)
            up_rest(0, 0)

            def add(g, t, half, lat_back, first, end):
                dve.wait_ge(dn_mm, HT * (g + 1) + t + 1)
                T = HT * half + t
                for h in range(2):
                    part, bank = acc[:, t, h * HALF:(h + 1) * HALF], pd[t % 2][h][:]
                    if first:
                        last = dve.tensor_copy(part, bank)
                    elif lat_back:
                        last = dve.scalar_tensor_tensor(out=part, in0=bank, scalar=gate_sum[:, T:T + 1], in1=part,
                                                        op0=ALU.mult, op1=ALU.add,
                                                        accum_out=sums[:, T, h:h + 1] if end else None)
                    else:
                        last = dve.tensor_tensor(part, bank, part, ALU.add)
                    last.then_inc(added, 1)

            def scale(T):
                dve.wait_ge(rooted, T + 1)
                dve.reciprocal(inv[:, T:T + 1], root[:, T:T + 1]).then_inc(inverted, 1)
                dve.wait_ge(inverted, T + 1)
                dve.tensor_tensor(shift[:, T:T + 1], nmean[:, T:T + 1], inv[:, T:T + 1], ALU.mult).then_inc(shifted, 1)

            def weigh(T):
                dve.wait_ge(normed, T + 1)
                if T == 0:
                    dve.wait_ge(gamma_loaded, 16)
                dve.tensor_tensor(acc[:, T % HT, :], acc[:, T % HT, :], gamma[:], ALU.mult).then_inc(scaled, 1)

            def gate_top(half):
                dve.wait_ge(g_turned, half + 1)
                dve.tensor_copy(logits[:], pd[0][1][:, 0:HT * EG]).then_inc(g_out, 1)
                dve.wait_ge(g_out, half + 1)
                for t in range(HT):
                    dve.max(out=top[:, t, :], in_=logits[:, t * EG:(t + 1) * EG]).then_inc(topped, 1)
                dve.wait_ge(topped, HT * (half + 1))
                dve.tensor_tensor(gate_sum[:, HT * half:HT * (half + 1)].unsqueeze(2), top[:, :, 0:1], top[:, :, 1:2],
                                  ALU.add).then_inc(g_summed, 1)
                dve.wait_ge(g_summed, half + 1)

            def body(g, u, use, half, front, back, lat=False, lat_back=False, first=False, end=False):
                if end:
                    for t in range(HT):
                        T = HT * (half - 1) + t
                        add(g, t, half - 1, lat_back, first, end)
                        dve.wait_ge(added, 2 * (HT * (g - 1) + t + 3))
                        dve.tensor_scalar(nmean[:, T:T + 1], sums[:, T, 0:1], sums[:, T, 1:2], -1.0 / D,
                                          ALU.add, ALU.mult).then_inc(centred, 1)
                        if t >= 1:
                            scale(T - 1)
                        if t >= 2:
                            weigh(T - 2)
                    scale(T)
                    weigh(T - 1)
                    weigh(T)
                if first and half:
                    dve.wait_ge(out_stored, 16 * HT)
                for q in range(Q):
                    if back and not end:
                        add(g, 2 * q, half, lat_back, first, end)
                        add(g, 2 * q + 1, half, lat_back, first, end)
                    if front:
                        i, cols = q // NB, slice((q % NB) * HALF, (q % NB + 1) * HALF)
                        dve.wait_ge(h_hi, Q * g + q + 1)
                        dve.tensor_tensor(hid[u][1][:, i, cols], pu[q][:] if lat else act_f[:, q % 2, :],
                                          hid[u][0][:, i, cols].bitcast(F32), ALU.subtract).then_inc(h_lo, 1)
                        if q == 0:
                            up_rest(g, 1)
                            if isinstance(g, int) and g % NPAIR == 0:
                                gate_top(half)
                        if q == 3 and not (lat and half == 1 and u == 1):
                            up_rest(g + 1, 0)
            steps(body)(dve)

        @block.tensor
        def _(pe):
            pe.sem_inc(dn_lo, 2)
            pe.sem_inc(up_mm, Q)
            pe.sem_inc(h_lo, Q)
            pe.sem_inc(dn_mm, 2 * HT)
            pe.sem_inc(added, 4)

            def upward(g, q, half):
                i, n = q // NB, q % NB
                pe.wait_ge(up_lo, 2 * g + i + 1)
                pe.wait_ge(y_loaded[n], 32 * (half + 1))
                pe.wait_ge(h_lo, Q * g + q + 1)
                for k in range(KC):
                    last = split_product(pe, pu[q][:], [w[:, k * P:(k + 1) * P] for w in up[i]],
                                         [v[:, k, n * HALF:(n + 1) * HALF] for v in y], k == 0, k == KC - 1)
                last.then_inc(up_mm, 1)

            def downward(g, u, t):
                v = 1 - u
                if t == 0:
                    pe.wait_ge(dn_lo, 2 * (g + 1))
                    pe.wait_ge(h_lo, Q * (g + 1))
                pe.wait_ge(added, 2 * (HT * (g - 1) + t + 1))
                for h in range(2):
                    for i in range(2):
                        last = split_product(pe, pd[t % 2][h][:], [w[:, i, t * P:(t + 1) * P] for w in hid[v]],
                                             [w[:, h * HALF:(h + 1) * HALF] for w in dn[v][i]], i == 0, i == 1)
                last.then_inc(dn_mm, 1)

            def body(g, u, use, half, front, back, lat=False, lat_back=False, first=False, end=False):
                if end:
                    for t in range(HT):
                        downward(g, u, t)
                if isinstance(g, int) and g % NPAIR == 0 and front:
                    if half == 0:
                        pe.wait_ge(gate_lo, 1)
                    else:
                        pe.wait_ge(added, 2 * (HT * g + 2))
                    for n in range(NB):
                        pe.wait_ge(y_loaded[n], 32 * (half + 1))
                        for k in range(KC):
                            last = split_product(pe, pd[n][0][0:EG, :], [w[:, k, :] for w in gate],
                                                 [v[:, k, n * HALF:(n + 1) * HALF] for v in y], k == 0, k == KC - 1)
                        last.then_inc(g_mm, 1)
                    upward(g, 0, half)
                    pe.wait_ge(gT_made, NB * (half + 1))
                    for t in range(HT):
                        last = pe.transpose(pd[0][1][:, t * EG:(t + 1) * EG], gT[:, t * P:(t + 1) * P], K["ident"][0:EG, 0:EG])
                    last.then_inc(g_turned, 1)
                    for q in range(1, Q):
                        upward(g, q, half)
                    pe.wait_ge(g_out, half + 1)
                elif not end:
                    for q in range(Q):
                        if front:
                            upward(g, q, half)
                        downward(g, u, 2 * q)
                        downward(g, u, 2 * q + 1)
            steps(body)(pe)


def build(nc, A, out):
    SC = {}
    for name, shape in (("att0", (BATCH, NK)), ("att3", (BATCH, NK)), ("bias0", (BATCH, CH)), ("bias3", (BATCH, CH)),
                        ("ctx2", (BATCH, CH)), ("g", (NLAT, P, KC, P)), ("x1", (NT, P, D)), ("y1", (NT, P, D)),
                        ("x2", (NT, P, D)), ("y2T", (NT, P, D)), ("x3b", (NT, P, D))):
        SC[name] = nc.dram_tensor("scratch_" + name, shape, F32).ap()
    SC["y3s"] = [nc.dram_tensor(f"scratch_y3_{part}", (P, KC, NT * P), F32).ap() for part in ("hi", "lo")]
    SC["g2"] = SC["g"].rearrange("c p k j -> c p (k j)")
    with ExitStack() as ctx:
        s = Scope(nc, ctx)
        K = dict(ident=s.sb("ident", [P, P]), ones=s.sb("ones", [P, P]), desc=s.sb("desc", [P, E2]),
                 gate=s.sb("gate", [P, KC, EG]))
        K["taps_loaded"], K["l0_loaded"], K["l2_loaded"] = s.sems("taps_loaded l0_weights_loaded l2_weights_loaded")
        K["qw_loaded"], K["g_stored"], K["x3b_loaded"] = [s.slot_sems(n) for n in ("qw_loaded", "g_stored", "x3b_loaded")]
        K["y3_loaded"] = s.slot_sems("y3_loaded")
        (K["out_stored"],) = s.sems("out_stored")
        with ExitStack() as c0:
            s0 = Scope(nc, c0)
            K["l2_base"], K["l2_B"] = s0.sb("l2_base", [P, KC, D]), s0.sb("l2_B", [P, KC, D])
            K["l2_war"] = s0.sb("l2_war", [P, KC, R2 + E2])
            K["att3"], K["kern3"] = s0.sb("att3", [P, NT, NK]), s0.sb("kern3", [P, CH, NK])
            K["bias3"] = s0.sb("bias3", [P, NT * P])
            with ExitStack() as c1:
                s1 = Scope(nc, c1)
                K["cbT"], K["scb_row"] = s1.sb("cbT", [P, KC, D], F32R), s1.sb("scb_row", [P, D])
                K["cmax"] = s1.sb("cmax", [P, HALF])
                K["ctx1"], K["ctx2"] = s1.sb("ctx1", [P, 2, NT]), s1.sb("ctx2", [P, NT * P])
                K["taps"] = [s1.sb(f"taps{i}", [P, SHIFTS, P]) for i in range(2)]
                with ExitStack() as c2:
                    s2 = Scope(nc, c2)
                    K["bias0"] = s2.sb("bias0", [P, NT * P])
                    K["att0"], K["kern0"] = s2.sb("att0", [P, NT, NK]), s2.sb("kern0", [P, CH, NK])
                    K["l0_wa"], K["l0_wb"] = s2.sb("l0_wa", [P, KC, P + E0]), s2.sb("l0_wb", [P, D])
                    K["kept_loads"] = [(K["l0_wa"][:], A["l0_wa"], K["l0_loaded"]), (K["l0_wb"][:], A["l0_wb"], K["l0_loaded"]),
                                       (K["l2_war"][:], A["l2_war"], K["l2_loaded"]), (K["gate"][:], A["gate"], K["l2_loaded"]),
                                       (K["l2_base"][:], A["l2_base"], K["l2_loaded"]), (K["l2_B"][:], A["l2_B"], K["l2_loaded"])]
                    phase_setup(nc, K, A, SC)
                    phase_l0(nc, K, A, SC)
                phase_l1(nc, K, A, SC)
            phase_l2(nc, K, A, SC)
        phase_l3(nc, K, A, SC, out)
    return SC


def lay_out(i):
    import numpy as np

    def c(a):
        return np.ascontiguousarray(a)

    def feat(a, axis=-1):
        a = np.moveaxis(np.asarray(a), axis, -1)
        a = a.reshape(a.shape[:-1] + (HALF, 2)).swapaxes(-1, -2).reshape(a.shape)
        return np.moveaxis(a, -1, axis)

    def chunks(a):
        return c(np.asarray(a).reshape(KC, P, -1).transpose(1, 0, 2))

    a = {}
    a["x"] = c(feat(i["x"])).reshape(NT, P, D)
    a["condT"] = c(np.asarray(i["cond_128"]).T)
    a["fside_S_0"] = c(i["fside_S_0"])
    a["L1_ffn_weight"] = c(feat(feat(i["L1_ffn_weight"], 0), 1))
    for n in ("L1_ffn_bias", "L2_ffn_base_b", "L3_ffn_ln_gamma", "L3_ffn_ln_beta"):
        a[n] = c(feat(i[n]))
    for L in "03":
        for n in ("W0", "b0", "W1", "b1", "W2", "b2", "bias_k"):
            a[f"L{L}_cond_{n}"] = c(i[f"L{L}_cond_{n}"])
        a[f"L{L}_cond_kernels"] = c(np.asarray(i[f"L{L}_cond_weight"])[..., 0].transpose(2, 1, 0)).reshape(CH, NK * CH)
    for L in "12":
        a[f"L{L}_cond_c_weight_T"] = c(np.asarray(i[f"L{L}_cond_c_weight"]).T)
        w = np.asarray(i[f"L{L}_cond_weight"]).reshape(GROUPS, GI, GI, TAPS)
        a[f"L{L}_cond_taps"] = c(w.transpose(0, 2, 3, 1)).reshape(GROUPS, GI, TAPS * GI)
    wa = np.concatenate([np.asarray(i["L0_ffn_A"]).reshape(E0 * R0, D), np.asarray(i["L0_ffn_route_w"])])
    a["l0_wa"] = chunks(feat(wa).T)
    a["l0_wb"] = c(feat(np.asarray(i["L0_ffn_Bw"]).transpose(0, 2, 1))).reshape(P, D)
    war = np.concatenate([np.asarray(i["L2_ffn_A"]), np.asarray(i["L2_ffn_router_w"])])
    a["l2_war"] = chunks(feat(war).T)
    a["l2_base"] = chunks(feat(feat(i["L2_ffn_base_w"], 0), 1).T)
    a["l2_B"] = chunks(feat(np.asarray(i["L2_ffn_B"]).transpose(0, 2, 1)).reshape(D, D))
    a["gate"] = chunks(feat(i["L3_ffn_gate_w"], 0))
    up = feat(i["L3_ffn_up_w"], 0)
    a["up"] = c(up.reshape(KC, P, NINT, P).transpose(2, 1, 0, 3)).reshape(NINT, P, D)
    a["down"] = c(feat(i["L3_ffn_down_w"])).reshape(NINT, P, D)
    a["fc1T"] = c(feat(i["L3_ffn_fc1_w"], 0).T)
    a["L3_ffn_expert_w"] = c(i["L3_ffn_expert_w"])
    a["fc2"] = c(feat(i["L3_ffn_fc2_w"])).reshape(NLAT, P, D)
    return a


def kernel(**inputs):
    import numpy as np
    import concourse.bacc as bacc
    from concourse.bass_utils import run_bass_kernel_spmd as run

    nc = bacc.Bacc("TRN2", target_bir_lowering=False, num_devices=1)
    arrays, aps = {}, {}
    for name, a in lay_out(inputs).items():
        arrays["in_" + name] = a
        aps[name] = nc.dram_tensor("in_" + name, a.shape, F32, kind="ExternalInput").ap()
    out = nc.dram_tensor("out", (NT, P, D), F32, kind="ExternalOutput").ap()
    build(nc, aps, out)
    result = run(nc, [arrays], core_ids=[0]).results[0]["out"]
    return np.asarray(result).reshape(BATCH, CH, 2, HALF).transpose(0, 1, 3, 2).reshape(BATCH, CH, D)
```
